# Optimizing a Trainium2 kernel written in Bass

```python
import numpy as np
import jax
import jax.numpy as jnp

def _softmax(x, axis=-1):
    return jax.nn.softmax(x, axis=axis)

def _gelu(x):
    return jax.nn.gelu(x, approximate=True)

def _silu(x):
    return jax.nn.silu(x)

def _sigmoid(x):
    return jax.nn.sigmoid(x)

def _layernorm(x, axis=-1, eps=1e-05):
    m = jnp.mean(x, axis=axis, keepdims=True)
    v = jnp.var(x, axis=axis, keepdims=True)
    return (x - m) / jnp.sqrt(v + eps)

def _scatter_add(tgt, idx, src, axis=0):
    return tgt.at[idx].add(src)

def _segment_sum(src, seg, n):
    return jax.ops.segment_sum(src, seg, n)
kernel_name = 'mk_adaln_d2_jaxref_r8_c6bebf'

def setup_inputs(seed: int=0):
    np.random.seed(seed)
    _w = jnp.asarray

    def _L0_attn_setup():
        import jax, jax.numpy as jnp
        import numpy as np
        D_MODEL = 128
        N_HEADS = 8
        D_STATE = 64
        HEAD_DIM = 64
        EXPAND = 2
        D_INNER = N_HEADS * HEAD_DIM
        BATCH = 2
        SEQ = 512

        def _ssd_scan(X, delta, B_ssm, C_ssm, A_log):
            neg_A = -jnp.exp(A_log)

            def step(h, inp):
                X_t, d_t, B_t, C_t = inp
                dA = jnp.exp(d_t * neg_A)
                dB = d_t[..., None] * B_t[:, None, :]
                h = dA[..., None, None] * h + X_t[..., None] * dB[:, :, None, :]
                y_t = jnp.einsum('bhpn,bn->bhp', h, C_t)
                return (h, y_t)
            b, t, hh, p = X.shape
            n = B_ssm.shape[-1]
            h0 = jnp.zeros((b, hh, p, n), dtype=X.dtype)
            xs = (jnp.swapaxes(X, 0, 1), jnp.swapaxes(delta, 0, 1), jnp.swapaxes(B_ssm, 0, 1), jnp.swapaxes(C_ssm, 0, 1))
            h_last, ys = jax.lax.scan(step, h0, xs)
            return (jnp.swapaxes(ys, 0, 1), h_last)

        def _reference_tuple_inner(x, Wz, Win, Wzg, Wout, dt_bias, A_log, D_param):
            b, t, _ = x.shape
            z = x @ Wz
            ssm_in = x @ Win
            B_ssm = ssm_in[..., :D_STATE]
            C_ssm = ssm_in[..., D_STATE:2 * D_STATE]
            dt_raw = ssm_in[..., 2 * D_STATE:2 * D_STATE + N_HEADS]
            X = ssm_in[..., 2 * D_STATE + N_HEADS:].reshape(b, t, N_HEADS, HEAD_DIM)
            delta = jax.nn.softplus(dt_raw + dt_bias)
            y, h_last = _ssd_scan(X, delta, B_ssm, C_ssm, A_log)
            y = y + D_param[None, None, :, None] * X
            y_flat = y.reshape(b, t, D_INNER)
            z_gated = jax.nn.silu(z) @ Wzg
            output = y_flat * z_gated @ Wout
            return (output, h_last)
        key = jax.random.key(seed)
        ks = jax.random.split(key, 6)
        s = 0.02
        x = jax.random.normal(ks[0], (BATCH, SEQ, D_MODEL), dtype=jnp.float32)
        Wz = jax.random.normal(ks[1], (D_MODEL, D_MODEL * EXPAND), dtype=jnp.float32) * s
        Win = jax.random.normal(ks[2], (D_MODEL, 2 * D_STATE + N_HEADS + D_INNER), dtype=jnp.float32) * s
        Wzg = jax.random.normal(ks[3], (D_MODEL * EXPAND, D_INNER), dtype=jnp.float32) * s
        Wout = jax.random.normal(ks[4], (D_INNER, D_MODEL), dtype=jnp.float32) * s
        dt_bias = jnp.full((N_HEADS,), np.log(0.1), dtype=jnp.float32)
        A_log = jnp.log(jnp.arange(1, N_HEADS + 1, dtype=jnp.float32))
        D_param = jnp.ones((N_HEADS,), dtype=jnp.float32)
        return {'x': x, 'Wz': Wz, 'Win': Win, 'Wzg': Wzg, 'Wout': Wout, 'dt_bias': dt_bias, 'A_log': A_log, 'D_param': D_param}
    _L0_attn_in = _L0_attn_setup()

    def _L0_ffn_setup():
        import jax, jax.numpy as jnp
        import numpy as np
        B, T, C, H, E = (1, 32, 128, 256, 8)
        STD = 0.02
        key = jax.random.key(seed)
        ks = jax.random.split(key, 8)
        f32 = jnp.float32
        return {'x': jax.random.normal(ks[0], (B, T, C), f32), 'up': jax.random.normal(ks[1], (E, H, C), f32) * STD, 'gate': jax.random.normal(ks[2], (E, H, C), f32) * STD, 'down': jax.random.normal(ks[3], (E, C, H), f32) * STD, 'router': jax.random.normal(ks[4], (E, C), f32) * STD, 'w_up_s': jax.random.normal(ks[5], (H, C), f32) * STD, 'w_gate_s': jax.random.normal(ks[6], (H, C), f32) * STD, 'w_down_s': jax.random.normal(ks[7], (C, H), f32) * STD}
    _L0_ffn_in = _L0_ffn_setup()
    _L0_c = _w((lambda *s: np.random.randn(*s).astype(np.float32) * 0.05)(2, 128))
    _L0_wmod = _w((lambda *s: np.random.randn(*s).astype(np.float32) * 0.05)(128, 6 * 128) * 128 ** (-0.5))

    def _L1_attn_setup():
        import jax, jax.numpy as jnp
        import numpy as np
        key = jax.random.key(seed)
        k_u, k_lam, k_B, k_C = jax.random.split(key, 4)
        batch, seq_len, d_model, N = (4, 512, 128, 64)
        return {'u': jax.random.normal(k_u, (batch, seq_len, d_model), dtype=jnp.float32), 'Lambda': jax.random.normal(k_lam, (N,), dtype=jnp.float32), 'log_dt': jnp.zeros((1,), dtype=jnp.float32), 'B': jax.random.normal(k_B, (N, d_model), dtype=jnp.float32), 'C': jax.random.normal(k_C, (d_model, N), dtype=jnp.float32), 'D': jnp.zeros((d_model,), dtype=jnp.float32)}
    _L1_attn_in = _L1_attn_setup()

    def _L1_ffn_setup():
        import jax, jax.numpy as jnp
        import numpy as np
        B, S, D, H, F = (4, 512, 128, 16, 512)
        CAP = 0.125
        ROPE_BASE = 10000.0

        def rmsnorm(x, g):
            return x * jax.lax.rsqrt(jnp.mean(x * x, -1, keepdims=True) + 1e-06) * g

        def rope(t, pos):
            hd = t.shape[-1]
            inv = 1.0 / ROPE_BASE ** (jnp.arange(0, hd, 2, dtype=jnp.float32) / hd)
            f = pos[:, None, :, None].astype(jnp.float32) * inv
            emb = jnp.concatenate([f, f], axis=-1)
            cos, sin = (jnp.cos(emb), jnp.sin(emb))
            rot = jnp.concatenate([-t[..., hd // 2:], t[..., :hd // 2]], axis=-1)
            return t * cos + rot * sin
        key = jax.random.key(seed)
        ks = jax.random.split(key, 9)
        scale = 0.02
        x = jax.random.normal(ks[0], (B, S, D), jnp.float32)
        causal = jnp.where(jnp.tril(jnp.ones((S, S), bool)), 0.0, -1000000000.0).astype(jnp.float32)
        attention_mask = jnp.broadcast_to(causal[None, None], (B, 1, S, S))
        position_ids = jnp.broadcast_to(jnp.arange(S, dtype=jnp.int32), (B, S))
        return {'x': x, 'attention_mask': attention_mask, 'position_ids': position_ids, 'router_w': jax.random.normal(ks[1], (D, 1), jnp.float32) * scale, 'router_b': jnp.zeros((1,), jnp.float32), 'wq': jax.random.normal(ks[2], (D, D), jnp.float32) * scale, 'wk': jax.random.normal(ks[3], (D, D), jnp.float32) * scale, 'wv': jax.random.normal(ks[4], (D, D), jnp.float32) * scale, 'wo': jax.random.normal(ks[5], (D, D), jnp.float32) * scale, 'w1': jax.random.normal(ks[6], (D, F), jnp.float32) * scale, 'w2': jax.random.normal(ks[7], (F, D), jnp.float32) * scale, 'ln1': jnp.ones((D,), jnp.float32), 'ln2': jnp.ones((D,), jnp.float32)}
    _L1_ffn_in = _L1_ffn_setup()
    _L1_c = _w((lambda *s: np.random.randn(*s).astype(np.float32) * 0.05)(2, 128))
    _L1_wmod = _w((lambda *s: np.random.randn(*s).astype(np.float32) * 0.05)(128, 6 * 128) * 128 ** (-0.5))
    _d = {'L0_attn_x': _L0_attn_in['x'], 'L0_attn_Wz': _L0_attn_in['Wz'], 'L0_attn_Win': _L0_attn_in['Win'], 'L0_attn_Wzg': _L0_attn_in['Wzg'], 'L0_attn_Wout': _L0_attn_in['Wout'], 'L0_attn_dt_bias': _L0_attn_in['dt_bias'], 'L0_attn_A_log': _L0_attn_in['A_log'], 'L0_attn_D_param': _L0_attn_in['D_param'], 'L0_ffn_up': _L0_ffn_in['up'], 'L0_ffn_gate': _L0_ffn_in['gate'], 'L0_ffn_down': _L0_ffn_in['down'], 'L0_ffn_router': _L0_ffn_in['router'], 'L0_ffn_w_up_s': _L0_ffn_in['w_up_s'], 'L0_ffn_w_gate_s': _L0_ffn_in['w_gate_s'], 'L0_ffn_w_down_s': _L0_ffn_in['w_down_s'], 'L0_c': _L0_c, 'L0_wmod': _L0_wmod, 'L1_attn_Lambda': _L1_attn_in['Lambda'], 'L1_attn_log_dt': _L1_attn_in['log_dt'], 'L1_attn_B': _L1_attn_in['B'], 'L1_attn_C': _L1_attn_in['C'], 'L1_attn_D': _L1_attn_in['D'], 'L1_ffn_attention_mask': _L1_ffn_in['attention_mask'], 'L1_ffn_position_ids': _L1_ffn_in['position_ids'], 'L1_ffn_router_w': _L1_ffn_in['router_w'], 'L1_ffn_router_b': _L1_ffn_in['router_b'], 'L1_ffn_wq': _L1_ffn_in['wq'], 'L1_ffn_wk': _L1_ffn_in['wk'], 'L1_ffn_wv': _L1_ffn_in['wv'], 'L1_ffn_wo': _L1_ffn_in['wo'], 'L1_ffn_w1': _L1_ffn_in['w1'], 'L1_ffn_w2': _L1_ffn_in['w2'], 'L1_ffn_ln1': _L1_ffn_in['ln1'], 'L1_ffn_ln2': _L1_ffn_in['ln2'], 'L1_c': _L1_c, 'L1_wmod': _L1_wmod}
    _x0 = _d['L0_attn_x']
    _d['L0_attn_x'] = jax.random.normal(jax.random.fold_in(jax.random.key(seed), 1), (2, 2048, 128), dtype=_x0.dtype)
    del _x0
    return _d

def reference(L0_attn_x, L0_attn_Wz, L0_attn_Win, L0_attn_Wzg, L0_attn_Wout, L0_attn_dt_bias, L0_attn_A_log, L0_attn_D_param, L0_ffn_up, L0_ffn_gate, L0_ffn_down, L0_ffn_router, L0_ffn_w_up_s, L0_ffn_w_gate_s, L0_ffn_w_down_s, L0_c, L0_wmod, L1_attn_Lambda, L1_attn_log_dt, L1_attn_B, L1_attn_C, L1_attn_D, L1_ffn_attention_mask, L1_ffn_position_ids, L1_ffn_router_w, L1_ffn_router_b, L1_ffn_wq, L1_ffn_wk, L1_ffn_wv, L1_ffn_wo, L1_ffn_w1, L1_ffn_w2, L1_ffn_ln1, L1_ffn_ln2, L1_c, L1_wmod):

    def _L0_attn_ref(x, Wz, Win, Wzg, Wout, dt_bias, A_log, D_param):
        import jax, jax.numpy as jnp
        import numpy as np
        D_MODEL = 128
        N_HEADS = 8
        D_STATE = 64
        HEAD_DIM = 64
        EXPAND = 2
        D_INNER = N_HEADS * HEAD_DIM
        BATCH = 2
        SEQ = 512

        def _ssd_scan(X, delta, B_ssm, C_ssm, A_log):
            neg_A = -jnp.exp(A_log)

            def step(h, inp):
                X_t, d_t, B_t, C_t = inp
                dA = jnp.exp(d_t * neg_A)
                dB = d_t[..., None] * B_t[:, None, :]
                h = dA[..., None, None] * h + X_t[..., None] * dB[:, :, None, :]
                y_t = jnp.einsum('bhpn,bn->bhp', h, C_t)
                return (h, y_t)
            b, t, hh, p = X.shape
            n = B_ssm.shape[-1]
            h0 = jnp.zeros((b, hh, p, n), dtype=X.dtype)
            xs = (jnp.swapaxes(X, 0, 1), jnp.swapaxes(delta, 0, 1), jnp.swapaxes(B_ssm, 0, 1), jnp.swapaxes(C_ssm, 0, 1))
            h_last, ys = jax.lax.scan(step, h0, xs)
            return (jnp.swapaxes(ys, 0, 1), h_last)

        def _reference_tuple_inner(x, Wz, Win, Wzg, Wout, dt_bias, A_log, D_param):
            b, t, _ = x.shape
            z = x @ Wz
            ssm_in = x @ Win
            B_ssm = ssm_in[..., :D_STATE]
            C_ssm = ssm_in[..., D_STATE:2 * D_STATE]
            dt_raw = ssm_in[..., 2 * D_STATE:2 * D_STATE + N_HEADS]
            X = ssm_in[..., 2 * D_STATE + N_HEADS:].reshape(b, t, N_HEADS, HEAD_DIM)
            delta = jax.nn.softplus(dt_raw + dt_bias)
            y, h_last = _ssd_scan(X, delta, B_ssm, C_ssm, A_log)
            y = y + D_param[None, None, :, None] * X
            y_flat = y.reshape(b, t, D_INNER)
            z_gated = jax.nn.silu(z) @ Wzg
            output = y_flat * z_gated @ Wout
            return (output, h_last)
        return _reference_tuple_inner(x, Wz, Win, Wzg, Wout, dt_bias, A_log, D_param)[0]

    def _L0_ffn_ref(x, up, gate, down, router, w_up_s, w_gate_s, w_down_s):
        import jax, jax.numpy as jnp
        import numpy as np
        B, T, C, H, E = (1, 32, 128, 256, 8)
        STD = 0.02
        b, t, c = x.shape
        x_ = x.reshape(b * t, c)
        logits = x_ @ router.T
        idx = jnp.argmax(logits, axis=-1)
        onehot = jax.nn.one_hot(idx, router.shape[0], dtype=x.dtype)
        u = jnp.einsum('bc,ehc->ebh', x_, up)
        g = jnp.einsum('bc,ehc->ebh', x_, gate)
        h = jax.nn.silu(g) * u
        ye = jnp.einsum('ebh,ech->ebc', h, down)
        y = jnp.einsum('ebc,be->bc', ye, onehot)
        ys = jax.nn.silu(x_ @ w_gate_s.T) * (x_ @ w_up_s.T) @ w_down_s.T
        return (y + ys).reshape(b, t, c)

    def _L1_attn_ref(u, Lambda, log_dt, B, C, D):
        import jax, jax.numpy as jnp
        import numpy as np
        dt = jnp.exp(log_dt)
        a = jnp.exp(-dt * jnp.exp(Lambda))
        Bu = jnp.einsum('bld,nd->bln', u, B)

        def step(x, bu_t):
            x = a * x + bu_t
            return (x, x)
        x0 = jnp.zeros((u.shape[0], Lambda.shape[0]), dtype=u.dtype)
        _, xs = jax.lax.scan(step, x0, jnp.swapaxes(Bu, 0, 1))
        xs = jnp.swapaxes(xs, 0, 1)
        return jnp.einsum('bln,dn->bld', xs, C) + D * u

    def _L1_ffn_ref(x, attention_mask, position_ids, router_w, router_b, wq, wk, wv, wo, w1, w2, ln1, ln2):
        import jax, jax.numpy as jnp
        import numpy as np
        B, S, D, H, F = (4, 512, 128, 16, 512)
        CAP = 0.125
        ROPE_BASE = 10000.0

        def rmsnorm(x, g):
            return x * jax.lax.rsqrt(jnp.mean(x * x, -1, keepdims=True) + 1e-06) * g

        def rope(t, pos):
            hd = t.shape[-1]
            inv = 1.0 / ROPE_BASE ** (jnp.arange(0, hd, 2, dtype=jnp.float32) / hd)
            f = pos[:, None, :, None].astype(jnp.float32) * inv
            emb = jnp.concatenate([f, f], axis=-1)
            cos, sin = (jnp.cos(emb), jnp.sin(emb))
            rot = jnp.concatenate([-t[..., hd // 2:], t[..., :hd // 2]], axis=-1)
            return t * cos + rot * sin
        b, s, d = x.shape
        hd = d // H
        weights = (x @ router_w)[..., 0] + router_b[0]
        k = int(CAP * s)
        topv, topi = jax.lax.top_k(weights, k)
        thr = topv[:, -1]
        sel_mask = (weights > thr[:, None]).astype(x.dtype)
        kc = k - 1
        sel_idx = jnp.sort(topi[:, :kc], axis=1)
        bidx = jnp.arange(b)[:, None]
        x_sel = x[bidx, sel_idx]
        pos_sel = position_ids[bidx, sel_idx]
        w_sel = weights[bidx, sel_idx]
        m = attention_mask[:, 0]
        m_sel = m[bidx[:, :, None], sel_idx[:, :, None], sel_idx[:, None, :]]
        hn = rmsnorm(x_sel, ln1)

        def heads(t):
            return t.reshape(b, kc, H, hd).transpose(0, 2, 1, 3)
        q = rope(heads(hn @ wq), pos_sel)
        kk = rope(heads(hn @ wk), pos_sel)
        v = heads(hn @ wv)
        sc = jnp.einsum('bhqd,bhkd->bhqk', q, kk) / np.sqrt(hd).astype(np.float32)
        sc = sc + m_sel[:, None]
        a = jax.nn.softmax(sc, axis=-1)
        o = jnp.einsum('bhqk,bhkd->bhqd', a, v).transpose(0, 2, 1, 3).reshape(b, kc, d) @ wo
        x1 = x_sel + o
        x2 = x1 + jax.nn.gelu(rmsnorm(x1, ln2) @ w1) @ w2
        proc = x2 * w_sel[..., None]
        out = jnp.zeros_like(x).at[bidx, sel_idx].set(proc)
        return out + x * (1.0 - sel_mask)[..., None]
    x = L0_attn_x
    mod = (_silu(L0_c) @ L0_wmod).reshape(L0_c.shape[0], 6, 1, -1)
    sa, ca, ga, sb, cb, gb = (mod[:, 0], mod[:, 1], mod[:, 2], mod[:, 3], mod[:, 4], mod[:, 5])
    ga = (2 * (ga >= 0) - 1) * jnp.maximum(jnp.abs(ga), 0.25)
    gb = (2 * (gb >= 0) - 1) * jnp.maximum(jnp.abs(gb), 0.25)
    h = _layernorm(x, axis=-1) * (1 + ca) + sa
    x = x + ga * _L0_attn_ref(h, L0_attn_Wz, L0_attn_Win, L0_attn_Wzg, L0_attn_Wout, L0_attn_dt_bias, L0_attn_A_log, L0_attn_D_param)
    h = _layernorm(x, axis=-1) * (1 + cb) + sb
    x = x + gb * _L0_ffn_ref(h, L0_ffn_up, L0_ffn_gate, L0_ffn_down, L0_ffn_router, L0_ffn_w_up_s, L0_ffn_w_gate_s, L0_ffn_w_down_s)
    mod = (_silu(L1_c) @ L1_wmod).reshape(L1_c.shape[0], 6, 1, -1)
    sa, ca, ga, sb, cb, gb = (mod[:, 0], mod[:, 1], mod[:, 2], mod[:, 3], mod[:, 4], mod[:, 5])
    ga = (2 * (ga >= 0) - 1) * jnp.maximum(jnp.abs(ga), 0.25)
    gb = (2 * (gb >= 0) - 1) * jnp.maximum(jnp.abs(gb), 0.25)
    h = _layernorm(x, axis=-1) * (1 + ca) + sa
    x = x + ga * _L1_attn_ref(h, L1_attn_Lambda, L1_attn_log_dt, L1_attn_B, L1_attn_C, L1_attn_D)
    h = _layernorm(x, axis=-1) * (1 + cb) + sb
    x = x + gb * _L1_ffn_ref(h, L1_ffn_attention_mask, L1_ffn_position_ids, L1_ffn_router_w, L1_ffn_router_b, L1_ffn_wq, L1_ffn_wk, L1_ffn_wv, L1_ffn_wo, L1_ffn_w1, L1_ffn_w2, L1_ffn_ln1, L1_ffn_ln2)
    return x

_drawn_inputs = setup_inputs


def setup_inputs(seed=0):
    import zlib

    import numpy as np

    out = dict(_drawn_inputs(seed))
    spreads = {'L0_attn_dt_bias': (-2.3025851249694824, 0.6),
     'L0_attn_D_param': (1.0, 0.6),
     'L1_attn_D': (0.0, 2.0),
     'L1_ffn_ln1': (1.0, 0.6),
     'L1_ffn_ln2': (1.0, 0.6)}
    factors = {'L0_attn_Wz': 8.0,
     'L0_attn_Win': 8.0,
     'L0_attn_Wzg': 8.0,
     'L0_attn_Wout': 8.0,
     'L0_attn_A_log': 8.0,
     'L0_ffn_up': 21.942,
     'L0_ffn_gate': 24.458,
     'L0_ffn_down': 21.85,
     'L0_ffn_router': 23.55,
     'L0_ffn_w_up_s': 22.099,
     'L0_ffn_w_gate_s': 24.613,
     'L0_ffn_w_down_s': 22.235,
     'L0_c': 8.0,
     'L0_wmod': 8.0,
     'L1_ffn_router_w': 24.836,
     'L1_ffn_wq': 28.738,
     'L1_ffn_wk': 28.445,
     'L1_ffn_wv': 27.351,
     'L1_ffn_wo': 27.596,
     'L1_ffn_w1': 33.707,
     'L1_ffn_w2': 29.046}
    for name, (base, spread) in spreads.items():
        noise = np.random.default_rng([zlib.crc32(name.encode()), seed]).standard_normal(out[name].shape)
        drawn = base * np.exp(spread * noise) if base else spread * noise
        out[name] = jnp.asarray(drawn.astype(out[name].dtype))
    for name, factor in factors.items():
        out[name] = (out[name] * factor).astype(out[name].dtype)
    return out
```

```python
from contextlib import ExitStack

import numpy as np

import concourse.bass as bass
from concourse import mybir
from concourse.alu_op_type import AluOpType as ALU

ACT = mybir.ActivationFunctionType
AX = mybir.AxisListType
F32 = mybir.dt.float32
BF16 = mybir.dt.bfloat16
I32 = mybir.dt.int32
U32 = mybir.dt.uint32

P = 128
B = 2
T = 2048
D = 128
NT = T // P
GT = 4
NG = NT // GT
GW = GT * P
H = 8
HD = 64
NS = 64
DI = H * HD
ZW = 2 * D
EX = 8
HID = 256
LN_EPS = 1e-5
RMS_EPS = 1e-6
AH = 16
AD = D // AH
FF = 512
ML = 512
TOPK = T // 8
SEL = TOPK - 1
NSEL = TOPK // P
ROPE_BASE = 10000.0


class Chain:

    def __init__(self, eng, sem):
        self.eng, self.sem, self.base, self.k = eng, sem, 0, 0

    def link(self, ins):
        self.k += 1
        ins.then_inc(self.sem, 1)
        self.eng.wait_ge(self.sem, self.base + self.k)

    def loop(self, count, per):
        outer = self.base + self.k
        with self.eng.Fori(0, count) as i:
            self.base, self.k = i * per + outer, 0
            yield i, self.link
            assert self.k == per, f"{self.k} links in a loop of {per}"
        self.base, self.k = outer + count * per, 0


def build(nc, io, out, dbg=None):
    ctx = ExitStack()
    with ctx:
        def sb(name, shape, dt=F32):
            return ctx.enter_context(nc.sbuf_tensor(name, shape, dt))

        def sem(name):
            return ctx.enter_context(nc.semaphore(name))

        bank = [ctx.enter_context(nc.psum_tensor(f"bank{i}", [P, 512], F32)) for i in range(8)]

        xs = sb("xs", [P, B, NT, D])
        stats = sb("stats", [P, B * NT, 6])
        mean = sb("mean", [P, B * NT])
        var = sb("var", [P, B * NT])
        std = sb("std", [P, B * NT])
        rstd = sb("rstd", [P, B * NT])
        tmp_ln = sb("tmp_ln", [P, B * NT])
        xhat = sb("xhat", [P, B, GT, D])
        hT = sb("hT", [P, B, GW])

        ident = sb("ident", [P, P])
        upper = sb("upper", [P, P])
        lower = sb("lower", [P, P])
        ones = sb("ones", [P, P])
        eps_ln = sb("eps_ln", [P, 1])

        cT = [sb(f"cT{l}", [P, B]) for l in range(2)]
        cE = [sb(f"cE{l}", [P, B]) for l in range(2)]
        cS = [sb(f"cS{l}", [P, B]) for l in range(2)]
        wmod = [sb(f"wmod{l}", [P, 6 * D]) for l in range(2)]
        modT = [sb(f"modT{l}", [P, 6, B]) for l in range(2)]

        gabc = [sb(f"gabc{l}", [P, B, D]) for l in range(2)]
        crep = [sb(f"crep{l}", [P, B, P]) for l in range(2)]
        gt0 = sb("gt0", [P, B, D])
        gt1 = sb("gt1", [P, B, D])

        keep, ssd_mem = sb, ctx.enter_context(ExitStack())

        def sb(name, shape, dt=F32):
            return ssd_mem.enter_context(nc.sbuf_tensor(name, shape, dt))

        wz = sb("wz", [P, ZW])
        win = sb("win", [P, 2 * NS + H + DI])
        wbdt = sb("wbdt", [P, NS + H])
        wzg = sb("wzg", [P, 2, DI])
        wout = sb("wout", [P, 4, D])
        woutg = sb("woutg", [P, B, 4, D])
        dtb = sb("dtb", [P, H])
        alog = sb("alog", [P, H])
        expa = sb("expa", [P, H])
        dpar = sb("dpar", [P, H])

        PK_H, PK_S, PK_B = 0, P, P + 2 * P
        PKW = P + 2 * P + NS
        pk = sb("pk", [P, B, NT, PKW])
        bcT = sb("bcT", [P, NT, 2, P])
        pk_slot = sb("pk_slot", [P, B, PKW])
        bc_slot = sb("bc_slot", [P, 2, P])

        TH = B * NT * H
        dts = sb("dts", [P, B, NT, H])
        v_ = sb("v_", [P, TH])
        e_ = sb("e_", [P, TH])
        u_ = sb("u_", [P, TH])
        l_ = sb("l_", [P, TH])
        r_ = sb("r_", [P, TH])
        delta = sb("delta", [P, B, NT, H])
        a_dec = sb("a_dec", [P, B, NT, H])
        e_cum = sb("e_cum", [P, B, NT, H])
        e_rest = sb("e_rest", [P, B, NT, H])
        dw = sb("dw", [P, B, NT, H])
        e_all = sb("e_all", [P, NT, H])

        seg_rhs = sb("seg_rhs", [P, B, H, P])
        E = sb("E", [P, B, H, P])
        M = sb("M", [P, B, H, P])
        Gm = sb("Gm", [P, B, P])
        dX = sb("dX", [P, B, DI])
        dXw = sb("dXw", [P, B, DI])
        Xsb = sb("Xsb", [P, B, DI])
        XD = sb("XD", [P, B, DI])
        yoff = sb("yoff", [P, B, DI])
        ysum = sb("ysum", [P, B, DI])
        y2 = sb("y2", [P, B, DI])
        yg = sb("yg", [P, B, DI])
        ygT = sb("ygT", [P, B, 4, P])
        S = sb("S", [P, DI])
        Sd = sb("Sd", [P, DI])

        ssd_mem.close()
        sb = keep

        s4_B = sb("s4_B", [P, NS])
        s4_C = sb("s4_C", [P, D])
        s4_Cg = sb("s4_Cg", [P, D])
        s4_lam = sb("s4_lam", [P, 1])
        s4_ldt = sb("s4_ldt", [P, 1])
        s4_D = sb("s4_D", [P, 1])
        s4_a = sb("s4_a", [P, 1])
        s4_abc = sb("s4_abc", [P, GW])
        s4_Dg = sb("s4_Dg", [P, B, D])
        s4_x = sb("s4_x", [P, GW])
        s4_carry = sb("s4_carry", [P, 1])

        NJ = 15
        NSTEP = 8
        NS4 = B * NSEL
        rows = sb("rows", [P, B, 3, D])
        w_all = sb("w_all", [P, B, NT])
        rw_row = sb("rw_row", [P, D])
        rb_col = sb("rb_col", [P, 1])
        ln_row = sb("ln_row", [P, 2, D])
        wqkv = sb("wqkv", [P, 3 * D])
        wo = sb("wo", [P, D])
        w1 = sb("w1", [P, FF])
        w2 = sb("w2", [P, FF // P, D])
        jt = sb("jt", [P, NJ], I32)
        scan_ones = sb("scan_ones", [P, NT])
        iota256 = sb("iota256", [P, TOPK])
        tokid = sb("tokid", [P, NT, 2], BF16)
        inv = sb("inv", [P, AD // 2])
        eps_rms = sb("eps_rms", [P, 1])
        headmask = sb("headmask", [P, AH])
        iotap = sb("iotap", [P, ML // P])

        moe_mem = ctx.enter_context(ExitStack())

        def sb(name, shape, dt=F32):
            return moe_mem.enter_context(nc.sbuf_tensor(name, shape, dt))

        NE = EX + 1
        wup = sb("wup", [P, NE, HID])
        wgate = sb("wgate", [P, NE, HID])
        wdown = sb("wdown", [P, NE, 2, D])
        wrouter = sb("wrouter", [P, EX])
        ident16 = sb("ident16", [P, P], BF16)
        eighths = sb("eighths", [P, EX])
        logits = sb("logits", [P, GT, EX])
        lmax = sb("lmax", [P, GT])
        picked = sb("picked", [P, GT, EX])
        onehot = sb("onehot", [P, GT, EX], BF16)
        hTe = sb("hTe", [P, 2, GW])
        sg = sb("sg", [P, 2, GW])
        hid = sb("hid", [P, 2, 2, GW])
        yT = sb("yT", [P, B, GW])

        moe_mem.close()
        sb = keep
        hx = sb("hx", [P, B, GT, 2 * D + 1])
        dflt = sb("dflt", [P, B, GT, D])
        hprod = sb("hprod", [P, GT, D])
        wred = sb("wred", [P, GT])
        J = sb("J", [P, NSTEP, NJ], I32)
        pre = sb("pre", [P, B], I32)
        digit = sb("digit", [P, B], I32)
        digitf = sb("digitf", [P, B])
        cand = sb("cand", [P, B, NJ], I32)
        candt = sb("candt", [P, B, NJ], I32)
        candf = sb("candf", [P, B, NJ], I32)
        cmp_ = sb("cmp_", [P, B, NJ, NT])
        cnt = sb("cnt", [P, B, NJ])
        ge256 = sb("ge256", [P, B, NJ])
        thr_t = sb("thr_t", [P, B], I32)
        thr = sb("thr", [P, B], I32)
        gteq = sb("gteq", [P, 2, B, NT])
        tot = sb("tot", [P, 3, B, NT])
        incl = sb("incl", [P, 2, B, NT])
        ngt = sb("ngt", [P, B])
        sel = sb("sel", [P, B, NT])
        pos = sb("pos", [P, B, NT])
        choose = sb("choose", [P, B, NT, TOPK], BF16)
        picks = sb("picks", [P, NS4, 2])
        idx = sb("idx", [P, NS4])
        cidx = sb("cidx", [P, NS4])
        gidx = sb("gidx", [P, 2, NS4], I32)
        sx = sb("sx", [P, NS4, 2 * D + 1])
        smask = sb("smask", [P, NS4, ML])
        spos = sb("spos", [P, NS4], I32)
        ang = sb("ang", [P, 2, NS4, AD // 2])
        angk = sb("angk", [P, 2, NS4, AD // 2])
        angi = sb("angi", [P, 2, NS4, AD // 2], I32)
        sc_ = sb("sc_", [P, 2, NS4, AD // 2])
        ss = sb("ss", [P, NS4])
        sroot = sb("sroot", [P, NS4])
        srr = sb("srr", [P, NS4])
        st = sb("st", [P, NS4])
        squares = sb("squares", [P, 2, NS4, D])
        hn = sb("hn", [P, NS4, D])
        hnT = sb("hnT", [P, NS4 * P])
        qk = sb("qk", [P, NS4, 2 * D])
        qks = sb("qks", [P, 2 * D])
        qkc = sb("qkc", [P, 2 * D])
        vv = sb("vv", [P, NS4, D])
        qT = sb("qT", [P, NS4 * P])
        kT = sb("kT", [P, NS4 * P])
        kTm = sb("kTm", [P, AH, TOPK])
        colsel = sb("colsel", [P, ML // P, TOPK])
        maskT = sb("maskT", [P, ML // P, P])
        msel = sb("msel", [P, TOPK])
        sc = sb("sc", [P, AH, TOPK])
        smax = sb("smax", [P, AH])
        ssum = sb("ssum", [P, AH])
        sinv = sb("sinv", [P, AH])
        pT = sb("pT", [P, AH * NSEL, P])
        on = sb("on", [P, NS4, D])
        onT = sb("onT", [P, NS4 * P])
        x1 = sb("x1", [P, NS4, D])
        hid1 = sb("hid1", [P, FF // P, NS4 * P])
        x2 = sb("x2", [P, NS4, D])
        notsel = sb("notsel", [P, NS4])
        res = sb("res", [P, NS4, D])

        hx_dram = nc.dram_tensor("hx_scratch", (B * T, 2 * D + 1), F32, kind="Internal").ap()

        def now(n):
            return n + 3

        def back1(n):
            return n + 2

        def back2(n):
            return n + 1

        own = {}

        def handoff(engine, *names):
            got = [sem(x) for x in names]
            own.setdefault(engine, []).extend(got)
            return got

        def credit(eng, engine):
            for s_ in own.get(engine, []):
                eng.sem_inc(s_, 2)

        dve_self = sem("dve_self")
        act_self = sem("act_self")
        pool_self = sem("pool_self")
        mod_loaded = sem("mod_loaded")
        x_loaded = [sem(f"x_loaded{i}") for i in range(2)]
        w_loaded = sem("w_loaded")
        consts_ready = sem("consts_ready")
        c_exp = sem("c_exp")
        c_silu = sem("c_silu")
        mod_ps = sem("mod_ps")
        mod_ready = sem("mod_ready")
        ga_ps = sem("ga_ps")
        ga_done = sem("ga_done")
        var_ready = sem("var_ready")
        std_ready = sem("std_ready")
        (xhat_ready, bc_kept, tok_kept) = handoff("dve", "xhat_ready", "bc_kept", "tok_kept")
        (trans_ps, z_ps, bc_ps, tok_ps) = handoff("pe", "trans_ps", "z_ps", "bc_ps", "tok_ps")
        (hT_ready, z_kept) = handoff("act", "hT_ready", "z_kept")
        (hT_kept,) = handoff("pool", "hT_kept")
        v_abs = sem("v_abs")
        e_exp = sem("e_exp")
        u_ready = sem("u_ready")
        ln_ready = sem("ln_ready")
        a_ready = sem("a_ready")
        cum_ps = sem("cum_ps")
        decays_ready = sem("decays_ready")
        dw_ready = sem("dw_ready")
        pk_loaded = [sem(f"pk_loaded{b}") for b in range(B)]
        (g_ps, segA_ps, segB_ps, x_ps, zg_ps, off_ps, diag_ps, ds_ps, yT_ps, out_ps) = handoff(
            "pe", "g_ps", "segA_ps", "segB_ps", "x_ps", "zg_ps", "off_ps", "diag_ps", "ds_ps", "yT_ps", "out_ps")
        (gm_done, dx_done, yoff_done, m_ready, y2_done, yg_done, s_upd, xres_done) = handoff(
            "dve", "gm_done", "dx_done", "yoff_done", "m_ready", "y2_done", "yg_done", "s_upd", "xres_done")
        (expA_done, expB_done, xsb_done, ygT_done) = handoff("act", "expA_done", "expB_done", "xsb_done", "ygT_done")
        (segrhs_ready, ysum_ready) = handoff("pool", "segrhs_ready", "ysum_ready")
        out_written = sem("out_written")
        moe_loaded = sem("moe_loaded")
        s4_loaded = sem("s4_loaded")
        moe_consts = sem("moe_consts")
        (xhat2_ready, onehot_ready, hTe_ready, hid_ready, xres2_done) = handoff(
            "dve", "xhat2_ready", "onehot_ready", "hTe_ready", "hid_ready", "xres2_done")
        (trans2_ps, router_ps, bcast_ps, gate_ps, up_ps, down_ps, yT2_ps) = handoff(
            "pe", "trans2_ps", "router_ps", "bcast_ps", "gate_ps", "up_ps", "down_ps", "yT2_ps")
        (hT2_ready, silu_done, yT2_kept) = handoff("act", "hT2_ready", "silu_done", "yT2_kept")
        s4_exp1 = sem("s4_exp1")
        s4_prod = sem("s4_prod")
        s4_exp2 = sem("s4_exp2")
        s4_ready = sem("s4_ready")
        (xhat3_ready, scan_done, xres3_done) = handoff("dve", "xhat3_ready", "scan_done", "xres3_done")
        (trans3_ps, bu_ps, s4out_ps) = handoff("pe", "trans3_ps", "bu_ps", "s4out_ps")
        (hT3_ready,) = handoff("act", "hT3_ready")

        (xhat4_ready, h4_ready, w4_ready) = handoff("dve", "xhat4_ready", "h4_ready", "w4_ready")
        (hxx_ready, dflt_ready) = handoff("pool", "hxx_ready", "dflt_ready")
        hx_stored = [sem(f"hx_stored{b}") for b in range(B)]
        dflt_stored = [sem(f"dflt_stored{b}") for b in range(B)]
        single = {}

        def once(name):
            if name not in single:
                single[name] = sem(name)
            return single[name]

        block = ctx.enter_context(nc.Block())

        x_t = io["L0_attn_x"].rearrange("b (c p) d -> p b c d", p=P)
        out_t = out.rearrange("b (c p) d -> p b c d", p=P)
        W_ALL = 16 * 7
        MOE_ALL = 16 * 7
        S4_ALL = 16 * 7
        L1_ALL = 16 * 10

        def flat(ap):
            return ap.rearrange("p a d -> p (a d)")

        def at(t, b, c):
            return flat(t[:, b, bass.ds(c, 1), :])

        def per_head(ap):
            return ap.unsqueeze(2).to_broadcast([P, H, HD])

        def heads(ap):
            return ap.rearrange("p (h d) -> p h d", h=H)

        @block.sync
        def _(sp):
            for l in range(2):
                sp.dma_start(cT[l][:], io[f"L{l}_cT"]).then_inc(mod_loaded, 16)
                sp.dma_start(wmod[l][:], io[f"L{l}_wmod"]).then_inc(mod_loaded, 16)
            for half in range(2):
                c0 = half * NT // 2
                for b in range(B):
                    sp.dma_start(xs[:, b, c0:c0 + NT // 2, :], x_t[:, b, c0:c0 + NT // 2, :]).then_inc(x_loaded[half], 16)
            sp.dma_start(wz[:], io["L0_attn_Wz"]).then_inc(w_loaded, 16)
            sp.dma_start(win[:], io["L0_attn_Win"]).then_inc(w_loaded, 16)
            sp.dma_start(wzg[:], io["L0_attn_Wzg"].rearrange("(k p) n -> p k n", p=P)).then_inc(w_loaded, 16)
            sp.dma_start(wout[:], io["L0_attn_Wout"].rearrange("(k p) n -> p k n", p=P)).then_inc(w_loaded, 16)
            sp.dma_start(dtb[:], io["L0_attn_dt_bias"].partition_broadcast(P)).then_inc(w_loaded, 16)
            sp.dma_start(alog[:], io["L0_attn_A_log"].partition_broadcast(P)).then_inc(w_loaded, 16)
            sp.dma_start(dpar[:], io["L0_attn_D_param"].partition_broadcast(P)).then_inc(w_loaded, 16)

            sp.wait_ge(hT_kept, now(2 * NG - 1))
            sp.wait_ge(z_kept, now(2 * NG - 1))
            sp.wait_ge(tok_kept, now(2 * NG - 1))
            sp.wait_ge(bc_kept, now(2 * NG - 1))
            with sp.Fori(0, NT) as c:
                for b in range(B):
                    sp.wait_ge(ds_ps, back2(2 * c + b))
                    sp.dma_start(pk_slot[:, b, :], at(pk, b, c)).then_inc(pk_loaded[b], 16)
                    sp.dma_start(bc_slot[b * NS:(b + 1) * NS], bcT[b * NS:(b + 1) * NS, bass.ds(c, 1), :, :].rearrange("p a k t -> p (a k) t")).then_inc(pk_loaded[b], 16)
            sp.wait_ge(out_ps, now(2 * NT - 1))
            sp.wait_ge(xres_done, now(2 * NT - 1))
            for w, src in ((wup, "up"), (wgate, "gate")):
                sp.dma_start(w[:, 0:EX], io[f"{src}T"].rearrange("e c h -> c e h")).then_inc(moe_loaded, 16)
                sp.dma_start(w[:, EX], io[f"{src}_sT"]).then_inc(moe_loaded, 16)
            sp.dma_start(wdown[:, 0:EX], io["downT"].rearrange("e (k p) c -> p e k c", p=P)).then_inc(moe_loaded, 16)
            sp.dma_start(wdown[:, EX], io["down_sT"].rearrange("(k p) c -> p k c", p=P)).then_inc(moe_loaded, 16)
            sp.dma_start(wrouter[:], io["routerT"]).then_inc(moe_loaded, 16)
            sp.dma_start(s4_B[:], io["s4_BT"]).then_inc(s4_loaded, 16)
            for b in range(B):
                sp.dma_start(s4_C[b * NS:(b + 1) * NS], io["s4_CT"]).then_inc(s4_loaded, 16)
                sp.dma_start(s4_lam[b * NS:(b + 1) * NS], io["L1_attn_Lambda"].unsqueeze(1)).then_inc(s4_loaded, 16)
            sp.dma_start(s4_ldt[:], io["L1_attn_log_dt"].partition_broadcast(P)).then_inc(s4_loaded, 16)
            sp.dma_start(s4_D[:], io["L1_attn_D"].unsqueeze(1)).then_inc(s4_loaded, 16)
            for j, name in enumerate(("wq", "wk", "wv")):
                sp.dma_start(wqkv[:, j * D:(j + 1) * D], io[f"L1_ffn_{name}"]).then_inc(once("l1_loaded"), 16)
            sp.dma_start(wo[:], io["L1_ffn_wo"]).then_inc(once("l1_loaded"), 16)
            sp.dma_start(w1[:], io["L1_ffn_w1"]).then_inc(once("l1_loaded"), 16)
            sp.dma_start(w2[:], io["L1_ffn_w2"].rearrange("(k p) d -> p k d", p=P)).then_inc(once("l1_loaded"), 16)
            for j in range(2):
                sp.dma_start(ln_row[:, j], io[f"L1_ffn_ln{j + 1}"].partition_broadcast(P)).then_inc(once("l1_loaded"), 16)
            sp.dma_start(rw_row[:], io["L1_ffn_router_w"].rearrange("d a -> (d a)").partition_broadcast(P)).then_inc(once("l1_loaded"), 16)
            sp.dma_start(rb_col[:], io["L1_ffn_router_b"].partition_broadcast(P)).then_inc(once("l1_loaded"), 16)
            hx_t = hx_dram.rearrange("(b c p) d -> p b c d", p=P, b=B)
            for b in range(B):
                sp.sem_inc(hx_stored[b], 16)
                sp.sem_inc(dflt_stored[b], 16)
            with sp.Fori(0, NG) as g:
                for b in range(B):
                    n = 2 * g + b
                    sp.wait_ge(w4_ready, now(n))
                    sp.wait_ge(hxx_ready, now(n))
                    sp.dma_start(hx_t[:, b, bass.ds(g * GT, GT), :], hx[:, b]).then_inc(hx_stored[b], 16)
                    sp.wait_ge(dflt_ready, now(n))
                    sp.dma_start(out_t[:, b, bass.ds(g * GT, GT), :], dflt[:, b]).then_inc(dflt_stored[b], 16)
            for b in range(B):
                sp.wait_ge(dflt_stored[b], 16 * (NG + 1))
            sp.wait_ge(once("rows_scattered"), 16 * NS4)

        @block.gpsimd
        def _(pool):
            credit(pool, "pool")
            ch = Chain(pool, pool_self)
            pool.memset(eps_ln[:], LN_EPS)
            pool.memset(ident[:], 0.0)
            pool.memset(upper[:], 1.0)
            ch.link(pool.memset(lower[:], 1.0))
            pool.affine_select(out=ident[:], in_=ident[:], compare_op=ALU.not_equal, fill=1.0, base=0,
                               pattern=[[-1, P]], channel_multiplier=1)
            pool.affine_select(out=upper[:], in_=upper[:], compare_op=ALU.is_ge, fill=0.0, base=0,
                               pattern=[[1, P]], channel_multiplier=-1)
            pool.affine_select(out=lower[:], in_=lower[:], compare_op=ALU.is_gt, fill=0.0, base=0,
                               pattern=[[-1, P]], channel_multiplier=1)
            pool.memset(S[:], 0.0)
            pool.memset(ones[:], 1.0).then_inc(consts_ready, 1)
            with pool.Fori(0, NG) as g:
                for b in range(B):
                    pool.wait_ge(hT_ready, now(2 * g + b))
                    pool.tensor_copy(pk[:, b, bass.ds(g * GT, GT), PK_H:PK_H + P],
                                     hT[:, b, :].rearrange("p (q t) -> p q t", q=GT)).then_inc(hT_kept, 1)
            pool.wait_ge(a_ready, 1)
            for (c, links) in ch.loop(NT, B):
                for b in range(B):
                    n = 2 * c + b
                    pool.wait_ge(segA_ps, back2(n))
                    pool.wait_ge(segB_ps, back2(n))
                    pool.tensor_tensor(seg_rhs[:, b], upper[:].unsqueeze(1).to_broadcast([P, H, P]),
                                       at(a_dec, b, c).unsqueeze(2).to_broadcast([P, H, P]), ALU.mult).then_inc(segrhs_ready, 1)
                for b in range(B):
                    n = 2 * c + b
                    pool.wait_ge(xsb_done, now(n))
                    links(pool.tensor_tensor(heads(XD[:, b]), heads(Xsb[:, b]), per_head(dpar[:]), ALU.mult))
                    pool.wait_ge(yoff_done, now(n))
                    pool.wait_ge(y2_done, back2(n))
                    pool.tensor_tensor(ysum[:, b], yoff[:, b], XD[:, b], ALU.add).then_inc(ysum_ready, 1)
            pool.wait_ge(out_ps, now(2 * NT - 1))
            pool.wait_ge(xres_done, now(2 * NT - 1))
            pool.tensor_copy(ident16[:], ident[:])
            pool.iota(eighths[:], pattern=[[-1, EX]], base=EX, channel_multiplier=0, allow_small_or_imprecise_dtypes=True)
            pool.memset(s4_carry[:], 0.0).then_inc(moe_consts, 1)
            pool.iota(jt[:], pattern=[[1, NJ]], base=1, channel_multiplier=0)
            pool.iota(iota256[:], pattern=[[1, TOPK]], base=0, channel_multiplier=0, allow_small_or_imprecise_dtypes=True)
            pool.iota(tokid[:, :, 0], pattern=[[1, NT]], base=0, channel_multiplier=0, allow_small_or_imprecise_dtypes=True)
            pool.iota(tokid[:, :, 1], pattern=[[0, NT]], base=0, channel_multiplier=1, allow_small_or_imprecise_dtypes=True)
            pool.iota(iotap[:], pattern=[[P, ML // P]], base=0, channel_multiplier=1, allow_small_or_imprecise_dtypes=True)
            pool.memset(scan_ones[:], 1.0)
            pool.memset(eps_rms[:], RMS_EPS)
            for i in range(AD // 2):
                pool.memset(inv[:, i:i + 1], float(np.float32(1.0) / np.float32(ROPE_BASE ** (2.0 * i / AD))))
            ch.link(pool.memset(headmask[:], 1.0))
            ch.link(pool.affine_select(out=headmask[:], in_=headmask[:], compare_op=ALU.is_ge, fill=0.0, base=0,
                                       pattern=[[-AD, AH]], channel_multiplier=1))
            pool.affine_select(out=headmask[:], in_=headmask[:], compare_op=ALU.is_ge, fill=0.0, base=AD - 1,
                               pattern=[[AD, AH]], channel_multiplier=-1).then_inc(once("l1_consts"), 1)
            pool.wait_ge(once("rows_ready"), 1)
            for (g, links) in ch.loop(NG, B):
                for b in range(B):
                    n = 2 * g + b
                    pool.wait_ge(hx_stored[b], 16 * (g + 1))
                    pool.wait_ge(dflt_stored[b], 16 * (g + 1))
                    pool.tensor_copy(hx[:, b, :, 0:D], xs[:, b, bass.ds(g * GT, GT), :]).then_inc(hxx_ready, 1)
                    pool.wait_ge(h4_ready, now(n))
                    links(pool.tensor_tensor(dflt[:, b], hx[:, b, :, D:2 * D], rows[:, b, 2:3, :].to_broadcast([P, GT, D]), ALU.mult))
                    pool.tensor_tensor(dflt[:, b], dflt[:, b], hx[:, b, :, 0:D], ALU.add).then_inc(dflt_ready, 1)
            for b in range(B):
                pool.wait_ge(hx_stored[b], 16 * (NG + 1))
            pool.wait_ge(once("gidx_ready"), 1)
            mask_t = io["L1_ffn_attention_mask"].rearrange("b a q k -> (b a q) k")
            pos_t = io["L1_ffn_position_ids"].rearrange("b (q a) -> (b q) a", a=1)
            for s_ in range(NS4):
                tok, mrow = gidx[:, 0, s_:s_ + 1], gidx[:, 1, s_:s_ + 1]
                pool.indirect_dma_start(out=sx[:, s_, :], out_offset=None, in_=hx_dram,
                                        in_offset=bass.IndirectOffsetOnAxis(ap=tok, axis=0)).then_inc(once("sx_loaded"), 16)
            for s_ in range(NS4):
                mrow = gidx[:, 1, s_:s_ + 1]
                pool.indirect_dma_start(out=spos[:, s_:s_ + 1], out_offset=None, in_=pos_t,
                                        in_offset=bass.IndirectOffsetOnAxis(ap=mrow, axis=0)).then_inc(once("spos_loaded"), 16)
            for s_ in range(NS4):
                mrow = gidx[:, 1, s_:s_ + 1]
                pool.indirect_dma_start(out=smask[:, s_, :], out_offset=None, in_=mask_t,
                                        in_offset=bass.IndirectOffsetOnAxis(ap=mrow, axis=0)).then_inc(once("smask_loaded"), 16)
            pool.wait_ge(once("res_ready"), 1)
            for b in range(B):
                pool.wait_ge(dflt_stored[b], 16 * (NG + 1))
            for s_ in range(NS4):
                m = P if s_ % NSEL < NSEL - 1 else P - (TOPK - SEL)
                pool.indirect_dma_start(out=out.rearrange("b t d -> (b t) d"), in_=res[0:m, s_, :], in_offset=None,
                                        out_offset=bass.IndirectOffsetOnAxis(ap=gidx[0:m, 0, s_:s_ + 1], axis=0)).then_inc(once("rows_scattered"), 16)
            pool.wait_ge(once("rows_scattered"), 16 * NS4)

        @block.scalar
        def _(act):
            credit(act, "act")
            act.wait_ge(mod_loaded, 64)
            for l in range(2):
                act.activation(cE[l][:], cT[l][:], ACT.Exp, scale=-1.0).then_inc(c_exp, 1)
            act.wait_ge(var_ready, 1)
            act.wait_ge(consts_ready, 1)
            act.activation(std[:], var[:], ACT.Sqrt, bias=eps_ln[:, 0:1]).then_inc(std_ready, 1)
            act.wait_ge(mod_ready, 1)
            with act.Fori(0, NG) as g:
                for b in range(B):
                    n = 2 * g + b
                    act.wait_ge(trans_ps, now(n))
                    act.wait_ge(hT_kept, back2(n))
                    act.wait_ge(tok_ps, back2(n))
                    act.activation(hT[:, b, :], bank[b][:], ACT.Identity, bias=modT[0][:, 0, b:b + 1],
                                   scale=modT[0][:, 1, b:b + 1]).then_inc(hT_ready, 1)
                for b in range(B):
                    act.wait_ge(z_ps, now(2 * g + b))
                    for k in range(2):
                        ins = act.activation(pk[:, b, bass.ds(g * GT, GT), PK_S + k * P:PK_S + (k + 1) * P],
                                             bank[2 + k][:].rearrange("p (q t) -> p q t", q=GT), ACT.Silu)
                    ins.then_inc(z_kept, 1)
            act.wait_ge(v_abs, 1)
            act.wait_ge(w_loaded, W_ALL)
            act.activation(expa[:], alog[:], ACT.Exp)
            act.activation(e_[:], r_[:], ACT.Exp, scale=-1.0).then_inc(e_exp, 1)
            act.wait_ge(u_ready, 1)
            act.activation(l_[:], u_[:], ACT.Ln).then_inc(ln_ready, 1)
            act.wait_ge(cum_ps, 1)
            act.activation(e_cum[:].rearrange("p b c h -> p (b c h)"), bank[0][:, 0:TH], ACT.Exp)
            act.activation(e_rest[:].rearrange("p b c h -> p (b c h)"), bank[1][:, 0:TH], ACT.Exp)
            for b in range(B):
                ins = act.activation(e_all[b * NS:(b + 1) * NS].rearrange("p c h -> p (c h)"),
                                     bank[2][b * NS:(b + 1) * NS, b * TH // B:(b + 1) * TH // B], ACT.Exp)
            ins.then_inc(decays_ready, 1)
            with act.Fori(0, NT) as c:
                for b in range(B):
                    n = 2 * c + b
                    act.wait_ge(segA_ps, now(n))
                    act.wait_ge(m_ready, back2(n))
                    act.activation(E[:, b, 0:4, :].rearrange("p h t -> p (h t)"), bank[0][:], ACT.Exp).then_inc(expA_done, 1)
                    act.wait_ge(segB_ps, now(n))
                    act.activation(E[:, b, 4:8, :].rearrange("p h t -> p (h t)"), bank[1][:], ACT.Exp).then_inc(expB_done, 1)
                    act.wait_ge(x_ps, now(n))
                    act.wait_ge(ysum_ready, back2(n))
                    act.wait_ge(dx_done, back2(n))
                    act.activation(Xsb[:, b], bank[2][:], ACT.Copy).then_inc(xsb_done, 1)
                for b in range(B):
                    n = 2 * c + b
                    act.wait_ge(yT_ps, now(n))
                    act.wait_ge(out_ps, back2(n))
                    act.activation(ygT[:, b].rearrange("p k t -> p (k t)"), bank[3][:], ACT.Copy).then_inc(ygT_done, 1)
            act.wait_ge(var_ready, 2)
            act.activation(std[:], var[:], ACT.Sqrt, bias=eps_ln[:, 0:1]).then_inc(std_ready, 1)
            with act.Fori(0, NG) as g:
                for b in range(B):
                    n = 2 * g + b
                    act.wait_ge(trans2_ps, now(n))
                    act.activation(hT[:, b, :], bank[0][:], ACT.Identity, bias=modT[0][:, 3, b:b + 1],
                                   scale=modT[0][:, 4, b:b + 1]).then_inc(hT2_ready, 1)
                    for e in range(NE):
                        m = n * NE + e
                        act.wait_ge(gate_ps, now(m))
                        act.wait_ge(hid_ready, back1(m))
                        for k in range(2):
                            ins = act.activation(sg[:, k, :], bank[2 + k][:], ACT.Silu)
                        ins.then_inc(silu_done, 1)
                    act.wait_ge(down_ps, now(n * NE + NE - 1))
                    act.wait_ge(yT2_ps, back2(n))
                    act.activation(yT[:, b, :], bank[1][:], ACT.Copy, scale=modT[0][:, 5, b:b + 1]).then_inc(yT2_kept, 1)
            act.wait_ge(s4_loaded, S4_ALL)
            act.activation(s4_ldt[:], s4_ldt[:], ACT.Exp)
            act.activation(s4_lam[:], s4_lam[:], ACT.Exp).then_inc(s4_exp1, 1)
            act.wait_ge(s4_prod, 1)
            act.activation(s4_a[:], s4_a[:], ACT.Exp, scale=-1.0).then_inc(s4_exp2, 1)
            act.wait_ge(var_ready, 3)
            act.activation(std[:], var[:], ACT.Sqrt, bias=eps_ln[:, 0:1]).then_inc(std_ready, 1)
            with act.Fori(0, NG) as g:
                for b in range(B):
                    n = 2 * g + b
                    act.wait_ge(trans3_ps, now(n))
                    act.wait_ge(s4out_ps, back2(n))
                    act.activation(hT[:, b, :], bank[b][:], ACT.Identity, bias=modT[1][:, 0, b:b + 1],
                                   scale=modT[1][:, 1, b:b + 1]).then_inc(hT3_ready, 1)

            act.wait_ge(var_ready, 4)
            act.activation(std[:], var[:], ACT.Sqrt, bias=eps_ln[:, 0:1]).then_inc(std_ready, 1)
            act.wait_ge(once("sx_loaded"), 16 * NS4)
            for s_ in range(NS4):
                ins = act.activation(squares[:, 0, s_], sx[:, s_, D:2 * D], ACT.Square, accum_out=ss[:, s_:s_ + 1])
            ins.then_inc(once("ss_ready"), 1)
            act.wait_ge(once("ms_ready"), 1)
            act.activation(sroot[:], ss[:], ACT.Sqrt).then_inc(once("sroot_ready"), 1)
            act.wait_ge(once("ang_ready"), 1)
            act.activation(sc_[:], ang[:], ACT.Sin).then_inc(once("sin_ready"), 1)
            act.wait_ge(once("hnT_ps"), 1)
            act.activation(hnT[:], bank[0][:], ACT.Copy).then_inc(once("hnT_ready"), 1)
            for s_ in range(NS4):
                act.wait_ge(once("qkv_ps"), s_ + 1)
                act.activation(vv[:, s_], bank[1 + s_][:, 2 * D:3 * D], ACT.Copy)
                act.activation(qk[:, s_], bank[1 + s_][:, 0:2 * D], ACT.Copy).then_inc(once("qk_ready"), 1)
            act.wait_ge(once("qT_ps"), 1)
            act.activation(qT[:], bank[5][:], ACT.Copy)
            act.activation(kT[:], bank[6][:], ACT.Copy).then_inc(once("qkT_ready"), 1)
            for i in range(NS4):
                b = i // NSEL
                act.wait_ge(once("maskT_ps"), i + 1)
                if i:
                    act.wait_ge(once("msel_ps"), i)
                act.activation(maskT[:].rearrange("p k q -> p (k q)"), bank[1][:], ACT.Copy).then_inc(once("maskT_ready"), 1)
                act.wait_ge(once("smax_ready"), i + 1)
                for h in range(AH):
                    ins = act.activation(sc[:, h, :], sc[:, h, :], ACT.Exp, bias=smax[:, h:h + 1], accum_out=ssum[:, h:h + 1])
                ins.then_inc(once("exp_ready"), 1)
                for k in range(AH * NSEL // 4):
                    m = i * 8 + k
                    act.wait_ge(once("pT_ps"), m + 1)
                    act.activation(pT[:, 4 * k:4 * k + 4, :].rearrange("p k q -> p (k q)"), bank[2 + k % 2][:], ACT.Copy).then_inc(once("pT_ready"), 1)
            act.wait_ge(once("onT_ps"), 1)
            act.activation(onT[:], bank[0][:], ACT.Copy).then_inc(once("onT_ready"), 1)
            act.wait_ge(once("x1_ready"), 1)
            for s_ in range(NS4):
                ins = act.activation(squares[:, 1, s_], x1[:, s_], ACT.Square, accum_out=ss[:, s_:s_ + 1])
            ins.then_inc(once("ss_ready"), 1)
            act.wait_ge(once("ms_ready"), 2)
            act.activation(sroot[:], ss[:], ACT.Sqrt).then_inc(once("sroot_ready"), 1)
            act.wait_ge(once("hnT_ps"), 2)
            act.activation(hnT[:], bank[0][:], ACT.Copy).then_inc(once("hnT_ready"), 1)
            for k in range(FF // P):
                act.wait_ge(once("hid_ps"), k + 1)
                act.activation(hid1[:, k], bank[1 + k][:], ACT.Gelu_apprx_tanh).then_inc(once("gelu_ready"), 1)

        def ln_finish(dve, ch):
            me, mo = stats[:, :, 1], stats[:, :, 4]
            ve, vo = stats[:, :, 2], stats[:, :, 5]
            dve.tensor_tensor(mean[:], me, mo, ALU.add)
            dve.tensor_tensor(tmp_ln[:], me, mo, ALU.subtract)
            ch.link(dve.tensor_tensor(var[:], ve, vo, ALU.add))
            dve.tensor_scalar(mean[:], mean[:], 0.5, None, ALU.mult)
            dve.tensor_scalar(var[:], var[:], 1.0 / D, None, ALU.mult)
            ch.link(dve.scalar_tensor_tensor(out=tmp_ln[:], in0=tmp_ln[:], scalar=0.25, in1=tmp_ln[:],
                                             op0=ALU.mult, op1=ALU.mult))
            dve.tensor_tensor(var[:], var[:], tmp_ln[:], ALU.add).then_inc(var_ready, 1)

        def ln_rstd(dve, ch, n):
            dve.wait_ge(std_ready, n)
            ch.link(dve.reciprocal(rstd[:], std[:]))
            ch.link(dve.tensor_tensor(tmp_ln[:], rstd[:], rstd[:], ALU.mult))
            ch.link(dve.scalar_tensor_tensor(out=tmp_ln[:], in0=var[:], scalar=eps_ln[:, 0:1], in1=tmp_ln[:], op0=ALU.add, op1=ALU.mult))
            ch.link(dve.tensor_scalar(tmp_ln[:], tmp_ln[:], -0.5, 1.5, ALU.mult, ALU.add))
            ch.link(dve.tensor_tensor(rstd[:], rstd[:], tmp_ln[:], ALU.mult))

        def normalise(dve, g, b):
            for q in range(GT):
                i = g * GT + (b * NT + q)
                ins = dve.tensor_scalar(xhat[:, b, q, :], at(xs, b, g * GT + q), mean[:, bass.ds(i, 1)],
                                        rstd[:, bass.ds(i, 1)], ALU.subtract, ALU.mult)
            return ins

        def gate_(dve, ch, m, t0, t1):
            dve.tensor_scalar(t0, m, 0.0, 2.0, ALU.is_ge, ALU.mult)
            ch.link(dve.scalar_tensor_tensor(out=t1, in0=m, scalar=-1.0, in1=m, op0=ALU.mult, op1=ALU.max))
            ch.link(dve.tensor_scalar(t1, t1, 0.25, None, ALU.max))
            ch.link(dve.scalar_tensor_tensor(out=m, in0=t0, scalar=-1.0, in1=t1, op0=ALU.add, op1=ALU.mult))

        def rank_in(ch, dve, k, in_tile):
            for b in range(B):
                ins = dve.tensor_tensor_scan(incl[:, 0, b], scan_ones[:], tot[:, k, b], 0.0, ALU.mult, ALU.add)
            ch.link(ins)
            ch.link(dve.tensor_tensor(incl[:, 1], incl[:, 0], tot[:, k], ALU.subtract))
            ch.link(dve.tensor_tensor(pos[:].rearrange("p b c -> p (b c)"), incl[:, 1].rearrange("p b c -> p (b c)"), in_tile, ALU.add))

        def hidden(dve, m, slot):
            dve.wait_ge(silu_done, now(m))
            dve.wait_ge(up_ps, now(m))
            dve.wait_ge(down_ps, back2(m))
            for k in range(2):
                ins = dve.tensor_tensor(hid[:, slot, k, :], sg[:, k, :], bank[4 + k][:], ALU.mult)
            ins.then_inc(hid_ready, 1)

        @block.vector
        def _(dve):
            credit(dve, "dve")
            ch = Chain(dve, dve_self)
            dve.wait_ge(c_exp, 2)
            dve.wait_ge(mod_loaded, 64)
            for l in range(2):
                ch.link(dve.tensor_scalar(cE[l][:], cE[l][:], 1.0, None, ALU.add))
                ch.link(dve.reciprocal(cE[l][:], cE[l][:]))
                ch.link(dve.tensor_tensor(cS[l][:], cT[l][:], cE[l][:], ALU.mult))
            dve.wait_ge(consts_ready, 1)
            for l in range(2):
                for b in range(B):
                    ins = dve.tensor_scalar(crep[l][:, b, :], ones[:], cS[l][:, b:b + 1], None, ALU.mult)
            ins.then_inc(c_silu, 1)
            for half in range(2):
                dve.wait_ge(x_loaded[half], 32)
                with dve.Fori(half * NT // 2, (half + 1) * NT // 2) as c:
                    for b in range(B):
                        dve.bn_stats(flat(stats[:, bass.ds(c + b * NT, 1), :]), at(xs, b, c))
            ch.link(dve.tensor_copy(tmp_ln[:, 0:1], ones[:, 0:1]))
            ln_finish(dve, ch)
            dve.wait_ge(mod_ps, 1)
            for l in range(2):
                m = modT[l]
                ch.link(dve.tensor_copy(m[:], bank[4 + l][:, 0:12].rearrange("p (j b) -> p j b", b=B)))
                for j in (1, 4):
                    dve.tensor_scalar(m[:, j, :], m[:, j, :], 1.0, None, ALU.add)
                for j in (2, 5):
                    gate_(dve, ch, m[:, j, :], tmp_ln[:, 0:B], tmp_ln[:, B:2 * B])
            dve.sem_inc(mod_ready, 1)
            dve.wait_ge(ga_ps, 1)
            dve.wait_ge(w_loaded, W_ALL)
            for l in range(2):
                ch.link(dve.tensor_copy(gabc[l][:], bank[6][:, l * B * P:(l + 1) * B * P].rearrange("p (b d) -> p b d", b=B)))
                gate_(dve, ch, gabc[l][:], gt0[:], gt1[:])
            for b in range(B):
                dve.tensor_tensor(woutg[:, b], wout[:], gabc[0][:, b:b + 1, :].to_broadcast([P, 4, D]), ALU.mult)
            dve.tensor_copy(wbdt[:, 0:NS], win[:, 0:NS])
            dve.tensor_copy(wbdt[:, NS:], win[:, 2 * NS:2 * NS + H]).then_inc(ga_done, 1)
            ln_rstd(dve, ch, 1)
            with dve.Fori(0, NG) as g:
                for b in range(B):
                    dve.wait_ge(trans_ps, back2(2 * g + b))
                    normalise(dve, g, b).then_inc(xhat_ready, 1)
                for b in range(B):
                    dve.wait_ge(bc_ps, now(2 * g + b))
                    for k in range(2):
                        ins = dve.tensor_copy(bcT[b * NS:(b + 1) * NS, bass.ds(g * GT, GT), k, :],
                                              bank[4 + k][b * NS:(b + 1) * NS, :].rearrange("p (q t) -> p q t", q=GT))
                    ins.then_inc(bc_kept, 1)
                    dve.wait_ge(tok_ps, now(2 * g + b))
                    tok = bank[6][:, 0:GT * (NS + H)].rearrange("p (q n) -> p q n", q=GT)
                    dve.tensor_copy(pk[:, b, bass.ds(g * GT, GT), PK_B:PK_B + NS], tok[:, :, 0:NS])
                    dve.tensor_copy(dts[:, b, bass.ds(g * GT, GT), :], tok[:, :, NS:]).then_inc(tok_kept, 1)
            def rep(ap):
                return ap.unsqueeze(1).to_broadcast([P, B * NT, H])

            def by8(ap):
                return ap.rearrange("p (i h) -> p i h", h=H)

            fl = "p b c h -> p (b c h)"
            dve.wait_ge(tok_kept, now(2 * NG - 1))
            ch.link(dve.tensor_tensor(by8(v_[:]), by8(dts[:].rearrange(fl)), rep(dtb[:]), ALU.add))
            dve.scalar_tensor_tensor(out=r_[:], in0=v_[:], scalar=-1.0, in1=v_[:], op0=ALU.mult, op1=ALU.max).then_inc(v_abs, 1)
            dve.wait_ge(e_exp, 1)
            dve.tensor_scalar(u_[:], e_[:], 1.0, None, ALU.add).then_inc(u_ready, 1)
            dve.wait_ge(u_ready, 1)
            dve.reciprocal(r_[:], u_[:])
            ch.link(dve.scalar_tensor_tensor(out=e_[:], in0=u_[:], scalar=-1.0, in1=e_[:], op0=ALU.add, op1=ALU.subtract))
            ch.link(dve.tensor_tensor(e_[:], e_[:], r_[:], ALU.mult))
            ch.link(dve.scalar_tensor_tensor(out=v_[:], in0=v_[:], scalar=0.0, in1=e_[:], op0=ALU.max, op1=ALU.subtract))
            dve.wait_ge(ln_ready, 1)
            ch.link(dve.tensor_tensor(delta[:].rearrange(fl), v_[:], l_[:], ALU.add))
            dve.scalar_tensor_tensor(out=by8(a_dec[:].rearrange(fl)), in0=by8(delta[:].rearrange(fl)), scalar=-1.0,
                                     in1=rep(expa[:]), op0=ALU.mult, op1=ALU.mult).then_inc(a_ready, 1)
            dve.wait_ge(decays_ready, 1)
            dve.tensor_tensor(dw[:].rearrange(fl), delta[:].rearrange(fl), e_rest[:].rearrange(fl), ALU.mult).then_inc(dw_ready, 1)
            dve.wait_ge(dw_ready, 1)
            for (c, links) in ch.loop(NT, 1):
                for b in range(B):
                    n = 2 * c + b
                    dve.wait_ge(g_ps, now(n))
                    dve.tensor_tensor(Gm[:, b], bank[6][:, 0:P], upper[:], ALU.mult).then_inc(gm_done, 1)
                    dve.wait_ge(xsb_done, now(n))
                    dve.tensor_tensor(heads(dX[:, b]), heads(Xsb[:, b]), per_head(at(delta, b, c)), ALU.mult)
                    dve.tensor_tensor(heads(dXw[:, b]), heads(Xsb[:, b]), per_head(at(dw, b, c)), ALU.mult).then_inc(dx_done, 1)
                    dve.wait_ge(off_ps, now(n))
                    dve.tensor_tensor(heads(yoff[:, b]), heads(bank[3][:]), per_head(at(e_cum, b, c)), ALU.mult).then_inc(yoff_done, 1)
                    dve.wait_ge(gm_done, now(n))
                    dve.wait_ge(expA_done, now(n))
                    dve.wait_ge(expB_done, now(n))
                    dve.tensor_tensor(M[:, b], Gm[:, b:b + 1, :].to_broadcast([P, H, P]), E[:, b], ALU.mult).then_inc(m_ready, 1)
                for b in range(B):
                    n = 2 * c + b
                    dve.wait_ge(diag_ps, now(n))
                    dve.wait_ge(ysum_ready, now(n))
                    dve.tensor_tensor(y2[:, b], bank[6][:], ysum[:, b], ALU.add).then_inc(y2_done, 1)
                    dve.wait_ge(y2_done, now(n))
                    dve.wait_ge(zg_ps, now(n))
                    dve.tensor_tensor(yg[:, b], y2[:, b], bank[4 + b][:], ALU.mult).then_inc(yg_done, 1)
                dve.wait_ge(decays_ready, 1)
                dve.wait_ge(ds_ps, now(2 * c + 1))
                links(dve.tensor_tensor(heads(Sd[:]), heads(S[:]), per_head(flat(e_all[:, bass.ds(c, 1), :])), ALU.mult))
                dve.tensor_tensor(S[:], Sd[:], bank[2][:], ALU.add).then_inc(s_upd, 1)
                for b in range(B):
                    n = 2 * c + b
                    dve.wait_ge(out_ps, now(n))
                    dve.tensor_tensor(at(xs, b, c), at(xs, b, c), bank[7][:, 0:P], ALU.add).then_inc(xres_done, 1)
                    dve.wait_ge(xres_done, now(n))
                    dve.bn_stats(flat(stats[:, bass.ds(c + b * NT, 1), :]), at(xs, b, c))
            ch.link(dve.tensor_copy(tmp_ln[:, 0:1], ones[:, 0:1]))
            ln_finish(dve, ch)
            ln_rstd(dve, ch, 2)
            dve.wait_ge(moe_consts, 1)
            for (g, links) in ch.loop(NG, B * 5):
                for b in range(B):
                    n = 2 * g + b
                    dve.wait_ge(trans2_ps, back2(n))
                    normalise(dve, g, b).then_inc(xhat2_ready, 1)
                    dve.wait_ge(router_ps, now(n))
                    links(dve.tensor_copy(logits[:], bank[6][:, 0:GT * EX].rearrange("p (q e) -> p q e", q=GT)))
                    links(dve.tensor_reduce(lmax[:], logits[:], AX.X, ALU.max))
                    links(dve.tensor_tensor(picked[:], logits[:], lmax[:].unsqueeze(2).to_broadcast([P, GT, EX]), ALU.is_equal))
                    links(dve.tensor_tensor(picked[:], picked[:], eighths[:].unsqueeze(1).to_broadcast([P, GT, EX]), ALU.mult))
                    links(dve.tensor_reduce(lmax[:], picked[:], AX.X, ALU.max))
                    dve.wait_ge(bcast_ps, n * EX + 2)
                    dve.tensor_tensor(onehot[:], picked[:], lmax[:].unsqueeze(2).to_broadcast([P, GT, EX]), ALU.is_equal).then_inc(onehot_ready, 1)
                    for e in range(NE):
                        if e < EX:
                            m = n * EX + e
                            dve.wait_ge(bcast_ps, now(m))
                            dve.wait_ge(up_ps, n * NE + e + 1)
                            dve.tensor_tensor(hTe[:, e % 2, :], hT[:, b, :], bank[7][:], ALU.mult).then_inc(hTe_ready, 1)
                        if e > 0:
                            hidden(dve, n * NE + e - 1, (e - 1) % 2)
                    hidden(dve, n * NE + NE - 1, (NE - 1) % 2)
                    dve.wait_ge(yT2_ps, now(n))
                    dve.tensor_tensor(xs[:, b, bass.ds(g * GT, GT), :], xs[:, b, bass.ds(g * GT, GT), :],
                                      bank[0][:].rearrange("p (q d) -> p q d", q=GT), ALU.add).then_inc(xres2_done, 1)
                    dve.wait_ge(xres2_done, now(n))
                    for q in range(GT):
                        dve.bn_stats(flat(stats[:, bass.ds(g * GT + (b * NT + q), 1), :]), at(xs, b, g * GT + q))
            dve.wait_ge(s4_exp1, 1)
            dve.tensor_tensor(s4_a[:], s4_ldt[:], s4_lam[:], ALU.mult).then_inc(s4_prod, 1)
            ch.link(dve.tensor_copy(tmp_ln[:, 0:1], ones[:, 0:1]))
            ln_finish(dve, ch)
            dve.wait_ge(s4_exp2, 1)
            for k in range(GT):
                dve.tensor_scalar(s4_abc[:, k * P:(k + 1) * P], ones[:], s4_a[:, 0:1], None, ALU.mult)
            for b in range(B):
                dve.tensor_tensor(s4_Cg[b * NS:(b + 1) * NS], s4_C[b * NS:(b + 1) * NS], gabc[1][b * NS:(b + 1) * NS, b, :], ALU.mult)
                ins = dve.tensor_scalar(s4_Dg[:, b], ident[:], s4_D[:, 0:1], modT[1][:, 2, b:b + 1], ALU.mult, ALU.mult)
            ch.link(ins)
            dve.sem_inc(s4_ready, 1)
            ln_rstd(dve, ch, 3)
            for (g, links) in ch.loop(NG, 1):
                for b in range(B):
                    dve.wait_ge(trans3_ps, back2(2 * g + b))
                    normalise(dve, g, b).then_inc(xhat3_ready, 1)
                dve.wait_ge(bu_ps, now(2 * g + 1))
                dve.wait_ge(s4out_ps, back1(2 * g))
                dve.tensor_tensor_scan(s4_x[:], s4_abc[:], bank[2][:], s4_carry[:, 0:1], ALU.mult, ALU.add).then_inc(scan_done, 1)
                dve.wait_ge(scan_done, now(g))
                links(dve.tensor_copy(s4_carry[:], s4_x[:, GW - 1:GW]))
                for b in range(B):
                    n = 2 * g + b
                    dve.wait_ge(s4out_ps, now(n))
                    dve.tensor_tensor(xs[:, b, bass.ds(g * GT, GT), :], xs[:, b, bass.ds(g * GT, GT), :],
                                      bank[4 + b][:].rearrange("p (q d) -> p q d", q=GT), ALU.add).then_inc(xres3_done, 1)
                    dve.wait_ge(xres3_done, now(n))
                    for q in range(GT):
                        dve.bn_stats(flat(stats[:, bass.ds(g * GT + (b * NT + q), 1), :]), at(xs, b, g * GT + q))

            dve.wait_ge(once("rows_ps"), 1)
            for b in range(B):
                dve.tensor_copy(rows[:, b], bank[6 + b][:, 0:3 * D].rearrange("p (j d) -> p j d", j=3))
            ch.link(dve.tensor_copy(tmp_ln[:, 0:1], ones[:, 0:1]))
            dve.tensor_scalar(rows[:, :, 1, :], rows[:, :, 1, :], 1.0, None, ALU.add)
            gate_(dve, ch, rows[:, :, 2, :], gt0[:], gt1[:])
            dve.sem_inc(once("rows_ready"), 1)
            ln_finish(dve, ch)
            ln_rstd(dve, ch, 4)
            dve.wait_ge(once("l1_loaded"), L1_ALL)
            for (g, links) in ch.loop(NG, B * 3):
                for b in range(B):
                    n = 2 * g + b
                    normalise(dve, g, b).then_inc(xhat4_ready, 1)
                    dve.wait_ge(xhat4_ready, now(n))
                    dve.wait_ge(hx_stored[b], 16 * (g + 1))
                    dve.wait_ge(dflt_ready, back2(n))
                    h_ = hx[:, b, :, D:2 * D]
                    links(dve.tensor_tensor(h_, xhat[:, b], rows[:, b, 1:2, :].to_broadcast([P, GT, D]), ALU.mult))
                    dve.tensor_tensor(h_, h_, rows[:, b, 0:1, :].to_broadcast([P, GT, D]), ALU.add).then_inc(h4_ready, 1)
                    dve.wait_ge(h4_ready, now(n))
                    links(dve.tensor_tensor(hprod[:], h_, rw_row[:].unsqueeze(1).to_broadcast([P, GT, D]), ALU.mult))
                    links(dve.tensor_reduce(wred[:], hprod[:], AX.X, ALU.add))
                    dve.tensor_scalar(w_all[:, b, bass.ds(g * GT, GT)], wred[:], rb_col[:, 0:1], None, ALU.add)
                    dve.tensor_scalar(hx[:, b, :, 2 * D], wred[:], rb_col[:, 0:1], None, ALU.add).then_inc(w4_ready, 1)
            dve.wait_ge(once("l1_consts"), 1)
            for k in range(NSTEP):
                ins = dve.tensor_scalar(J[:, k], jt[:], 28 - 4 * k, None, ALU.logical_shift_left)
            ch.link(ins)
            ch.link(dve.memset(pre[:], 0))

            def to_float_bits(out_, tmp, u):
                ch.link(dve.tensor_scalar(tmp, u, 31, -1, ALU.arith_shift_right, ALU.bitwise_xor))
                ch.link(dve.scalar_tensor_tensor(out=out_, in0=tmp, scalar=-2**31, in1=u, op0=ALU.bitwise_or, op1=ALU.bitwise_xor))

            for k in range(NSTEP):
                ch.link(dve.tensor_tensor(cand[:], pre[:].unsqueeze(2).to_broadcast([P, B, NJ]),
                                          J[:, k:k + 1, :].to_broadcast([P, B, NJ]), ALU.bitwise_or))
                to_float_bits(candf[:], candt[:], cand[:])
                ch.link(dve.tensor_tensor(cmp_[:], w_all[:].unsqueeze(2).to_broadcast([P, B, NJ, NT]),
                                          candf[:].bitcast(F32).unsqueeze(3).to_broadcast([P, B, NJ, NT]), ALU.is_ge))
                dve.tensor_reduce(cnt[:], cmp_[:], AX.X, ALU.add).then_inc(once("cnt_ready"), 1)
                dve.wait_ge(once("cnt_ps"), k + 1)
                ch.link(dve.tensor_scalar(ge256[:].rearrange("p b j -> p (b j)"), bank[0][:, 0:B * NJ], float(TOPK), None, ALU.is_ge))
                ch.link(dve.tensor_reduce(digitf[:], ge256[:], AX.X, ALU.add))
                ch.link(dve.tensor_copy(digit[:], digitf[:]))
                ch.link(dve.scalar_tensor_tensor(out=pre[:], in0=digit[:], scalar=28 - 4 * k, in1=pre[:],
                                                 op0=ALU.logical_shift_left, op1=ALU.bitwise_or))
            to_float_bits(thr[:], thr_t[:], pre[:])
            thrb = thr[:].bitcast(F32).unsqueeze(2).to_broadcast([P, B, NT])
            dve.tensor_tensor(gteq[:, 0], w_all[:], thrb, ALU.is_gt)
            dve.tensor_tensor(gteq[:, 1], w_all[:], thrb, ALU.is_equal).then_inc(once("gteq_ready"), 1)
            dve.wait_ge(once("gteq_ps"), 1)
            ch.link(dve.tensor_copy(tot[:, 0:2].rearrange("p k b c -> p (k b c)"), bank[0][:, 0:2 * B * NT]))
            rank_in(ch, dve, 1, bank[0][:, 2 * B * NT:3 * B * NT])
            ch.link(dve.tensor_reduce(ngt[:], tot[:, 0], AX.X, ALU.add))
            ch.link(dve.tensor_scalar(ngt[:], ngt[:], -1.0, float(SEL), ALU.mult, ALU.add))
            ch.link(dve.tensor_tensor(sel[:], pos[:], ngt[:].unsqueeze(2).to_broadcast([P, B, NT]), ALU.is_le))
            ch.link(dve.tensor_tensor(sel[:], sel[:], gteq[:, 1], ALU.mult))
            dve.tensor_tensor(sel[:], sel[:], gteq[:, 0], ALU.add).then_inc(once("sel_ready"), 1)
            dve.wait_ge(once("sel_ps"), 1)
            ch.link(dve.tensor_copy(tot[:, 1].rearrange("p b c -> p (b c)"), bank[0][:, 0:B * NT]))
            rank_in(ch, dve, 1, bank[0][:, B * NT:2 * B * NT])
            ch.link(dve.tensor_tensor(pos[:], pos[:], sel[:], ALU.mult))
            ch.link(dve.tensor_scalar(pos[:], pos[:], -1.0, None, ALU.add))
            for b in range(B):
                with dve.Fori(0, NT) as c:
                    dve.tensor_scalar(flat(choose[:, b, bass.ds(c, 1), :]), iota256[:], pos[:, b, bass.ds(c, 1)], None, ALU.is_equal)
            ch.link(dve.tensor_copy(tmp_ln[:, 0:1], ones[:, 0:1]))
            dve.sem_inc(once("choose_ready"), 1)
            dve.wait_ge(once("picks_ps"), 1)
            ch.link(dve.tensor_copy(picks[:].rearrange("p s j -> p (s j)"), bank[1][:, 0:2 * NS4]))
            ch.link(dve.scalar_tensor_tensor(out=idx[:], in0=picks[:, :, 0], scalar=float(P), in1=picks[:, :, 1], op0=ALU.mult, op1=ALU.add))
            ch.link(dve.tensor_scalar(cidx[:], idx[:], float(ML - 1), None, ALU.min))
            for b in range(B):
                c0, c1 = b * NSEL, (b + 1) * NSEL
                dve.tensor_scalar(gidx[:, 0, c0:c1], idx[:, c0:c1], float(b * T), None, ALU.add)
                ins = dve.tensor_scalar(gidx[:, 1, c0:c1], cidx[:, c0:c1], float(b * ML), None, ALU.add)
            ins.then_inc(once("gidx_ready"), 1)

            def rms(src, j):
                dve.wait_ge(once("ss_ready"), j + 1)
                ch.link(dve.tensor_scalar(ss[:], ss[:], 1.0 / D, RMS_EPS, ALU.mult, ALU.add))
                dve.sem_inc(once("ms_ready"), 1)
                dve.wait_ge(once("sroot_ready"), j + 1)
                ch.link(dve.reciprocal(srr[:], sroot[:]))
                ch.link(dve.tensor_tensor(st[:], srr[:], srr[:], ALU.mult))
                ch.link(dve.tensor_tensor(st[:], st[:], ss[:], ALU.mult))
                ch.link(dve.tensor_scalar(st[:], st[:], -0.5, 1.5, ALU.mult, ALU.add))
                ch.link(dve.tensor_tensor(srr[:], srr[:], st[:], ALU.mult))
                ch.link(dve.tensor_tensor(hn[:], src, srr[:].unsqueeze(2).to_broadcast([P, NS4, D]), ALU.mult))
                dve.tensor_tensor(hn[:], hn[:], ln_row[:, j:j + 1, :].to_broadcast([P, NS4, D]), ALU.mult).then_inc(once("hn_ready"), 1)

            dve.wait_ge(once("sx_loaded"), 16 * NS4)
            rms(sx[:, :, D:2 * D], 0)
            dve.wait_ge(once("spos_loaded"), 16 * NS4)
            ch.link(dve.tensor_copy(st[:], spos[:]))
            ch.link(dve.tensor_tensor(ang[:, 0], st[:].unsqueeze(2).to_broadcast([P, NS4, AD // 2]),
                                      inv[:].unsqueeze(1).to_broadcast([P, NS4, AD // 2]), ALU.mult))
            ch.link(dve.tensor_scalar(ang[:, 1], ang[:, 0], 0.0, None, ALU.add))
            two_pi = 2.0 * np.pi
            ch.link(dve.tensor_scalar(angk[:, 0], ang[:, 0], 1.0 / two_pi, None, ALU.mult))
            ch.link(dve.tensor_scalar(angk[:, 1], ang[:, 1], 1.0 / two_pi, 0.25, ALU.mult, ALU.add))
            ch.link(dve.tensor_copy(angi[:], angk[:]))
            ch.link(dve.tensor_copy(angk[:], angi[:]))
            part1 = 6.28125
            part2 = 1.9350051879882812e-3
            part3 = two_pi - part1 - part2
            for part in (part1, part2, part3):
                ch.link(dve.scalar_tensor_tensor(out=ang[:].rearrange("p t s i -> p (t s i)"), in0=angk[:].rearrange("p t s i -> p (t s i)"),
                                                 scalar=-part, in1=ang[:].rearrange("p t s i -> p (t s i)"), op0=ALU.mult, op1=ALU.add))
            ch.link(dve.tensor_scalar(ang[:, 1], ang[:, 1], float(np.pi / 2), None, ALU.add))
            dve.tensor_scalar(ang[:], ang[:], 3.1415925, -3.1415925, ALU.min, ALU.max).then_inc(once("ang_ready"), 1)
            dve.wait_ge(once("sin_ready"), 1)
            for s_ in range(NS4):
                dve.wait_ge(once("qk_ready"), s_ + 1)

                def halves(t):
                    return t.rearrange("p (h t i) -> p h t i", t=2, i=AD // 2)

                def angle(j):
                    return sc_[:, j, s_:s_ + 1, :].unsqueeze(1).to_broadcast([P, 2 * AH, 2, AD // 2])

                dve.tensor_tensor(halves(qks[:]), halves(qk[:, s_]), angle(0), ALU.mult)
                ch.link(dve.tensor_tensor(halves(qkc[:]), halves(qk[:, s_]), angle(1), ALU.mult))
                c_, n_, o_ = halves(qkc[:]), halves(qks[:]), halves(qk[:, s_])
                dve.tensor_tensor(o_[:, :, 0, :], c_[:, :, 0, :], n_[:, :, 1, :], ALU.subtract)
                ch.link(dve.tensor_tensor(o_[:, :, 1, :], c_[:, :, 1, :], n_[:, :, 0, :], ALU.add))
                dve.tensor_scalar(qk[:, s_, 0:D], qk[:, s_, 0:D], float(1.0 / np.sqrt(AD)), None, ALU.mult).then_inc(once("rope_ready"), 1)
            dve.wait_ge(once("qkT_ready"), 1)
            for i in range(NS4):
                b = i // NSEL
                if i % NSEL == 0:
                    for h in range(AH):
                        if i:
                            dve.wait_ge(once("score_ps"), 8 * i)
                        dve.tensor_scalar(kTm[:, h, :], kT[:, b * TOPK:(b + 1) * TOPK], headmask[:, h:h + 1], None, ALU.mult)
                    dve.wait_ge(once("cidx_ps"), b + 1)
                    for k in range(ML // P):
                        ins = dve.tensor_scalar(colsel[:, k, :], bank[7][:, 0:TOPK], iotap[:, k:k + 1], None, ALU.is_equal)
                    ins.then_inc(once("colsel_ready"), 1)
                dve.wait_ge(once("msel_ps"), i + 1)
                ch.link(dve.tensor_copy(msel[:], bank[4][:, 0:TOPK]))
                ch.link(dve.memset(msel[:, SEL:TOPK], -3.0e38))
                if i:
                    dve.wait_ge(once("pT_ps"), 8 * i)
                for k in range(AH // 2):
                    dve.wait_ge(once("score_ps"), 8 * i + k + 1)
                    dve.tensor_tensor(sc[:, 2 * k:2 * k + 2, :], bank[5 + k % 2][:].rearrange("p (h k) -> p h k", h=2),
                                      msel[:].unsqueeze(1).to_broadcast([P, 2, TOPK]), ALU.add).then_inc(once("masked_ready"), 1)
                dve.wait_ge(once("masked_ready"), 8 * i + 8)
                dve.tensor_reduce(smax[:], sc[:], AX.X, ALU.max, negate=True).then_inc(once("smax_ready"), 1)
                dve.wait_ge(once("exp_ready"), i + 1)
                ch.link(dve.reciprocal(sinv[:], ssum[:]))
                dve.wait_ge(once("o_ps"), i + 1)
                dve.tensor_tensor(on[:, i].rearrange("p (h d) -> p h d", h=AH), bank[0][:, 0:D].rearrange("p (h d) -> p h d", h=AH),
                                  sinv[:].unsqueeze(2).to_broadcast([P, AH, AD]), ALU.mult).then_inc(once("on_ready"), 1)
            dve.wait_ge(once("wo_ps"), 1)
            dve.tensor_tensor(x1[:], bank[1][:].rearrange("p (s d) -> p s d", s=NS4), sx[:, :, D:2 * D], ALU.add).then_inc(once("x1_ready"), 1)
            rms(x1[:], 1)
            dve.wait_ge(once("w2_ps"), 1)
            ch.link(dve.tensor_tensor(x2[:], bank[5][:].rearrange("p (s d) -> p s d", s=NS4), x1[:], ALU.add))
            ch.link(dve.tensor_tensor(x2[:], x2[:], sx[:, :, 2 * D:].to_broadcast([P, NS4, D]), ALU.mult))
            for b in range(B):
                c0, c1 = b * NSEL, (b + 1) * NSEL
                ins = dve.tensor_scalar(notsel[:, c0:c1], sx[:, c0:c1, 2 * D], thr[:, b:b + 1].bitcast(F32), None, ALU.is_le)
            ch.link(ins)
            ch.link(dve.tensor_tensor(res[:], sx[:, :, D:2 * D], notsel[:].unsqueeze(2).to_broadcast([P, NS4, D]), ALU.mult))
            ch.link(dve.tensor_tensor(x2[:], x2[:], res[:], ALU.add))
            for b in range(B):
                c0, c1 = b * NSEL, (b + 1) * NSEL
                ins = dve.tensor_tensor(x2[:, c0:c1], x2[:, c0:c1], rows[:, b, 2:3, :].to_broadcast([P, NSEL, D]), ALU.mult)
            ch.link(ins)
            dve.tensor_tensor(res[:], x2[:], sx[:, :, 0:D], ALU.add).then_inc(once("res_ready"), 1)

        def transposes(pe, g, b):
            n = 2 * g + b
            pe.wait_ge(xhat_ready, now(n))
            pe.wait_ge(hT_ready, back2(n))
            for q in range(GT):
                ins = pe.transpose(bank[b][:, q * P:(q + 1) * P], xhat[:, b, q, :], ident[:])
            ins.then_inc(trans_ps, 1)

        def expert_down(pe, n, e):
            pe.wait_ge(hid_ready, now(n * NE + e))
            if e == 0:
                pe.wait_ge(yT2_kept, back1(n))
            for k in range(2):
                ins = pe.matmul(bank[1][:], wdown[:, e, k, :], hid[:, e % 2, k, :], start=e == 0 and k == 0, stop=e == NE - 1 and k == 1)
            ins.then_inc(down_ps, 1)

        @block.tensor
        def _(pe):
            credit(pe, "pe")
            pe.wait_ge(c_silu, 1)
            pe.wait_ge(mod_loaded, 64)
            pe.wait_ge(consts_ready, 1)
            for l in range(2):
                for j in range(6):
                    ins = pe.matmul(bank[4 + l][:, 2 * j:2 * j + 2], wmod[l][:, j * D:(j + 1) * D], cS[l][:], start=True, stop=True)
            ins.then_inc(mod_ps, 1)
            for l in range(2):
                for b in range(B):
                    i = l * B + b
                    ins = pe.matmul(bank[6][:, i * P:(i + 1) * P], crep[l][:, b, :], wmod[l][:, 2 * D:3 * D], start=True, stop=True)
            ins.then_inc(ga_ps, 1)
            pe.wait_ge(w_loaded, W_ALL)
            pe.wait_ge(ga_done, 1)
            with pe.Fori(0, NG) as g:
                for b in range(B):
                    transposes(pe, g, b)
                for b in range(B):
                    n = 2 * g + b
                    pe.wait_ge(hT_ready, now(n))
                    pe.wait_ge(z_kept, back1(n))
                    for k in range(2):
                        ins = pe.matmul(bank[2 + k][:], wz[:, k * P:(k + 1) * P], hT[:, b, :], start=True, stop=True)
                    ins.then_inc(z_ps, 1)
                    pe.wait_ge(bc_kept, back1(n))
                    for k in range(2):
                        ins = pe.matmul(bank[4 + k][b * NS:(b + 1) * NS, :], win[:, k * NS:(k + 1) * NS], hT[:, b, :], start=True, stop=True)
                    ins.then_inc(bc_ps, 1)
                    pe.wait_ge(tok_kept, back1(n))
                    for q in range(GT):
                        ins = pe.matmul(bank[6][:, q * (NS + H):(q + 1) * (NS + H)], hT[:, b, q * P:(q + 1) * P], wbdt[:], start=True, stop=True)
                    ins.then_inc(tok_ps, 1)
            pe.wait_ge(a_ready, 1)
            pe.wait_ge(z_kept, now(2 * NG - 1))
            af = a_dec[:].rearrange("p b c h -> p (b c h)")
            for i, mask in enumerate((upper, lower, ones)):
                ins = pe.matmul(bank[i][:, 0:TH], mask[:], af, start=True, stop=True)
            ins.then_inc(cum_ps, 1)
            pe.wait_ge(decays_ready, 1)
            pe.wait_ge(bc_kept, now(2 * NG - 1))
            pe.wait_ge(tok_kept, now(2 * NG - 1))
            with pe.Fori(0, NT) as c:
                for b in range(B):
                    n = 2 * c + b
                    lo, hi = b * NS, (b + 1) * NS
                    pe.wait_ge(pk_loaded[b], 32 * (c + 1))
                    pe.wait_ge(gm_done, back1(n))
                    if b == 0:
                        pe.wait_ge(y2_done, back1(n))
                    pe.matmul(bank[6][:, 0:P], bc_slot[lo:hi, 0, :], bc_slot[lo:hi, 1, :], start=True, stop=True).then_inc(g_ps, 1)
                    pe.wait_ge(segrhs_ready, now(n))
                    pe.wait_ge(expA_done, back1(n))
                    pe.matmul(bank[0][:], lower[:], seg_rhs[:, b, 0:4, :].rearrange("p h t -> p (h t)"), start=True, stop=True).then_inc(segA_ps, 1)
                    pe.wait_ge(expB_done, back1(n))
                    pe.matmul(bank[1][:], lower[:], seg_rhs[:, b, 4:8, :].rearrange("p h t -> p (h t)"), start=True, stop=True).then_inc(segB_ps, 1)
                    pe.wait_ge(xsb_done, back1(n))
                    pe.wait_ge(s_upd, back1(c))
                    pe.matmul(bank[2][:], pk_slot[:, b, PK_H:PK_H + P], win[:, 2 * NS + H:], start=True, stop=True).then_inc(x_ps, 1)
                    pe.wait_ge(yoff_done, back1(n))
                    pe.wait_ge(yg_done, back2(n))
                    for k in range(2):
                        ins = pe.matmul(bank[4 + b][:], pk_slot[:, b, PK_S + k * P:PK_S + (k + 1) * P], wzg[:, k, :], start=k == 0, stop=k == 1)
                    ins.then_inc(zg_ps, 1)
                    if b == 0:
                        pe.wait_ge(ygT_done, back1(n))
                    pe.matmul(bank[3][:], bc_slot[lo:hi, 1, :], S[lo:hi, :], start=True, stop=True).then_inc(off_ps, 1)
                for b in range(B):
                    n = 2 * c + b
                    pe.wait_ge(m_ready, now(n))
                    if b == 0:
                        pe.wait_ge(gm_done, now(n + 1))
                    else:
                        pe.wait_ge(y2_done, back1(n))
                    for h in range(H):
                        ins = pe.matmul(bank[6][:, h * HD:(h + 1) * HD], M[:, b, h, :], dX[:, b, h * HD:(h + 1) * HD], start=True, stop=True)
                    ins.then_inc(diag_ps, 1)
                    pe.wait_ge(xsb_done, now(2 * c + 1))
                    pe.wait_ge(dx_done, now(n))
                    pe.matmul(bank[2][b * NS:(b + 1) * NS, :], pk_slot[:, b, PK_B:PK_B + NS], dXw[:, b], start=True, stop=True).then_inc(ds_ps, 1)
                for b in range(B):
                    n = 2 * c + b
                    pe.wait_ge(yg_done, now(n))
                    pe.wait_ge(ygT_done, back1(n))
                    for k in range(4):
                        ins = pe.transpose(bank[3][:, k * P:(k + 1) * P], yg[:, b, k * P:(k + 1) * P], ident[:])
                    ins.then_inc(yT_ps, 1)
                for b in range(B):
                    n = 2 * c + b
                    pe.wait_ge(ygT_done, now(n))
                    pe.wait_ge(xres_done, back1(n))
                    for k in range(4):
                        ins = pe.matmul(bank[7][:, 0:P], ygT[:, b, k, :], woutg[:, b, k, :], start=k == 0, stop=k == 3)
                    ins.then_inc(out_ps, 1)

            pe.wait_ge(moe_loaded, MOE_ALL)
            pe.wait_ge(moe_consts, 1)
            pe.wait_ge(xres_done, now(2 * NT - 1))
            with pe.Fori(0, NG) as g:
                for b in range(B):
                    n = 2 * g + b
                    pe.wait_ge(xhat2_ready, now(n))
                    pe.wait_ge(xres2_done, back1(n))
                    for q in range(GT):
                        ins = pe.transpose(bank[0][:, q * P:(q + 1) * P], xhat[:, b, q, :], ident[:])
                    ins.then_inc(trans2_ps, 1)
                    pe.wait_ge(hT2_ready, now(n))
                    for q in range(GT):
                        ins = pe.matmul(bank[6][:, q * EX:(q + 1) * EX], hT[:, b, q * P:(q + 1) * P], wrouter[:], start=True, stop=True)
                    ins.then_inc(router_ps, 1)
                    pe.wait_ge(onehot_ready, now(n))
                    for e in range(NE):
                        m = n * NE + e
                        if e < EX:
                            pe.wait_ge(hTe_ready, n * EX + e + 2)
                            for q in range(GT):
                                ins = pe.matmul(bank[7][:, q * P:(q + 1) * P], onehot[:, q, e:e + 1].to_broadcast([P, P]), ident16[:], start=True, stop=True)
                            ins.then_inc(bcast_ps, 1)
                            pe.wait_ge(hTe_ready, now(n * EX + e))
                        rhs = hTe[:, e % 2, :] if e < EX else hT[:, b, :]
                        pe.wait_ge(silu_done, back1(m))
                        for k in range(2):
                            ins = pe.matmul(bank[2 + k][:], wgate[:, e, k * P:(k + 1) * P], rhs, start=True, stop=True)
                        ins.then_inc(gate_ps, 1)
                        pe.wait_ge(hid_ready, back1(m))
                        for k in range(2):
                            ins = pe.matmul(bank[4 + k][:], wup[:, e, k * P:(k + 1) * P], rhs, start=True, stop=True)
                        ins.then_inc(up_ps, 1)
                        if e > 0:
                            expert_down(pe, n, e - 1)
                    expert_down(pe, n, NE - 1)
                    pe.wait_ge(yT2_kept, now(n))
                    for q in range(GT):
                        ins = pe.transpose(bank[0][:, q * P:(q + 1) * P], yT[:, b, q * P:(q + 1) * P], ident[:])
                    ins.then_inc(yT2_ps, 1)
            pe.wait_ge(s4_ready, 1)
            pe.wait_ge(s4_loaded, S4_ALL)
            pe.wait_ge(xres2_done, now(2 * NG - 1))
            pe.wait_ge(yT2_kept, now(2 * NG - 1))
            with pe.Fori(0, NG) as g:
                for b in range(B):
                    n = 2 * g + b
                    pe.wait_ge(xhat3_ready, now(n))
                    pe.wait_ge(hT3_ready, back2(n))
                    for q in range(GT):
                        ins = pe.transpose(bank[b][:, q * P:(q + 1) * P], xhat[:, b, q, :], ident[:])
                    ins.then_inc(trans3_ps, 1)
                pe.wait_ge(scan_done, back1(g))
                for b in range(B):
                    n = 2 * g + b
                    pe.wait_ge(hT3_ready, now(n))
                    pe.matmul(bank[2][b * NS:(b + 1) * NS, :], s4_B[:], hT[:, b, :], start=True, stop=True).then_inc(bu_ps, 1)
                for b in range(B):
                    n = 2 * g + b
                    lo, hi = b * NS, (b + 1) * NS
                    pe.wait_ge(scan_done, now(g))
                    pe.wait_ge(xres3_done, back2(n))
                    for q in range(GT):
                        o = bank[4 + b][:, q * P:(q + 1) * P]
                        pe.matmul(o, hT[:, b, q * P:(q + 1) * P], s4_Dg[:, b], start=True, stop=False)
                        ins = pe.matmul(o, s4_x[lo:hi, q * P:(q + 1) * P], s4_Cg[lo:hi], start=False, stop=True)
                    ins.then_inc(s4out_ps, 1)
            for b in range(B):
                ins = pe.matmul(bank[6 + b][:, 0:3 * D], crep[1][:, b, :], wmod[1][:, 3 * D:6 * D], start=True, stop=True)
            ins.then_inc(once("rows_ps"), 1)
            pe.wait_ge(xres3_done, now(2 * NG - 1))
            pe.wait_ge(hT3_ready, now(2 * NG - 1))
            for k in range(NSTEP):
                pe.wait_ge(once("cnt_ready"), k + 1)
                pe.matmul(bank[0][:, 0:B * NJ], ones[:], cnt[:].rearrange("p b j -> p (b j)"), start=True, stop=True).then_inc(once("cnt_ps"), 1)
            pe.wait_ge(once("gteq_ready"), 1)
            w_ = 2 * B * NT
            pe.matmul(bank[0][:, 0:w_], ones[:], gteq[:].rearrange("p k b c -> p (k b c)"), start=True, stop=True)
            pe.matmul(bank[0][:, w_:w_ + B * NT], upper[:], gteq[:, 1].rearrange("p b c -> p (b c)"), start=True, stop=True).then_inc(once("gteq_ps"), 1)
            pe.wait_ge(once("sel_ready"), 1)
            sf = sel[:].rearrange("p b c -> p (b c)")
            pe.matmul(bank[0][:, 0:B * NT], ones[:], sf, start=True, stop=True)
            pe.matmul(bank[0][:, B * NT:2 * B * NT], upper[:], sf, start=True, stop=True).then_inc(once("sel_ps"), 1)
            pe.wait_ge(once("choose_ready"), 1)
            for s_ in range(NS4):
                b, k = s_ // NSEL, s_ % NSEL
                for c in range(NT):
                    ins = pe.matmul(bank[1][:, 2 * s_:2 * s_ + 2], choose[:, b, c, k * P:(k + 1) * P], tokid[:, c, :], start=c == 0, stop=c == NT - 1)
            ins.then_inc(once("picks_ps"), 1)
            pe.wait_ge(once("hn_ready"), 1)
            for s_ in range(NS4):
                ins = pe.transpose(bank[0][:, s_ * P:(s_ + 1) * P], hn[:, s_], ident[:])
            ins.then_inc(once("hnT_ps"), 1)
            pe.wait_ge(once("hnT_ready"), 1)
            pe.wait_ge(once("l1_loaded"), L1_ALL)
            for s_ in range(NS4):
                pe.matmul(bank[1 + s_][:, 0:3 * D], hnT[:, s_ * P:(s_ + 1) * P], wqkv[:], start=True, stop=True).then_inc(once("qkv_ps"), 1)
            pe.wait_ge(once("rope_ready"), NS4)
            for j in range(2):
                for s_ in range(NS4):
                    ins = pe.transpose(bank[5 + j][:, s_ * P:(s_ + 1) * P], qk[:, s_, j * D:(j + 1) * D], ident[:])
            ins.then_inc(once("qT_ps"), 1)
            pe.wait_ge(once("qkT_ready"), 1)
            pe.wait_ge(once("smask_loaded"), 16 * NS4)
            for i in range(NS4):
                b, qh = i // NSEL, i % NSEL
                if qh == 0:
                    if i:
                        pe.wait_ge(once("colsel_ready"), b)
                    for k in range(NSEL):
                        ins = pe.matmul(bank[7][:, k * P:(k + 1) * P], cidx[:, b * NSEL + k:b * NSEL + k + 1].to_broadcast([P, P]), ident[:], start=True, stop=True)
                    ins.then_inc(once("cidx_ps"), 1)
                if i:
                    pe.wait_ge(once("maskT_ready"), i)
                for k in range(ML // P):
                    ins = pe.transpose(bank[1][:, k * P:(k + 1) * P], smask[:, i, k * P:(k + 1) * P], ident[:])
                ins.then_inc(once("maskT_ps"), 1)
                pe.wait_ge(once("maskT_ready"), i + 1)
                pe.wait_ge(once("colsel_ready"), b + 1)
                for k in range(ML // P):
                    ins = pe.matmul(bank[4][:, 0:TOPK], maskT[:, k, :], colsel[:, k, :], start=k == 0, stop=k == ML // P - 1)
                ins.then_inc(once("msel_ps"), 1)
                for k in range(AH // 2):
                    m = 8 * i + k
                    if m >= 2:
                        pe.wait_ge(once("masked_ready"), m - 1)
                    pe.matmul(bank[5 + k % 2][:], qT[:, i * P:(i + 1) * P], kTm[:, 2 * k:2 * k + 2, :].rearrange("p h k -> p (h k)"),
                              start=True, stop=True).then_inc(once("score_ps"), 1)
                pe.wait_ge(once("exp_ready"), i + 1)
                for k in range(AH * NSEL // 4):
                    m = 8 * i + k
                    if m >= 2:
                        pe.wait_ge(once("pT_ready"), m - 1)
                    for j in range(4):
                        h, kh = (4 * k + j) // NSEL, (4 * k + j) % NSEL
                        ins = pe.transpose(bank[2 + k % 2][:, j * P:(j + 1) * P], sc[:, h, kh * P:(kh + 1) * P], ident[:])
                    ins.then_inc(once("pT_ps"), 1)
                if i:
                    pe.wait_ge(once("on_ready"), i)
                for h in range(AH):
                    pe.wait_ge(once("pT_ready"), 8 * i + h // 2 + 1)
                    for kh in range(NSEL):
                        ins = pe.matmul(bank[0][:, h * AD:(h + 1) * AD], pT[:, h * NSEL + kh, :], vv[:, b * NSEL + kh, h * AD:(h + 1) * AD],
                                        start=kh == 0, stop=kh == NSEL - 1)
                ins.then_inc(once("o_ps"), 1)
            pe.wait_ge(once("on_ready"), NS4)
            for s_ in range(NS4):
                ins = pe.transpose(bank[0][:, s_ * P:(s_ + 1) * P], on[:, s_], ident[:])
            ins.then_inc(once("onT_ps"), 1)
            pe.wait_ge(once("onT_ready"), 1)
            for s_ in range(NS4):
                ins = pe.matmul(bank[1][:, s_ * D:(s_ + 1) * D], onT[:, s_ * P:(s_ + 1) * P], wo[:], start=True, stop=True)
            ins.then_inc(once("wo_ps"), 1)
            pe.wait_ge(once("hn_ready"), 2)
            for s_ in range(NS4):
                ins = pe.transpose(bank[0][:, s_ * P:(s_ + 1) * P], hn[:, s_], ident[:])
            ins.then_inc(once("hnT_ps"), 1)
            pe.wait_ge(once("hnT_ready"), 2)
            for k in range(FF // P):
                pe.matmul(bank[1 + k][:], w1[:, k * P:(k + 1) * P], hnT[:], start=True, stop=True).then_inc(once("hid_ps"), 1)
            pe.wait_ge(once("gelu_ready"), FF // P)
            for s_ in range(NS4):
                for k in range(FF // P):
                    ins = pe.matmul(bank[5][:, s_ * D:(s_ + 1) * D], hid1[:, k, s_ * P:(s_ + 1) * P], w2[:, k, :], start=k == 0, stop=k == FF // P - 1)
            ins.then_inc(once("w2_ps"), 1)


_INS = ["L0_attn_x", "L0_attn_Wz", "L0_attn_Win", "L0_attn_Wzg", "L0_attn_Wout", "L0_attn_dt_bias", "L0_attn_A_log",
        "L0_attn_D_param", "L0_wmod", "L1_wmod", "L1_attn_Lambda", "L1_attn_log_dt", "L1_attn_D",
        "L1_ffn_attention_mask", "L1_ffn_position_ids", "L1_ffn_router_w", "L1_ffn_router_b", "L1_ffn_wq", "L1_ffn_wk",
        "L1_ffn_wv", "L1_ffn_wo", "L1_ffn_w1", "L1_ffn_w2", "L1_ffn_ln1", "L1_ffn_ln2"]
_TRANSPOSED = {"L0_cT": "L0_c", "L1_cT": "L1_c", "upT": "L0_ffn_up", "gateT": "L0_ffn_gate", "downT": "L0_ffn_down",
               "routerT": "L0_ffn_router", "up_sT": "L0_ffn_w_up_s", "gate_sT": "L0_ffn_w_gate_s",
               "down_sT": "L0_ffn_w_down_s", "s4_BT": "L1_attn_B", "s4_CT": "L1_attn_C"}


def kernel(**inputs):
    import concourse.bacc as bacc
    from concourse.bass_utils import run_bass_kernel_spmd

    nc = bacc.Bacc("TRN2", target_bir_lowering=False, num_devices=1)
    arrays = {n: np.ascontiguousarray(inputs[n]) for n in _INS}
    for n, src in _TRANSPOSED.items():
        arrays[n] = np.ascontiguousarray(np.swapaxes(np.asarray(inputs[src]), -1, -2))
    io = {n: nc.dram_tensor(f"in_{n}", a.shape, mybir.dt.from_np(a.dtype), kind="ExternalInput").ap() for n, a in arrays.items()}
    out = nc.dram_tensor("out_0", (B, T, D), F32, kind="ExternalOutput").ap()
    build(nc, io, out)
    r = run_bass_kernel_spmd(nc, [{f"in_{n}": a for n, a in arrays.items()}], core_ids=[0])
    return r.results[0]["out_0"]
```

```python
from contextlib import ExitStack

import numpy as np

import concourse.bass as bass
from concourse import mybir
from concourse.alu_op_type import AluOpType as ALU

ACT = mybir.ActivationFunctionType
AX = mybir.AxisListType
F32 = mybir.dt.float32
BF16 = mybir.dt.bfloat16
I32 = mybir.dt.int32
U32 = mybir.dt.uint32

P = 128
B = 2
T = 2048
D = 128
NT = T // P
GT = 4
NG = NT // GT
GW = GT * P
H = 8
HD = 64
NS = 64
DI = H * HD
ZW = 2 * D
EX = 8
HID = 256
NSORT = (B * T + EX * (P - 1)) // P
SLOTS = 3
LN_EPS = 1e-5
RMS_EPS = 1e-6
AH = 16
AD = D // AH
FF = 512
ML = 512
TOPK = T // 8
SEL = TOPK - 1
NSEL = TOPK // P
ROPE_BASE = 10000.0


class Chain:

    def __init__(self, eng, sem):
        self.eng, self.sem, self.base, self.k = eng, sem, 0, 0

    def link(self, ins):
        self.k += 1
        ins.then_inc(self.sem, 1)
        self.eng.wait_ge(self.sem, self.base + self.k)

    def loop(self, count, per):
        outer = self.base + self.k
        with self.eng.Fori(0, count) as i:
            self.base, self.k = i * per + outer, 0
            yield i, self.link
            assert self.k == per, f"{self.k} links in a loop of {per}"
        self.base, self.k = outer + count * per, 0


def build(nc, io, out, dbg=None):
    ctx = ExitStack()
    with ctx:
        def sb(name, shape, dt=F32):
            return ctx.enter_context(nc.sbuf_tensor(name, shape, dt))

        def sem(name):
            return ctx.enter_context(nc.semaphore(name))

        bank = [ctx.enter_context(nc.psum_tensor(f"bank{i}", [P, 512], F32)) for i in range(8)]

        xs = sb("xs", [P, B, NT, D])
        stats = sb("stats", [P, B * NT, 6])
        mean = sb("mean", [P, B * NT])
        var = sb("var", [P, B * NT])
        std = sb("std", [P, B * NT])
        rstd = sb("rstd", [P, B * NT])
        tmp_ln = sb("tmp_ln", [P, B * NT])
        xhat = sb("xhat", [P, B, GT, D])
        hT = sb("hT", [P, B, GW])

        ident = sb("ident", [P, P])
        upper = sb("upper", [P, P])
        lower = sb("lower", [P, P])
        ones = sb("ones", [P, P])
        eps_ln = sb("eps_ln", [P, 1])

        cT = [sb(f"cT{l}", [P, B]) for l in range(2)]
        cE = [sb(f"cE{l}", [P, B]) for l in range(2)]
        cS = [sb(f"cS{l}", [P, B]) for l in range(2)]
        wmod = [sb(f"wmod{l}", [P, 6 * D]) for l in range(2)]
        modT = [sb(f"modT{l}", [P, 6, B]) for l in range(2)]

        gabc = [sb(f"gabc{l}", [P, B, D]) for l in range(2)]
        crep = [sb(f"crep{l}", [P, B, P]) for l in range(2)]
        gt0 = sb("gt0", [P, B, D])
        gt1 = sb("gt1", [P, B, D])

        wrouter = sb("wrouter", [P, EX])
        keep, ssd_mem = sb, ctx.enter_context(ExitStack())

        def sb(name, shape, dt=F32):
            return ssd_mem.enter_context(nc.sbuf_tensor(name, shape, dt))

        wz = sb("wz", [P, ZW])
        win = sb("win", [P, 2 * NS + H + DI])
        wbdt = sb("wbdt", [P, NS + H])
        wzg = sb("wzg", [P, 2, DI])
        wout = sb("wout", [P, 4, D])
        woutg = sb("woutg", [P, B, 4, D])
        dtb = sb("dtb", [P, H])
        alog = sb("alog", [P, H])
        expa = sb("expa", [P, H])
        dpar = sb("dpar", [P, H])

        PK_H, PK_S, PK_B = 0, P, P + 2 * P
        PKW = P + 2 * P + NS
        pk = sb("pk", [P, B, NT, PKW])
        bcT = sb("bcT", [P, NT, 2, P])
        pk_slot = sb("pk_slot", [P, B, PKW])
        bc_slot = sb("bc_slot", [P, 2, P])

        TH = B * NT * H
        dts = sb("dts", [P, B, NT, H])
        v_ = sb("v_", [P, TH])
        e_ = sb("e_", [P, TH])
        u_ = sb("u_", [P, TH])
        l_ = sb("l_", [P, TH])
        r_ = sb("r_", [P, TH])
        delta = sb("delta", [P, B, NT, H])
        a_dec = sb("a_dec", [P, B, NT, H])
        e_cum = sb("e_cum", [P, B, NT, H])
        e_rest = sb("e_rest", [P, B, NT, H])
        dw = sb("dw", [P, B, NT, H])
        e_all = sb("e_all", [P, NT, H])

        seg_rhs = sb("seg_rhs", [P, B, H, P])
        E = sb("E", [P, B, H, P])
        M = sb("M", [P, B, H, P])
        Gm = sb("Gm", [P, B, P])
        dX = sb("dX", [P, B, DI])
        dXw = sb("dXw", [P, B, DI])
        Xsb = sb("Xsb", [P, B, DI])
        XD = sb("XD", [P, B, DI])
        yoff = sb("yoff", [P, B, DI])
        ysum = sb("ysum", [P, B, DI])
        y2 = sb("y2", [P, B, DI])
        yg = sb("yg", [P, B, DI])
        ygT = sb("ygT", [P, B, 4, P])
        S = sb("S", [P, DI])
        Sd = sb("Sd", [P, DI])

        ssd_mem.close()
        sb = keep

        s4_B = sb("s4_B", [P, NS])
        s4_C = sb("s4_C", [P, D])
        s4_Cg = sb("s4_Cg", [P, D])
        s4_lam = sb("s4_lam", [P, 1])
        s4_ldt = sb("s4_ldt", [P, 1])
        s4_D = sb("s4_D", [P, 1])
        s4_a = sb("s4_a", [P, 1])
        s4_abc = sb("s4_abc", [P, GW])
        s4_Dg = sb("s4_Dg", [P, B, D])
        s4_x = sb("s4_x", [P, GW])
        s4_carry = sb("s4_carry", [P, 1])

        NJ = 15
        NSTEP = 8
        NS4 = B * NSEL
        rows = sb("rows", [P, B, 3, D])
        w_all = sb("w_all", [P, B, NT])
        rw_row = sb("rw_row", [P, D])
        rb_col = sb("rb_col", [P, 1])
        ln_row = sb("ln_row", [P, 2, D])
        wqkv = sb("wqkv", [P, 3 * D])
        wo = sb("wo", [P, D])
        w1 = sb("w1", [P, FF])
        w2 = sb("w2", [P, FF // P, D])
        jt = sb("jt", [P, NJ], I32)
        scan_ones = sb("scan_ones", [P, NT])
        iota256 = sb("iota256", [P, TOPK])
        tokid = sb("tokid", [P, NT, 2], BF16)
        inv = sb("inv", [P, AD // 2])
        eps_rms = sb("eps_rms", [P, 1])
        headmask = sb("headmask", [P, AH])
        iotap = sb("iotap", [P, ML // P])

        moe_mem = ctx.enter_context(ExitStack())

        def sb(name, shape, dt=F32):
            return moe_mem.enter_context(nc.sbuf_tensor(name, shape, dt))

        ROW = D + 1
        wgu = sb("wgu", [P, EX, 2 * HID])
        wdown = sb("wdown", [P, EX, HID // P, D])
        wgu_s = sb("wgu_s", [P, 2 * HID])
        wdown_s = sb("wdown_s", [P, HID // P, D])
        wdown_g = sb("wdown_g", [P, B, HID // P, D])
        rows0 = sb("rows0", [P, B, 3, D])
        h_all = sb("h_all", [P, B, NT, ROW])
        hT_all = sb("hT_all", [P, B, T])
        logits = sb("logits", [P, B * NT, EX])
        eighths = sb("eighths", [P, EX])
        lmax = sb("lmax", [P, B * NT])
        onehot = sb("onehot", [P, B * NT, EX])
        tile_tot = sb("tile_tot", [P, EX, B * NT])
        keep_cum = sb("keep_cum", [P, EX, B * NT])
        tile_cum = sb("tile_cum", [P, EX, B * NT])
        need_i = sb("need_i", [P, EX], I32)
        need = sb("need", [P, EX])
        ends = sb("ends", [P, EX])
        starts = sb("starts", [P, EX])
        place = sb("place", [P, B * NT, EX])
        place_f = sb("place_f", [P, B * NT])
        place_i = sb("place_i", [P, B * NT], I32)
        tile_no = sb("tile_no", [P, NSORT])
        past = sb("past", [P, NSORT, EX])
        expert_f = sb("expert_f", [P, NSORT])
        expert_i = sb("expert_i", [P, NSORT], I32)
        fill = sb("fill", [P, NSORT, ROW])
        spare = sb("spare", [P, SLOTS], I32)
        sg = sb("sg", [P, B, HID // P, GW])
        hid = sb("hid", [P, B, HID // P, GW])
        hs = sb("hs", [P, SLOTS, ROW])
        token_no = sb("token_no", [P, SLOTS], I32)
        hsT = sb("hsT", [P, SLOTS, P])
        sgs = sb("sgs", [P, SLOTS, HID])
        hids = sb("hids", [P, SLOTS, HID])
        hidsT = sb("hidsT", [P, SLOTS, HID])
        ys = sb("ys", [P, SLOTS, D])
        yx = sb("yx", [P, B, NT, D])

        moe_mem.close()
        sb = keep
        hx = sb("hx", [P, B, GT, 2 * D + 1])
        dflt = sb("dflt", [P, B, GT, D])
        hprod = sb("hprod", [P, GT, D])
        wred = sb("wred", [P, GT])
        J = sb("J", [P, NSTEP, NJ], I32)
        pre = sb("pre", [P, B], I32)
        digit = sb("digit", [P, B], I32)
        digitf = sb("digitf", [P, B])
        cand = sb("cand", [P, B, NJ], I32)
        candt = sb("candt", [P, B, NJ], I32)
        candf = sb("candf", [P, B, NJ], I32)
        cmp_ = sb("cmp_", [P, B, NJ, NT])
        cnt = sb("cnt", [P, B, NJ])
        ge256 = sb("ge256", [P, B, NJ])
        thr_t = sb("thr_t", [P, B], I32)
        thr = sb("thr", [P, B], I32)
        gteq = sb("gteq", [P, 2, B, NT])
        tot = sb("tot", [P, 3, B, NT])
        incl = sb("incl", [P, 2, B, NT])
        ngt = sb("ngt", [P, B])
        sel = sb("sel", [P, B, NT])
        pos = sb("pos", [P, B, NT])
        choose = sb("choose", [P, B, NT, TOPK], BF16)
        picks = sb("picks", [P, NS4, 2])
        idx = sb("idx", [P, NS4])
        cidx = sb("cidx", [P, NS4])
        gidx = sb("gidx", [P, 2, NS4], I32)
        sx = sb("sx", [P, NS4, 2 * D + 1])
        smask = sb("smask", [P, NS4, ML])
        spos = sb("spos", [P, NS4], I32)
        ang = sb("ang", [P, 2, NS4, AD // 2])
        angk = sb("angk", [P, 2, NS4, AD // 2])
        angi = sb("angi", [P, 2, NS4, AD // 2], I32)
        sc_ = sb("sc_", [P, 2, NS4, AD // 2])
        ss = sb("ss", [P, NS4])
        sroot = sb("sroot", [P, NS4])
        srr = sb("srr", [P, NS4])
        st = sb("st", [P, NS4])
        squares = sb("squares", [P, NS4, D])
        hn = sb("hn", [P, NS4, D])
        hnT = sb("hnT", [P, NS4 * P])
        qk = sb("qk", [P, NS4, 2 * D])
        qks = sb("qks", [P, 2 * D])
        qkc = sb("qkc", [P, 2 * D])
        vv = sb("vv", [P, NS4, D])
        qT = sb("qT", [P, NS4 * P])
        kT = sb("kT", [P, NS4 * P])
        kTm = sb("kTm", [P, B, AH, TOPK])
        colsel = sb("colsel", [P, B, ML // P, TOPK])
        maskT = sb("maskT", [P, 2, ML // P, P])
        msel = sb("msel", [P, NS4, TOPK])
        SC_SLOTS = 4
        sc = sb("sc", [P, SC_SLOTS, 2, TOPK])
        smax = sb("smax", [P, NS4, AH])
        ssum = sb("ssum", [P, NS4, AH])
        sinv = sb("sinv", [P, 2, AH])
        pT = sb("pT", [P, SC_SLOTS, 2 * NSEL, P])
        on = sb("on", [P, NS4, D])
        onT = sb("onT", [P, NS4 * P])
        x1 = sb("x1", [P, NS4, D])
        hid1 = sb("hid1", [P, FF // P, NS4 * P])
        x2 = sb("x2", [P, NS4, D])
        notsel = sb("notsel", [P, NS4])
        res = sb("res", [P, NS4, D])

        assert NSORT % SLOTS == 0
        hs_dram = nc.dram_tensor("sorted_scratch", ((NSORT + SLOTS) * P, ROW), F32, kind="Internal").ap()
        ys_dram = nc.dram_tensor("expert_scratch", (B * T + (NSORT + SLOTS) * P, D), F32, kind="Internal").ap()
        hx_dram = nc.dram_tensor("hx_scratch", (B * T, 2 * D + 1), F32, kind="Internal").ap()

        def now(n):
            return n + 4

        def back1(n):
            return n + 3

        def back2(n):
            return n + 2

        def back3(n):
            return n + 1

        own = {}

        def handoff(engine, *names):
            got = [sem(x) for x in names]
            own.setdefault(engine, []).extend(got)
            return got

        def credit(eng, engine):
            for s_ in own.get(engine, []):
                eng.sem_inc(s_, 3)

        dve_self = sem("dve_self")
        act_self = sem("act_self")
        pool_self = sem("pool_self")
        pool_awake = sem("pool_awake")
        mod_loaded = sem("mod_loaded")
        x_loaded = [sem(f"x_loaded{i}") for i in range(2)]
        w_loaded = sem("w_loaded")
        consts_ready = sem("consts_ready")
        c_exp = sem("c_exp")
        c_silu = sem("c_silu")
        mod_ps = sem("mod_ps")
        mod_ready = sem("mod_ready")
        ga_ps = sem("ga_ps")
        ga_done = sem("ga_done")
        var_ready = sem("var_ready")
        std_ready = sem("std_ready")
        (xhat_ready, bc_kept, tok_kept) = handoff("dve", "xhat_ready", "bc_kept", "tok_kept")
        (trans_ps, z_ps, bc_ps, tok_ps) = handoff("pe", "trans_ps", "z_ps", "bc_ps", "tok_ps")
        (hT_ready, z_kept) = handoff("act", "hT_ready", "z_kept")
        (hT_kept,) = handoff("pool", "hT_kept")
        v_abs = sem("v_abs")
        e_exp = sem("e_exp")
        u_ready = sem("u_ready")
        ln_ready = sem("ln_ready")
        a_ready = sem("a_ready")
        cum_ps = sem("cum_ps")
        decays_ready = sem("decays_ready")
        dw_ready = sem("dw_ready")
        pk_loaded = [sem(f"pk_loaded{b}") for b in range(B)]
        (g_ps, segA_ps, segB_ps, x_ps, zg_ps, off_ps, diag_ps, ds_ps, yT_ps, out_ps) = handoff(
            "pe", "g_ps", "segA_ps", "segB_ps", "x_ps", "zg_ps", "off_ps", "diag_ps", "ds_ps", "yT_ps", "out_ps")
        (gm_done, dx_done, yoff_done, m_ready, y2_done, yg_done, s_upd, xres_done) = handoff(
            "dve", "gm_done", "dx_done", "yoff_done", "m_ready", "y2_done", "yg_done", "s_upd", "xres_done")
        (expA_done, expB_done, xsb_done, ygT_done) = handoff("act", "expA_done", "expB_done", "xsb_done", "ygT_done")
        (segrhs_ready, ysum_ready) = handoff("pool", "segrhs_ready", "ysum_ready")
        moe_loaded = sem("moe_loaded")
        s4_loaded = sem("s4_loaded")
        moe_consts = sem("moe_consts")
        (xhat2_ready, logits_kept, hid_ready, xres2_done, hids_ready, yx_added) = handoff(
            "dve", "xhat2_ready", "logits_kept", "hid_ready", "xres2_done", "hids_ready", "yx_added")
        (trans2_ps, router_ps, gate_ps, up_ps, down_ps, hsT_ps, gu_ps, hidsT_ps, ys_ps) = handoff(
            "pe", "trans2_ps", "router_ps", "gate_ps", "up_ps", "down_ps", "hsT_ps", "gu_ps", "hidsT_ps", "ys_ps")
        (hT2_ready, silu_done, hsT_ready, silus_done, hidsT_ready, ys_ready) = handoff(
            "act", "hT2_ready", "silu_done", "hsT_ready", "silus_done", "hidsT_ready", "ys_ready")
        (h2_ready, numbers_kept, yg_ready) = handoff("pool", "h2_ready", "numbers_kept", "yg_ready")
        hs_loaded = [sem(f"hs_loaded{i}") for i in range(SLOTS)]
        yx_loaded = [sem(f"yx_loaded{b}") for b in range(2)]
        ys_stored = [sem(f"ys_stored{i}") for i in range(SLOTS)]
        s4_exp1 = sem("s4_exp1")
        s4_prod = sem("s4_prod")
        s4_exp2 = sem("s4_exp2")
        s4_ready = sem("s4_ready")
        (xhat3_ready, scan_done, xres3_done) = handoff("dve", "xhat3_ready", "scan_done", "xres3_done")
        (trans3_ps, bu_ps, s4out_ps) = handoff("pe", "trans3_ps", "bu_ps", "s4out_ps")
        (hT3_ready,) = handoff("act", "hT3_ready")

        (xhat4_ready, h4_ready, w4_ready) = handoff("dve", "xhat4_ready", "h4_ready", "w4_ready")
        (hxx_ready, dflt_ready) = handoff("pool", "hxx_ready", "dflt_ready")
        hx_stored = [sem(f"hx_stored{b}") for b in range(B)]
        dflt_stored = [sem(f"dflt_stored{b}") for b in range(B)]
        single = {}

        def once(name):
            if name not in single:
                single[name] = sem(name)
            return single[name]

        PAIRS = AH // 2
        NM = NS4 * PAIRS
        LAG_T, LAG_V, LAG_O = 2, 3, 4

        def attention(*steps):
            return [name for m in range(NM + LAG_O) for name, lag in steps if 0 <= m - lag < NM]

        def attention_dve():
            names = []
            for m in range(NM + LAG_O):
                names += (["masked_ready", "smax_ready"] if m < NM else []) + (["on_ready"] if m >= LAG_O and (m - LAG_O) % PAIRS == PAIRS - 1 else [])
            return names

        STEPS = {
            "pe": ["rows0_ps", "ranks_ps", "rows_ps"] + NSTEP * ["cnt_ps"] + ["gteq_ps", "sel_ps", "picks_ps"] + B * ["cidx_ps"]
                  + ["hnT_ps"] + NS4 * ["qkv_ps"] + ["maskT_ps"] + (NS4 - 1) * ["maskT_ps", "msel_ps"] + ["msel_ps", "qT_ps"]
                  + attention(("score_ps", 0), ("pT_ps", LAG_T), ("pv_ps", LAG_V))
                  + ["onT_ps", "wo_ps", "hnT_ps"] + FF // P * ["hid_ps"] + ["w2_ps"],
            "dve": ["rows0_ready", "onehot_ready", "place_ready", "expert_ready", "rows_ready"] + NSTEP * ["cnt_ready"]
                   + ["gteq_ready", "sel_ready", "choose_ready", "gidx_ready"] + B * ["colsel_ready"] + ["ms_ready", "hn_ready", "ang_ready"] + NS4 * ["rope_ready"]
                   + ["msel_ready"] + attention_dve() + ["x1_ready", "ms_ready", "hn_ready", "res_ready"],
            "act": ["ss_ready", "sroot_ready", "hnT_ready", "sin_ready"] + NS4 * ["qk_ready"] + NS4 * ["maskT_ready"] + ["qkT_ready"]
                   + attention(("exp_ready", 0), ("pT_ready", LAG_T))
                   + ["onT_ready", "ss_ready", "sroot_ready", "hnT_ready"] + FF // P * ["gelu_ready"],
            "pool": ["l1_consts"],
        }
        kTm_ready = sem("kTm_ready")
        step_sem = {e: sem(f"{e}_step") for e in STEPS}
        taken = {e: 0 for e in STEPS}

        def did(name):
            e = next(e for e in STEPS if name in STEPS[e])
            assert STEPS[e][taken[e]] == name, f"{e} takes {name}, not {STEPS[e][taken[e]]}"
            taken[e] += 1
            return step_sem[e]

        def upto(name, nth):
            e = next(e for e in STEPS if name in STEPS[e])
            at_ = [i for i, x in enumerate(STEPS[e]) if x == name]
            return step_sem[e], at_[nth - 1] + 1

        block = ctx.enter_context(nc.Block())

        x_t = io["L0_attn_x"].rearrange("b (c p) d -> p b c d", p=P)
        out_t = out.rearrange("b (c p) d -> p b c d", p=P)
        W_ALL = 16 * 8
        MOE_ALL = 16 * 9
        S4_ALL = 16 * 7
        L1_ALL = 16 * 10

        def flat(ap):
            return ap.rearrange("p a d -> p (a d)")

        def at(t, b, c):
            return flat(t[:, b, bass.ds(c, 1), :])

        def per_head(ap):
            return ap.unsqueeze(2).to_broadcast([P, H, HD])

        def heads(ap):
            return ap.rearrange("p (h d) -> p h d", h=H)

        @block.sync
        def _(sp):
            for l in range(2):
                sp.dma_start(cT[l][:], io[f"L{l}_cT"]).then_inc(mod_loaded, 16)
                sp.dma_start(wmod[l][:], io[f"L{l}_wmod"]).then_inc(mod_loaded, 16)
            for half in range(2):
                c0 = half * NT // 2
                for b in range(B):
                    sp.dma_start(xs[:, b, c0:c0 + NT // 2, :], x_t[:, b, c0:c0 + NT // 2, :]).then_inc(x_loaded[half], 16)
            sp.dma_start(wz[:], io["L0_attn_Wz"]).then_inc(w_loaded, 16)
            sp.dma_start(win[:], io["L0_attn_Win"]).then_inc(w_loaded, 16)
            sp.dma_start(wzg[:], io["L0_attn_Wzg"].rearrange("(k p) n -> p k n", p=P)).then_inc(w_loaded, 16)
            sp.dma_start(wout[:], io["L0_attn_Wout"].rearrange("(k p) n -> p k n", p=P)).then_inc(w_loaded, 16)
            sp.dma_start(wrouter[:], io["routerT"]).then_inc(w_loaded, 16)
            sp.dma_start(dtb[:], io["L0_attn_dt_bias"].partition_broadcast(P)).then_inc(w_loaded, 16)
            sp.dma_start(alog[:], io["L0_attn_A_log"].partition_broadcast(P)).then_inc(w_loaded, 16)
            sp.dma_start(dpar[:], io["L0_attn_D_param"].partition_broadcast(P)).then_inc(w_loaded, 16)

            sp.wait_ge(hT_kept, now(2 * NG - 1))
            sp.wait_ge(z_kept, now(2 * NG - 1))
            sp.wait_ge(tok_kept, now(2 * NG - 1))
            sp.wait_ge(bc_kept, now(2 * NG - 1))
            with sp.Fori(0, NT) as c:
                for b in range(B):
                    sp.wait_ge(ds_ps, back2(2 * c + b))
                    sp.dma_start(pk_slot[:, b, :], at(pk, b, c)).then_inc(pk_loaded[b], 16)
                    sp.dma_start(bc_slot[b * NS:(b + 1) * NS], bcT[b * NS:(b + 1) * NS, bass.ds(c, 1), :, :].rearrange("p a k t -> p (a k) t")).then_inc(pk_loaded[b], 16)
            sp.wait_ge(out_ps, now(2 * NT - 1))
            sp.wait_ge(xres_done, now(2 * NT - 1))
            for j, src in enumerate(("gate", "up")):
                sp.dma_start(wgu_s[:, j * HID:(j + 1) * HID], io[f"{src}_sT"]).then_inc(moe_loaded, 16)
            sp.dma_start(wdown_s[:], io["down_sT"].rearrange("(k p) c -> p k c", p=P)).then_inc(moe_loaded, 16)
            for j, src in enumerate(("gate", "up")):
                for half in range(2):
                    e0, e1 = half * EX // 2, (half + 1) * EX // 2
                    sp.dma_start(wgu[:, e0:e1, j * HID:(j + 1) * HID], io[f"{src}T"][e0:e1].rearrange("e c h -> c e h")).then_inc(moe_loaded, 16)
            for half in range(2):
                e0, e1 = half * EX // 2, (half + 1) * EX // 2
                sp.dma_start(wdown[:, e0:e1], io["downT"][e0:e1].rearrange("e (k p) c -> p e k c", p=P)).then_inc(moe_loaded, 16)
            sp.wait_ge(moe_consts, 1)
            sp.dma_start(hs_dram[0:NSORT * P].rearrange("(j p) d -> p j d", p=P), fill[:]).then_inc(once("filled"), 16)
            sp.dma_start(hs_dram[NSORT * P:].rearrange("(j p) d -> p j d", p=P), fill[:, 0:SLOTS]).then_inc(once("filled"), 16)
            sp.dma_start(s4_B[:], io["s4_BT"]).then_inc(s4_loaded, 16)
            for b in range(B):
                sp.dma_start(s4_C[b * NS:(b + 1) * NS], io["s4_CT"]).then_inc(s4_loaded, 16)
                sp.dma_start(s4_lam[b * NS:(b + 1) * NS], io["L1_attn_Lambda"].unsqueeze(1)).then_inc(s4_loaded, 16)
            sp.dma_start(s4_ldt[:], io["L1_attn_log_dt"].partition_broadcast(P)).then_inc(s4_loaded, 16)
            sp.dma_start(s4_D[:], io["L1_attn_D"].unsqueeze(1)).then_inc(s4_loaded, 16)
            for j, name in enumerate(("wq", "wk", "wv")):
                sp.dma_start(wqkv[:, j * D:(j + 1) * D], io[f"L1_ffn_{name}"]).then_inc(once("l1_loaded"), 16)
            sp.dma_start(wo[:], io["L1_ffn_wo"]).then_inc(once("l1_loaded"), 16)
            sp.dma_start(w1[:], io["L1_ffn_w1"]).then_inc(once("l1_loaded"), 16)
            sp.dma_start(w2[:], io["L1_ffn_w2"].rearrange("(k p) d -> p k d", p=P)).then_inc(once("l1_loaded"), 16)
            for j in range(2):
                sp.dma_start(ln_row[:, j], io[f"L1_ffn_ln{j + 1}"].partition_broadcast(P)).then_inc(once("l1_loaded"), 16)
            sp.dma_start(rw_row[:], io["L1_ffn_router_w"].rearrange("d a -> (d a)").partition_broadcast(P)).then_inc(once("l1_loaded"), 16)
            sp.dma_start(rb_col[:], io["L1_ffn_router_b"].partition_broadcast(P)).then_inc(once("l1_loaded"), 16)
            sp.wait_ge(once("rows_sorted"), 16 * B * NT)
            with sp.Fori(0, NSORT // SLOTS + 1) as i:
                for s_ in range(SLOTS):
                    n = SLOTS * i + s_
                    sp.wait_ge(hsT_ps, back3(n))
                    sp.wait_ge(numbers_kept, back3(n))
                    sp.dma_start(hs[:, s_, :], hs_dram.rearrange("(j p) d -> p j d", p=P)[:, bass.ds(n, 1), :].rearrange("p a d -> p (a d)")).then_inc(hs_loaded[s_], 16)
            for s_ in range(SLOTS):
                sp.wait_ge(ys_stored[s_], 16 * (NSORT // SLOTS + 1))
            ys_t = ys_dram[0:B * T].rearrange("(b c p) d -> p b c d", p=P, b=B)
            for half in range(2):
                c0, c1 = half * NT // 2, (half + 1) * NT // 2
                for b in range(B):
                    sp.dma_start(yx[:, b, c0:c1, :], ys_t[:, b, c0:c1, :]).then_inc(yx_loaded[half], 16)
            hx_t = hx_dram.rearrange("(b c p) d -> p b c d", p=P, b=B)
            for b in range(B):
                sp.sem_inc(hx_stored[b], 16)
                sp.sem_inc(dflt_stored[b], 16)
            with sp.Fori(0, NG) as g:
                for b in range(B):
                    n = 2 * g + b
                    sp.wait_ge(w4_ready, now(n))
                    sp.wait_ge(hxx_ready, now(n))
                    sp.dma_start(hx_t[:, b, bass.ds(g * GT, GT), :], hx[:, b]).then_inc(hx_stored[b], 16)
                    sp.wait_ge(dflt_ready, now(n))
                    sp.dma_start(out_t[:, b, bass.ds(g * GT, GT), :], dflt[:, b]).then_inc(dflt_stored[b], 16)
            for b in range(B):
                sp.wait_ge(dflt_stored[b], 16 * (NG + 1))
            sp.wait_ge(once("rows_scattered"), 16 * NS4)

        @block.gpsimd
        def _(pool):
            credit(pool, "pool")
            ch = Chain(pool, pool_self)
            pool.memset(eps_ln[:], LN_EPS)
            pool.memset(ident[:], 0.0)
            pool.memset(upper[:], 1.0)
            ch.link(pool.memset(lower[:], 1.0))
            pool.affine_select(out=ident[:], in_=ident[:], compare_op=ALU.not_equal, fill=1.0, base=0,
                               pattern=[[-1, P]], channel_multiplier=1)
            pool.affine_select(out=upper[:], in_=upper[:], compare_op=ALU.is_ge, fill=0.0, base=0,
                               pattern=[[1, P]], channel_multiplier=-1)
            pool.affine_select(out=lower[:], in_=lower[:], compare_op=ALU.is_gt, fill=0.0, base=0,
                               pattern=[[-1, P]], channel_multiplier=1)
            pool.memset(S[:], 0.0)
            pool.memset(ones[:], 1.0).then_inc(consts_ready, 1)
            with pool.Fori(0, NG) as g:
                for b in range(B):
                    pool.wait_ge(hT_ready, now(2 * g + b))
                    pool.tensor_copy(pk[:, b, bass.ds(g * GT, GT), PK_H:PK_H + P],
                                     hT[:, b, :].rearrange("p (q t) -> p q t", q=GT)).then_inc(hT_kept, 1)
            pool.wait_ge(a_ready, 1)
            for (c, links) in ch.loop(NT, B):
                for b in range(B):
                    n = 2 * c + b
                    pool.wait_ge(segA_ps, back2(n))
                    pool.wait_ge(segB_ps, back2(n))
                    pool.tensor_tensor(seg_rhs[:, b], upper[:].unsqueeze(1).to_broadcast([P, H, P]),
                                       at(a_dec, b, c).unsqueeze(2).to_broadcast([P, H, P]), ALU.mult).then_inc(segrhs_ready, 1)
                for b in range(B):
                    n = 2 * c + b
                    pool.wait_ge(xsb_done, now(n))
                    links(pool.tensor_tensor(heads(XD[:, b]), heads(Xsb[:, b]), per_head(dpar[:]), ALU.mult))
                    pool.wait_ge(yoff_done, now(n))
                    pool.wait_ge(y2_done, back2(n))
                    pool.tensor_tensor(ysum[:, b], yoff[:, b], XD[:, b], ALU.add).then_inc(ysum_ready, 1)
            pool.wait_ge(out_ps, now(2 * NT - 1))
            pool.wait_ge(xres_done, now(2 * NT - 1))
            pool.iota(eighths[:], pattern=[[-1, EX]], base=EX, channel_multiplier=0, allow_small_or_imprecise_dtypes=True)
            pool.iota(tile_no[:], pattern=[[1, NSORT]], base=0, channel_multiplier=0, allow_small_or_imprecise_dtypes=True)
            ch.link(pool.memset(keep_cum[:], 1.0))
            pool.memset(keep_cum[:, :, 0], 0.0)
            pool.iota(h_all[:, :, :, D].bitcast(I32), pattern=[[T, B], [P, NT]], base=0, channel_multiplier=1)
            pool.iota(spare[:], pattern=[[P, SLOTS]], base=B * T + NSORT * P, channel_multiplier=1)
            ch.link(pool.memset(fill[:], 0.0))
            pool.iota(fill[:, :, D].bitcast(I32), pattern=[[P, NSORT]], base=B * T, channel_multiplier=1)
            pool.memset(s4_carry[:], 0.0).then_inc(moe_consts, 1)
            pool.wait_ge(*upto("rows0_ready", 1))
            for (g, links) in ch.loop(NG, B):
                for b in range(B):
                    h_ = h_all[:, b, bass.ds(g * GT, GT), 0:D]
                    pool.wait_ge(xhat2_ready, now(2 * g + b))
                    pool.sem_inc(pool_awake, 1)
                    links(pool.tensor_tensor(h_, xhat[:, b], rows0[:, b, 1:2, :].to_broadcast([P, GT, D]), ALU.mult))
                    pool.sem_inc(pool_awake, 1)
                    pool.tensor_tensor(h_, h_, rows0[:, b, 0:1, :].to_broadcast([P, GT, D]), ALU.add).then_inc(h2_ready, 1)
            pool.wait_ge(once("filled"), 32)
            pool.wait_ge(*upto("place_ready", 1))
            pool.wait_ge(h2_ready, now(2 * NG - 1))
            for b in range(B):
                for c in range(NT):
                    i = b * NT + c
                    pool.indirect_dma_start(out=hs_dram, in_=h_all[:, b, c, :], in_offset=None,
                                            out_offset=bass.IndirectOffsetOnAxis(ap=place_i[:, i:i + 1], axis=0)).then_inc(once("rows_sorted"), 16)
            for s_ in range(SLOTS):
                pool.indirect_dma_start(out=ys_dram, in_=fill[:, 0, 0:D], in_offset=None,
                                        out_offset=bass.IndirectOffsetOnAxis(ap=spare[:, s_:s_ + 1], axis=0)).then_inc(ys_stored[s_], 16)
            with pool.Fori(0, NSORT // SLOTS) as i:
                for s_ in range(SLOTS):
                    n = SLOTS * i + s_
                    pool.wait_ge(hs_loaded[s_], 16 * (i + 1))
                    pool.wait_ge(ys_stored[s_], 16 * (i + 1))
                    pool.sem_inc(pool_awake, 1)
                    pool.tensor_copy(token_no[:, s_:s_ + 1], hs[:, s_, D:].bitcast(I32)).then_inc(numbers_kept, 1)
                for s_ in range(SLOTS):
                    n = SLOTS * i + s_
                    pool.wait_ge(numbers_kept, now(n))
                    pool.wait_ge(ys_ready, now(n))
                    pool.sem_inc(pool_awake, 1)
                    pool.indirect_dma_start(out=ys_dram, in_=ys[:, s_, :], in_offset=None,
                                            out_offset=bass.IndirectOffsetOnAxis(ap=token_no[:, s_:s_ + 1], axis=0)).then_inc(ys_stored[s_], 16)
            for half in range(2):
                pool.wait_ge(yx_loaded[half], 16 * B)
                with pool.Fori(half * NG // 2, (half + 1) * NG // 2) as g:
                  for b in range(B):
                    y_ = yx[:, b, bass.ds(g * GT, GT), :]
                    pool.tensor_tensor(y_, y_, rows0[:, b, 2:3, :].to_broadcast([P, GT, D]), ALU.mult).then_inc(yg_ready, 1)
            pool.iota(jt[:], pattern=[[1, NJ]], base=1, channel_multiplier=0)
            pool.iota(iota256[:], pattern=[[1, TOPK]], base=0, channel_multiplier=0, allow_small_or_imprecise_dtypes=True)
            pool.iota(tokid[:, :, 0], pattern=[[1, NT]], base=0, channel_multiplier=0, allow_small_or_imprecise_dtypes=True)
            pool.iota(tokid[:, :, 1], pattern=[[0, NT]], base=0, channel_multiplier=1, allow_small_or_imprecise_dtypes=True)
            pool.iota(iotap[:], pattern=[[P, ML // P]], base=0, channel_multiplier=1, allow_small_or_imprecise_dtypes=True)
            pool.memset(scan_ones[:], 1.0)
            pool.memset(eps_rms[:], RMS_EPS)
            for i in range(AD // 2):
                pool.memset(inv[:, i:i + 1], float(np.float32(1.0) / np.float32(ROPE_BASE ** (2.0 * i / AD))))
            ch.link(pool.memset(headmask[:], 1.0))
            ch.link(pool.affine_select(out=headmask[:], in_=headmask[:], compare_op=ALU.is_ge, fill=0.0, base=0,
                                       pattern=[[-AD, AH]], channel_multiplier=1))
            pool.affine_select(out=headmask[:], in_=headmask[:], compare_op=ALU.is_ge, fill=0.0, base=AD - 1,
                               pattern=[[AD, AH]], channel_multiplier=-1).then_inc(did("l1_consts"), 1)
            pool.wait_ge(*upto("rows_ready", 1))
            for (g, links) in ch.loop(NG, B):
                for b in range(B):
                    n = 2 * g + b
                    pool.wait_ge(hx_stored[b], 16 * (g + 1))
                    pool.wait_ge(dflt_stored[b], 16 * (g + 1))
                    pool.tensor_copy(hx[:, b, :, 0:D], xs[:, b, bass.ds(g * GT, GT), :]).then_inc(hxx_ready, 1)
                    pool.wait_ge(h4_ready, now(n))
                    links(pool.tensor_tensor(dflt[:, b], hx[:, b, :, D:2 * D], rows[:, b, 2:3, :].to_broadcast([P, GT, D]), ALU.mult))
                    pool.tensor_tensor(dflt[:, b], dflt[:, b], hx[:, b, :, 0:D], ALU.add).then_inc(dflt_ready, 1)
            for b in range(B):
                pool.wait_ge(hx_stored[b], 16 * (NG + 1))
            pool.wait_ge(*upto("gidx_ready", 1))
            mask_t = io["L1_ffn_attention_mask"].rearrange("b a q k -> (b a q) k")
            pos_t = io["L1_ffn_position_ids"].rearrange("b (q a) -> (b q) a", a=1)
            for s_ in range(NS4):
                tok, mrow = gidx[:, 0, s_:s_ + 1], gidx[:, 1, s_:s_ + 1]
                pool.indirect_dma_start(out=sx[:, s_, :], out_offset=None, in_=hx_dram,
                                        in_offset=bass.IndirectOffsetOnAxis(ap=tok, axis=0)).then_inc(once("sx_loaded"), 16)
            for s_ in range(NS4):
                mrow = gidx[:, 1, s_:s_ + 1]
                pool.indirect_dma_start(out=spos[:, s_:s_ + 1], out_offset=None, in_=pos_t,
                                        in_offset=bass.IndirectOffsetOnAxis(ap=mrow, axis=0)).then_inc(once("spos_loaded"), 16)
            for s_ in range(NS4):
                mrow = gidx[:, 1, s_:s_ + 1]
                pool.indirect_dma_start(out=smask[:, s_, :], out_offset=None, in_=mask_t,
                                        in_offset=bass.IndirectOffsetOnAxis(ap=mrow, axis=0)).then_inc(once("smask_loaded"), 16)
            pool.wait_ge(*upto("res_ready", 1))
            for b in range(B):
                pool.wait_ge(dflt_stored[b], 16 * (NG + 1))
            for s_ in range(NS4):
                m = P if s_ % NSEL < NSEL - 1 else P - (TOPK - SEL)
                pool.indirect_dma_start(out=out.rearrange("b t d -> (b t) d"), in_=res[0:m, s_, :], in_offset=None,
                                        out_offset=bass.IndirectOffsetOnAxis(ap=gidx[0:m, 0, s_:s_ + 1], axis=0)).then_inc(once("rows_scattered"), 16)
            pool.wait_ge(once("rows_scattered"), 16 * NS4)

        @block.scalar
        def _(act):
            credit(act, "act")
            act.wait_ge(mod_loaded, 64)
            for l in range(2):
                act.activation(cE[l][:], cT[l][:], ACT.Exp, scale=-1.0).then_inc(c_exp, 1)
            act.wait_ge(var_ready, 1)
            act.wait_ge(consts_ready, 1)
            act.activation(std[:], var[:], ACT.Sqrt, bias=eps_ln[:, 0:1]).then_inc(std_ready, 1)
            act.wait_ge(mod_ready, 1)
            with act.Fori(0, NG) as g:
                for b in range(B):
                    n = 2 * g + b
                    act.wait_ge(trans_ps, now(n))
                    act.wait_ge(hT_kept, back2(n))
                    act.wait_ge(tok_ps, back2(n))
                    act.activation(hT[:, b, :], bank[b][:], ACT.Identity, bias=modT[0][:, 0, b:b + 1],
                                   scale=modT[0][:, 1, b:b + 1]).then_inc(hT_ready, 1)
                for b in range(B):
                    act.wait_ge(z_ps, now(2 * g + b))
                    for k in range(2):
                        ins = act.activation(pk[:, b, bass.ds(g * GT, GT), PK_S + k * P:PK_S + (k + 1) * P],
                                             bank[2 + k][:].rearrange("p (q t) -> p q t", q=GT), ACT.Silu)
                    ins.then_inc(z_kept, 1)
            act.wait_ge(v_abs, 1)
            act.wait_ge(w_loaded, W_ALL)
            act.activation(expa[:], alog[:], ACT.Exp)
            act.activation(e_[:], r_[:], ACT.Exp, scale=-1.0).then_inc(e_exp, 1)
            act.wait_ge(u_ready, 1)
            act.activation(l_[:], u_[:], ACT.Ln).then_inc(ln_ready, 1)
            act.wait_ge(cum_ps, 1)
            act.activation(e_cum[:].rearrange("p b c h -> p (b c h)"), bank[0][:, 0:TH], ACT.Exp)
            act.activation(e_rest[:].rearrange("p b c h -> p (b c h)"), bank[1][:, 0:TH], ACT.Exp)
            for b in range(B):
                ins = act.activation(e_all[b * NS:(b + 1) * NS].rearrange("p c h -> p (c h)"),
                                     bank[2][b * NS:(b + 1) * NS, b * TH // B:(b + 1) * TH // B], ACT.Exp)
            ins.then_inc(decays_ready, 1)
            with act.Fori(0, NT) as c:
                for b in range(B):
                    n = 2 * c + b
                    act.wait_ge(segA_ps, now(n))
                    act.wait_ge(m_ready, back2(n))
                    act.activation(E[:, b, 0:4, :].rearrange("p h t -> p (h t)"), bank[0][:], ACT.Exp).then_inc(expA_done, 1)
                    act.wait_ge(segB_ps, now(n))
                    act.activation(E[:, b, 4:8, :].rearrange("p h t -> p (h t)"), bank[1][:], ACT.Exp).then_inc(expB_done, 1)
                    act.wait_ge(x_ps, now(n))
                    act.wait_ge(ysum_ready, back2(n))
                    act.wait_ge(dx_done, back2(n))
                    act.activation(Xsb[:, b], bank[2][:], ACT.Copy).then_inc(xsb_done, 1)
                for b in range(B):
                    n = 2 * c + b
                    act.wait_ge(yT_ps, now(n))
                    act.wait_ge(out_ps, back2(n))
                    act.activation(ygT[:, b].rearrange("p k t -> p (k t)"), bank[3][:], ACT.Copy).then_inc(ygT_done, 1)
            act.wait_ge(var_ready, 2)
            act.activation(std[:], var[:], ACT.Sqrt, bias=eps_ln[:, 0:1]).then_inc(std_ready, 1)
            with act.Fori(0, NG) as g:
                for b in range(B):
                    act.wait_ge(trans2_ps, now(2 * g + b))
                    act.wait_ge(router_ps, back2(2 * g + b))
                    for out_ in (hT_all[:, b, bass.ds(g * GW, GW)], hT[:, b, :]):
                        ins = act.activation(out_, bank[b][:], ACT.Identity, bias=modT[0][:, 3, b:b + 1], scale=modT[0][:, 4, b:b + 1])
                    ins.then_inc(hT2_ready, 1)
            with act.Fori(0, NG) as g:
                for b in range(B):
                    n = 2 * g + b
                    act.wait_ge(gate_ps, now(n))
                    act.wait_ge(hid_ready, back2(n))
                    for k in range(HID // P):
                        ins = act.activation(sg[:, b, k, :], bank[4 * b + k][:], ACT.Silu)
                    ins.then_inc(silu_done, 1)
            def keep_hsT(i):
                act.wait_ge(hsT_ps, now(SLOTS * i + SLOTS - 1))
                act.wait_ge(gu_ps, back1(SLOTS * i))
                act.activation(hsT[:].rearrange("p s q -> p (s q)"), bank[6][:, 0:SLOTS * P], ACT.Copy).then_inc(hsT_ready, 1)

            keep_hsT(0)
            with act.Fori(0, NSORT // SLOTS) as i:
                for s_ in range(SLOTS):
                    n = SLOTS * i + s_
                    act.wait_ge(gu_ps, now(n))
                    act.wait_ge(hids_ready, back3(n))
                    act.activation(sgs[:, s_, :], bank[s_][:, 0:HID], ACT.Silu).then_inc(silus_done, 1)
                keep_hsT(i + 1)
                for s_ in range(SLOTS):
                    n = SLOTS * i + s_
                    act.wait_ge(hidsT_ps, now(n))
                    act.wait_ge(ys_ps, back3(n))
                    act.activation(hidsT[:, s_, :], bank[3 + s_][:, 0:HID], ACT.Copy).then_inc(hidsT_ready, 1)
                for s_ in range(SLOTS):
                    n = SLOTS * i + s_
                    act.wait_ge(ys_ps, now(n))
                    act.wait_ge(ys_stored[s_], 16 * (i + 1))
                    act.activation(ys[:, s_, :], bank[s_][:, 0:D], ACT.Copy).then_inc(ys_ready, 1)
            act.wait_ge(s4_loaded, S4_ALL)
            act.activation(s4_ldt[:], s4_ldt[:], ACT.Exp)
            act.activation(s4_lam[:], s4_lam[:], ACT.Exp).then_inc(s4_exp1, 1)
            act.wait_ge(s4_prod, 1)
            act.activation(s4_a[:], s4_a[:], ACT.Exp, scale=-1.0).then_inc(s4_exp2, 1)
            act.wait_ge(var_ready, 3)
            act.activation(std[:], var[:], ACT.Sqrt, bias=eps_ln[:, 0:1]).then_inc(std_ready, 1)
            with act.Fori(0, NG) as g:
                for b in range(B):
                    n = 2 * g + b
                    act.wait_ge(trans3_ps, now(n))
                    act.wait_ge(s4out_ps, back2(n))
                    act.activation(hT[:, b, :], bank[b][:], ACT.Identity, bias=modT[1][:, 0, b:b + 1],
                                   scale=modT[1][:, 1, b:b + 1]).then_inc(hT3_ready, 1)

            act.wait_ge(var_ready, 4)
            act.activation(std[:], var[:], ACT.Sqrt, bias=eps_ln[:, 0:1]).then_inc(std_ready, 1)
            act.wait_ge(once("sx_loaded"), 16 * NS4)
            for s_ in range(NS4):
                ins = act.activation(squares[:, s_], sx[:, s_, D:2 * D], ACT.Square, accum_out=ss[:, s_:s_ + 1])
            ins.then_inc(did("ss_ready"), 1)
            act.wait_ge(*upto("ms_ready", 1))
            act.activation(sroot[:], ss[:], ACT.Sqrt).then_inc(did("sroot_ready"), 1)
            act.wait_ge(*upto("hnT_ps", 1))
            act.activation(hnT[:], bank[0][:], ACT.Copy).then_inc(did("hnT_ready"), 1)
            act.wait_ge(*upto("ang_ready", 1))
            act.activation(sc_[:], ang[:], ACT.Sin).then_inc(did("sin_ready"), 1)
            for s_ in range(NS4):
                act.wait_ge(*upto("qkv_ps", s_ + 1))
                act.activation(vv[:, s_], bank[1 + s_][:, 2 * D:3 * D], ACT.Copy)
                act.activation(qk[:, s_], bank[1 + s_][:, 0:2 * D], ACT.Copy).then_inc(did("qk_ready"), 1)
            for i in range(NS4):
                act.wait_ge(*upto("maskT_ps", i + 1))
                if i >= 2:
                    act.wait_ge(*upto("msel_ps", i - 1))
                act.activation(maskT[:, i % 2].rearrange("p k q -> p (k q)"), bank[5 * (1 - i % 2)][:], ACT.Copy).then_inc(did("maskT_ready"), 1)
            act.wait_ge(*upto("qT_ps", 1))
            act.activation(qT[:], bank[5][:], ACT.Copy)
            act.activation(kT[:], bank[6][:], ACT.Copy).then_inc(did("qkT_ready"), 1)
            for m in range(NM + LAG_O):
                if m < NM:
                    i, p, slot = m // PAIRS, m % PAIRS, m % SC_SLOTS
                    act.wait_ge(*upto("smax_ready", m + 1))
                    for k in range(2):
                        h = 2 * p + k
                        ins = act.activation(sc[:, slot, k], sc[:, slot, k], ACT.Exp, bias=smax[:, i, h:h + 1], accum_out=ssum[:, i, h:h + 1])
                    ins.then_inc(did("exp_ready"), 1)
                t = m - LAG_T
                if 0 <= t < NM:
                    act.wait_ge(*upto("pT_ps", t + 1))
                    if t >= SC_SLOTS:
                        act.wait_ge(*upto("pv_ps", t - SC_SLOTS + 1))
                    act.activation(pT[:, t % SC_SLOTS].rearrange("p k q -> p (k q)"), bank[2 + t % 2][:], ACT.Copy).then_inc(did("pT_ready"), 1)
            act.wait_ge(*upto("onT_ps", 1))
            act.activation(onT[:], bank[0][:], ACT.Copy).then_inc(did("onT_ready"), 1)
            act.wait_ge(*upto("x1_ready", 1))
            for s_ in range(NS4):
                ins = act.activation(squares[:, s_], x1[:, s_], ACT.Square, accum_out=ss[:, s_:s_ + 1])
            ins.then_inc(did("ss_ready"), 1)
            act.wait_ge(*upto("ms_ready", 2))
            act.activation(sroot[:], ss[:], ACT.Sqrt).then_inc(did("sroot_ready"), 1)
            act.wait_ge(*upto("hnT_ps", 2))
            act.activation(hnT[:], bank[0][:], ACT.Copy).then_inc(did("hnT_ready"), 1)
            for k in range(FF // P):
                act.wait_ge(*upto("hid_ps", k + 1))
                act.activation(hid1[:, k], bank[1 + k][:], ACT.Gelu_apprx_tanh).then_inc(did("gelu_ready"), 1)

        def ln_finish(dve, ch):
            me, mo = stats[:, :, 1], stats[:, :, 4]
            ve, vo = stats[:, :, 2], stats[:, :, 5]
            dve.tensor_tensor(mean[:], me, mo, ALU.add)
            dve.tensor_tensor(tmp_ln[:], me, mo, ALU.subtract)
            ch.link(dve.tensor_tensor(var[:], ve, vo, ALU.add))
            dve.tensor_scalar(mean[:], mean[:], 0.5, None, ALU.mult)
            dve.tensor_scalar(var[:], var[:], 1.0 / D, None, ALU.mult)
            ch.link(dve.scalar_tensor_tensor(out=tmp_ln[:], in0=tmp_ln[:], scalar=0.25, in1=tmp_ln[:],
                                             op0=ALU.mult, op1=ALU.mult))
            dve.tensor_tensor(var[:], var[:], tmp_ln[:], ALU.add).then_inc(var_ready, 1)

        def ln_rstd(dve, ch, n):
            dve.wait_ge(std_ready, n)
            ch.link(dve.reciprocal(rstd[:], std[:]))
            ch.link(dve.tensor_tensor(tmp_ln[:], rstd[:], rstd[:], ALU.mult))
            ch.link(dve.scalar_tensor_tensor(out=tmp_ln[:], in0=var[:], scalar=eps_ln[:, 0:1], in1=tmp_ln[:], op0=ALU.add, op1=ALU.mult))
            ch.link(dve.tensor_scalar(tmp_ln[:], tmp_ln[:], -0.5, 1.5, ALU.mult, ALU.add))
            ch.link(dve.tensor_tensor(rstd[:], rstd[:], tmp_ln[:], ALU.mult))

        def normalise(dve, g, b):
            for q in range(GT):
                i = g * GT + (b * NT + q)
                ins = dve.tensor_scalar(xhat[:, b, q, :], at(xs, b, g * GT + q), mean[:, bass.ds(i, 1)],
                                        rstd[:, bass.ds(i, 1)], ALU.subtract, ALU.mult)
            return ins

        def gate_(dve, ch, m, t0, t1):
            dve.tensor_scalar(t0, m, 0.0, 2.0, ALU.is_ge, ALU.mult)
            ch.link(dve.scalar_tensor_tensor(out=t1, in0=m, scalar=-1.0, in1=m, op0=ALU.mult, op1=ALU.max))
            ch.link(dve.tensor_scalar(t1, t1, 0.25, None, ALU.max))
            ch.link(dve.scalar_tensor_tensor(out=m, in0=t0, scalar=-1.0, in1=t1, op0=ALU.add, op1=ALU.mult))

        def rank_in(ch, dve, k, in_tile):
            for b in range(B):
                ins = dve.tensor_tensor_scan(incl[:, 0, b], scan_ones[:], tot[:, k, b], 0.0, ALU.mult, ALU.add)
            ch.link(ins)
            ch.link(dve.tensor_tensor(incl[:, 1], incl[:, 0], tot[:, k], ALU.subtract))
            ch.link(dve.tensor_tensor(pos[:].rearrange("p b c -> p (b c)"), incl[:, 1].rearrange("p b c -> p (b c)"), in_tile, ALU.add))

        @block.vector
        def _(dve):
            credit(dve, "dve")
            ch = Chain(dve, dve_self)
            dve.wait_ge(c_exp, 2)
            dve.wait_ge(mod_loaded, 64)
            for l in range(2):
                ch.link(dve.tensor_scalar(cE[l][:], cE[l][:], 1.0, None, ALU.add))
                ch.link(dve.reciprocal(cE[l][:], cE[l][:]))
                ch.link(dve.tensor_tensor(cS[l][:], cT[l][:], cE[l][:], ALU.mult))
            dve.wait_ge(consts_ready, 1)
            for l in range(2):
                for b in range(B):
                    ins = dve.tensor_scalar(crep[l][:, b, :], ones[:], cS[l][:, b:b + 1], None, ALU.mult)
            ins.then_inc(c_silu, 1)
            for half in range(2):
                dve.wait_ge(x_loaded[half], 32)
                with dve.Fori(half * NT // 2, (half + 1) * NT // 2) as c:
                    for b in range(B):
                        dve.bn_stats(flat(stats[:, bass.ds(c + b * NT, 1), :]), at(xs, b, c))
            ch.link(dve.tensor_copy(tmp_ln[:, 0:1], ones[:, 0:1]))
            ln_finish(dve, ch)
            dve.wait_ge(mod_ps, 1)
            for l in range(2):
                m = modT[l]
                ch.link(dve.tensor_copy(m[:], bank[4 + l][:, 0:12].rearrange("p (j b) -> p j b", b=B)))
                for j in (1, 4):
                    dve.tensor_scalar(m[:, j, :], m[:, j, :], 1.0, None, ALU.add)
                for j in (2, 5):
                    gate_(dve, ch, m[:, j, :], tmp_ln[:, 0:B], tmp_ln[:, B:2 * B])
            dve.sem_inc(mod_ready, 1)
            dve.wait_ge(ga_ps, 1)
            dve.wait_ge(w_loaded, W_ALL)
            for l in range(2):
                ch.link(dve.tensor_copy(gabc[l][:], bank[6][:, l * B * P:(l + 1) * B * P].rearrange("p (b d) -> p b d", b=B)))
                gate_(dve, ch, gabc[l][:], gt0[:], gt1[:])
            for b in range(B):
                dve.tensor_tensor(woutg[:, b], wout[:], gabc[0][:, b:b + 1, :].to_broadcast([P, 4, D]), ALU.mult)
            dve.tensor_copy(wbdt[:, 0:NS], win[:, 0:NS])
            dve.tensor_copy(wbdt[:, NS:], win[:, 2 * NS:2 * NS + H]).then_inc(ga_done, 1)
            ln_rstd(dve, ch, 1)
            with dve.Fori(0, NG) as g:
                for b in range(B):
                    dve.wait_ge(trans_ps, back2(2 * g + b))
                    normalise(dve, g, b).then_inc(xhat_ready, 1)
                for b in range(B):
                    dve.wait_ge(bc_ps, now(2 * g + b))
                    for k in range(2):
                        ins = dve.tensor_copy(bcT[b * NS:(b + 1) * NS, bass.ds(g * GT, GT), k, :],
                                              bank[4 + k][b * NS:(b + 1) * NS, :].rearrange("p (q t) -> p q t", q=GT))
                    ins.then_inc(bc_kept, 1)
                    dve.wait_ge(tok_ps, now(2 * g + b))
                    tok = bank[6][:, 0:GT * (NS + H)].rearrange("p (q n) -> p q n", q=GT)
                    dve.tensor_copy(pk[:, b, bass.ds(g * GT, GT), PK_B:PK_B + NS], tok[:, :, 0:NS])
                    dve.tensor_copy(dts[:, b, bass.ds(g * GT, GT), :], tok[:, :, NS:]).then_inc(tok_kept, 1)
            def rep(ap):
                return ap.unsqueeze(1).to_broadcast([P, B * NT, H])

            def by8(ap):
                return ap.rearrange("p (i h) -> p i h", h=H)

            fl = "p b c h -> p (b c h)"
            dve.wait_ge(tok_kept, now(2 * NG - 1))
            ch.link(dve.tensor_tensor(by8(v_[:]), by8(dts[:].rearrange(fl)), rep(dtb[:]), ALU.add))
            dve.scalar_tensor_tensor(out=r_[:], in0=v_[:], scalar=-1.0, in1=v_[:], op0=ALU.mult, op1=ALU.max).then_inc(v_abs, 1)
            dve.wait_ge(e_exp, 1)
            dve.tensor_scalar(u_[:], e_[:], 1.0, None, ALU.add).then_inc(u_ready, 1)
            dve.wait_ge(u_ready, 1)
            dve.reciprocal(r_[:], u_[:])
            ch.link(dve.scalar_tensor_tensor(out=e_[:], in0=u_[:], scalar=-1.0, in1=e_[:], op0=ALU.add, op1=ALU.subtract))
            ch.link(dve.tensor_tensor(e_[:], e_[:], r_[:], ALU.mult))
            ch.link(dve.scalar_tensor_tensor(out=v_[:], in0=v_[:], scalar=0.0, in1=e_[:], op0=ALU.max, op1=ALU.subtract))
            dve.wait_ge(ln_ready, 1)
            ch.link(dve.tensor_tensor(delta[:].rearrange(fl), v_[:], l_[:], ALU.add))
            dve.scalar_tensor_tensor(out=by8(a_dec[:].rearrange(fl)), in0=by8(delta[:].rearrange(fl)), scalar=-1.0,
                                     in1=rep(expa[:]), op0=ALU.mult, op1=ALU.mult).then_inc(a_ready, 1)
            dve.wait_ge(decays_ready, 1)
            dve.tensor_tensor(dw[:].rearrange(fl), delta[:].rearrange(fl), e_rest[:].rearrange(fl), ALU.mult).then_inc(dw_ready, 1)
            dve.wait_ge(dw_ready, 1)
            for (c, links) in ch.loop(NT, 1):
                for b in range(B):
                    n = 2 * c + b
                    dve.wait_ge(g_ps, now(n))
                    dve.tensor_tensor(Gm[:, b], bank[6][:, 0:P], upper[:], ALU.mult).then_inc(gm_done, 1)
                    dve.wait_ge(xsb_done, now(n))
                    dve.tensor_tensor(heads(dX[:, b]), heads(Xsb[:, b]), per_head(at(delta, b, c)), ALU.mult)
                    dve.tensor_tensor(heads(dXw[:, b]), heads(Xsb[:, b]), per_head(at(dw, b, c)), ALU.mult).then_inc(dx_done, 1)
                    dve.wait_ge(off_ps, now(n))
                    dve.tensor_tensor(heads(yoff[:, b]), heads(bank[3][:]), per_head(at(e_cum, b, c)), ALU.mult).then_inc(yoff_done, 1)
                    dve.wait_ge(gm_done, now(n))
                    dve.wait_ge(expA_done, now(n))
                    dve.wait_ge(expB_done, now(n))
                    dve.tensor_tensor(M[:, b], Gm[:, b:b + 1, :].to_broadcast([P, H, P]), E[:, b], ALU.mult).then_inc(m_ready, 1)
                for b in range(B):
                    n = 2 * c + b
                    dve.wait_ge(diag_ps, now(n))
                    dve.wait_ge(ysum_ready, now(n))
                    dve.tensor_tensor(y2[:, b], bank[6][:], ysum[:, b], ALU.add).then_inc(y2_done, 1)
                    dve.wait_ge(y2_done, now(n))
                    dve.wait_ge(zg_ps, now(n))
                    dve.tensor_tensor(yg[:, b], y2[:, b], bank[4 + b][:], ALU.mult).then_inc(yg_done, 1)
                dve.wait_ge(decays_ready, 1)
                dve.wait_ge(ds_ps, now(2 * c + 1))
                links(dve.tensor_tensor(heads(Sd[:]), heads(S[:]), per_head(flat(e_all[:, bass.ds(c, 1), :])), ALU.mult))
                dve.tensor_tensor(S[:], Sd[:], bank[2][:], ALU.add).then_inc(s_upd, 1)
                for b in range(B):
                    n = 2 * c + b
                    dve.wait_ge(out_ps, now(n))
                    dve.tensor_tensor(at(xs, b, c), at(xs, b, c), bank[7][:, 0:P], ALU.add).then_inc(xres_done, 1)
                    dve.wait_ge(xres_done, now(n))
                    dve.bn_stats(flat(stats[:, bass.ds(c + b * NT, 1), :]), at(xs, b, c))
            ch.link(dve.tensor_copy(tmp_ln[:, 0:1], ones[:, 0:1]))
            ln_finish(dve, ch)
            ln_rstd(dve, ch, 2)
            dve.wait_ge(*upto("rows0_ps", 1))
            for b in range(B):
                dve.tensor_copy(rows0[:, b], bank[6 + b][:, 0:3 * D].rearrange("p (j d) -> p j d", j=3))
            ch.link(dve.tensor_copy(tmp_ln[:, 0:1], ones[:, 0:1]))
            dve.tensor_scalar(rows0[:, :, 1, :], rows0[:, :, 1, :], 1.0, None, ALU.add)
            gate_(dve, ch, rows0[:, :, 2, :], gt0[:], gt1[:])
            dve.sem_inc(did("rows0_ready"), 1)
            with dve.Fori(0, NG) as g:
                for b in range(B):
                    n = 2 * g + b
                    dve.wait_ge(h2_ready, back2(n))
                    dve.wait_ge(trans2_ps, back2(n))
                    normalise(dve, g, b).then_inc(xhat2_ready, 1)
                for b in range(B):
                    n = 2 * g + b
                    dve.wait_ge(router_ps, now(n))
                    dve.tensor_copy(logits[:, bass.ds(g * GT + b * NT, GT), :],
                                    bank[2 + b][:, 0:GT * EX].rearrange("p (q e) -> p q e", q=GT)).then_inc(logits_kept, 1)
            dve.wait_ge(moe_consts, 1)
            dve.wait_ge(logits_kept, now(2 * NG - 1))

            def experts(ap):
                return ap.unsqueeze(2).to_broadcast([P, B * NT, EX])

            ch.link(dve.tensor_reduce(lmax[:], logits[:], AX.X, ALU.max))
            ch.link(dve.tensor_tensor(onehot[:], logits[:], experts(lmax[:]), ALU.is_equal))
            ch.link(dve.tensor_tensor(onehot[:], onehot[:], eighths[:].unsqueeze(1).to_broadcast([P, B * NT, EX]), ALU.mult))
            ch.link(dve.tensor_reduce(lmax[:], onehot[:], AX.X, ALU.max))
            dve.tensor_tensor(onehot[:], onehot[:], experts(lmax[:]), ALU.is_equal).then_inc(did("onehot_ready"), 1)
            dve.wait_ge(moe_loaded, MOE_ALL)
            for b in range(B):
                dve.tensor_tensor(wdown_g[:, b], wdown_s[:], rows0[:, b, 2:3, :].to_broadcast([P, HID // P, D]), ALU.mult)
            dve.wait_ge(*upto("ranks_ps", 1))
            by_expert = "p (i e) -> p e i"
            ch.link(dve.tensor_copy(tile_tot[:], bank[1][:, 0:B * NT * EX].rearrange(by_expert, e=EX)))
            ch.link(dve.tensor_tensor_scan(tile_cum[:].rearrange("p e i -> p (e i)"), keep_cum[:].rearrange("p e i -> p (e i)"),
                                           tile_tot[:].rearrange("p e i -> p (e i)"), 0.0, ALU.mult, ALU.add))
            ch.link(dve.tensor_scalar(need_i[:], tile_cum[:, :, B * NT - 1], float(P - 1), None, ALU.add))
            ch.link(dve.tensor_scalar(need_i[:], need_i[:], 7, None, ALU.arith_shift_right))
            ch.link(dve.tensor_copy(need[:], need_i[:]))
            ch.link(dve.tensor_tensor_scan(ends[:], ones[:, 0:EX], need[:], 0.0, ALU.mult, ALU.add))
            ch.link(dve.tensor_tensor(starts[:], ends[:], need[:], ALU.subtract))
            ch.link(dve.tensor_scalar(starts[:], starts[:], float(P), -1.0, ALU.mult, ALU.add))
            ch.link(dve.tensor_tensor(tile_cum[:], tile_cum[:], tile_tot[:], ALU.subtract))
            ch.link(dve.tensor_tensor(tile_cum[:], tile_cum[:], starts[:].unsqueeze(2).to_broadcast([P, EX, B * NT]), ALU.add))
            ch.link(dve.tensor_tensor(place[:], bank[0][:, 0:B * NT * EX].rearrange("p (i e) -> p i e", e=EX),
                                      tile_cum[:].rearrange("p e i -> p i e"), ALU.add))
            ch.link(dve.tensor_tensor(place[:], place[:], onehot[:], ALU.mult))
            ch.link(dve.tensor_reduce(place_f[:], place[:], AX.X, ALU.add))
            ch.link(dve.tensor_copy(place_i[:], place_f[:]))
            dve.sem_inc(did("place_ready"), 1)
            ch.link(dve.tensor_tensor(past[:], tile_no[:].unsqueeze(2).to_broadcast([P, NSORT, EX]),
                                      ends[:].unsqueeze(1).to_broadcast([P, NSORT, EX]), ALU.is_ge))
            ch.link(dve.tensor_reduce(expert_f[:], past[:], AX.X, ALU.add))
            ch.link(dve.tensor_scalar(expert_i[:], expert_f[:], float(EX - 1), None, ALU.min))
            dve.sem_inc(did("expert_ready"), 1)
            with dve.Fori(0, NG) as g:
                for b in range(B):
                    n = 2 * g + b
                    dve.wait_ge(silu_done, now(n))
                    dve.wait_ge(up_ps, now(n))
                    dve.wait_ge(down_ps, back2(n))
                    for k in range(HID // P):
                        ins = dve.tensor_tensor(hid[:, b, k, :], sg[:, b, k, :], bank[4 * b + 2 + k][:], ALU.mult)
                    ins.then_inc(hid_ready, 1)
                for b in range(B):
                    dve.wait_ge(down_ps, now(2 * g + b))
                    dve.tensor_tensor(xs[:, b, bass.ds(g * GT, GT), :], xs[:, b, bass.ds(g * GT, GT), :],
                                      bank[4 * b][:].rearrange("p (q d) -> p q d", q=GT), ALU.add).then_inc(xres2_done, 1)
            with dve.Fori(0, NSORT // SLOTS) as i:
                for s_ in range(SLOTS):
                    n = SLOTS * i + s_
                    dve.wait_ge(silus_done, now(n))
                    dve.wait_ge(hidsT_ps, back3(n))
                    dve.tensor_tensor(hids[:, s_, :], sgs[:, s_, :], bank[s_][:, HID:], ALU.mult).then_inc(hids_ready, 1)
            with dve.Fori(0, NG) as g:
                for b in range(B):
                    n = 2 * g + b
                    dve.wait_ge(yg_ready, now(n))
                    dve.tensor_tensor(xs[:, b, bass.ds(g * GT, GT), :], xs[:, b, bass.ds(g * GT, GT), :],
                                      yx[:, b, bass.ds(g * GT, GT), :], ALU.add).then_inc(yx_added, 1)
                    dve.wait_ge(yx_added, now(n))
                    for q in range(GT):
                        dve.bn_stats(flat(stats[:, bass.ds(g * GT + (b * NT + q), 1), :]), at(xs, b, g * GT + q))
            dve.wait_ge(s4_exp1, 1)
            dve.tensor_tensor(s4_a[:], s4_ldt[:], s4_lam[:], ALU.mult).then_inc(s4_prod, 1)
            ch.link(dve.tensor_copy(tmp_ln[:, 0:1], ones[:, 0:1]))
            ln_finish(dve, ch)
            dve.wait_ge(s4_exp2, 1)
            for k in range(GT):
                dve.tensor_scalar(s4_abc[:, k * P:(k + 1) * P], ones[:], s4_a[:, 0:1], None, ALU.mult)
            for b in range(B):
                dve.tensor_tensor(s4_Cg[b * NS:(b + 1) * NS], s4_C[b * NS:(b + 1) * NS], gabc[1][b * NS:(b + 1) * NS, b, :], ALU.mult)
                ins = dve.tensor_scalar(s4_Dg[:, b], ident[:], s4_D[:, 0:1], modT[1][:, 2, b:b + 1], ALU.mult, ALU.mult)
            ch.link(ins)
            dve.sem_inc(s4_ready, 1)
            ln_rstd(dve, ch, 3)
            for (g, links) in ch.loop(NG, 1):
                for b in range(B):
                    dve.wait_ge(trans3_ps, back2(2 * g + b))
                    normalise(dve, g, b).then_inc(xhat3_ready, 1)
                dve.wait_ge(bu_ps, now(2 * g + 1))
                dve.wait_ge(s4out_ps, back1(2 * g))
                dve.tensor_tensor_scan(s4_x[:], s4_abc[:], bank[2][:], s4_carry[:, 0:1], ALU.mult, ALU.add).then_inc(scan_done, 1)
                dve.wait_ge(scan_done, now(g))
                links(dve.tensor_copy(s4_carry[:], s4_x[:, GW - 1:GW]))
                for b in range(B):
                    n = 2 * g + b
                    dve.wait_ge(s4out_ps, now(n))
                    dve.tensor_tensor(xs[:, b, bass.ds(g * GT, GT), :], xs[:, b, bass.ds(g * GT, GT), :],
                                      bank[4 + b][:].rearrange("p (q d) -> p q d", q=GT), ALU.add).then_inc(xres3_done, 1)
                    dve.wait_ge(xres3_done, now(n))
                    for q in range(GT):
                        dve.bn_stats(flat(stats[:, bass.ds(g * GT + (b * NT + q), 1), :]), at(xs, b, g * GT + q))

            dve.wait_ge(*upto("rows_ps", 1))
            for b in range(B):
                dve.tensor_copy(rows[:, b], bank[6 + b][:, 0:3 * D].rearrange("p (j d) -> p j d", j=3))
            ch.link(dve.tensor_copy(tmp_ln[:, 0:1], ones[:, 0:1]))
            dve.tensor_scalar(rows[:, :, 1, :], rows[:, :, 1, :], 1.0, None, ALU.add)
            gate_(dve, ch, rows[:, :, 2, :], gt0[:], gt1[:])
            dve.sem_inc(did("rows_ready"), 1)
            ln_finish(dve, ch)
            ln_rstd(dve, ch, 4)
            dve.wait_ge(once("l1_loaded"), L1_ALL)
            for (g, links) in ch.loop(NG, B * 3):
                for b in range(B):
                    n = 2 * g + b
                    normalise(dve, g, b).then_inc(xhat4_ready, 1)
                    dve.wait_ge(xhat4_ready, now(n))
                    dve.wait_ge(hx_stored[b], 16 * (g + 1))
                    dve.wait_ge(dflt_ready, back2(n))
                    h_ = hx[:, b, :, D:2 * D]
                    links(dve.tensor_tensor(h_, xhat[:, b], rows[:, b, 1:2, :].to_broadcast([P, GT, D]), ALU.mult))
                    dve.tensor_tensor(h_, h_, rows[:, b, 0:1, :].to_broadcast([P, GT, D]), ALU.add).then_inc(h4_ready, 1)
                    dve.wait_ge(h4_ready, now(n))
                    links(dve.tensor_tensor(hprod[:], h_, rw_row[:].unsqueeze(1).to_broadcast([P, GT, D]), ALU.mult))
                    links(dve.tensor_reduce(wred[:], hprod[:], AX.X, ALU.add))
                    dve.tensor_scalar(w_all[:, b, bass.ds(g * GT, GT)], wred[:], rb_col[:, 0:1], None, ALU.add)
                    dve.tensor_scalar(hx[:, b, :, 2 * D], wred[:], rb_col[:, 0:1], None, ALU.add).then_inc(w4_ready, 1)
            dve.wait_ge(*upto("l1_consts", 1))
            for k in range(NSTEP):
                ins = dve.tensor_scalar(J[:, k], jt[:], 28 - 4 * k, None, ALU.logical_shift_left)
            ch.link(ins)
            ch.link(dve.memset(pre[:], 0))

            def to_float_bits(out_, tmp, u):
                ch.link(dve.tensor_scalar(tmp, u, 31, -1, ALU.arith_shift_right, ALU.bitwise_xor))
                ch.link(dve.scalar_tensor_tensor(out=out_, in0=tmp, scalar=-2**31, in1=u, op0=ALU.bitwise_or, op1=ALU.bitwise_xor))

            for k in range(NSTEP):
                ch.link(dve.tensor_tensor(cand[:], pre[:].unsqueeze(2).to_broadcast([P, B, NJ]),
                                          J[:, k:k + 1, :].to_broadcast([P, B, NJ]), ALU.bitwise_or))
                to_float_bits(candf[:], candt[:], cand[:])
                ch.link(dve.tensor_tensor(cmp_[:], w_all[:].unsqueeze(2).to_broadcast([P, B, NJ, NT]),
                                          candf[:].bitcast(F32).unsqueeze(3).to_broadcast([P, B, NJ, NT]), ALU.is_ge))
                dve.tensor_reduce(cnt[:], cmp_[:], AX.X, ALU.add).then_inc(did("cnt_ready"), 1)
                dve.wait_ge(*upto("cnt_ps", k + 1))
                ch.link(dve.tensor_scalar(ge256[:].rearrange("p b j -> p (b j)"), bank[0][:, 0:B * NJ], float(TOPK), None, ALU.is_ge))
                ch.link(dve.tensor_reduce(digitf[:], ge256[:], AX.X, ALU.add))
                ch.link(dve.tensor_copy(digit[:], digitf[:]))
                ch.link(dve.scalar_tensor_tensor(out=pre[:], in0=digit[:], scalar=28 - 4 * k, in1=pre[:],
                                                 op0=ALU.logical_shift_left, op1=ALU.bitwise_or))
            to_float_bits(thr[:], thr_t[:], pre[:])
            thrb = thr[:].bitcast(F32).unsqueeze(2).to_broadcast([P, B, NT])
            dve.tensor_tensor(gteq[:, 0], w_all[:], thrb, ALU.is_gt)
            dve.tensor_tensor(gteq[:, 1], w_all[:], thrb, ALU.is_equal).then_inc(did("gteq_ready"), 1)
            dve.wait_ge(*upto("gteq_ps", 1))
            ch.link(dve.tensor_copy(tot[:, 0:2].rearrange("p k b c -> p (k b c)"), bank[0][:, 0:2 * B * NT]))
            rank_in(ch, dve, 1, bank[0][:, 2 * B * NT:3 * B * NT])
            ch.link(dve.tensor_reduce(ngt[:], tot[:, 0], AX.X, ALU.add))
            ch.link(dve.tensor_scalar(ngt[:], ngt[:], -1.0, float(SEL), ALU.mult, ALU.add))
            ch.link(dve.tensor_tensor(sel[:], pos[:], ngt[:].unsqueeze(2).to_broadcast([P, B, NT]), ALU.is_le))
            ch.link(dve.tensor_tensor(sel[:], sel[:], gteq[:, 1], ALU.mult))
            dve.tensor_tensor(sel[:], sel[:], gteq[:, 0], ALU.add).then_inc(did("sel_ready"), 1)
            dve.wait_ge(*upto("sel_ps", 1))
            ch.link(dve.tensor_copy(tot[:, 1].rearrange("p b c -> p (b c)"), bank[0][:, 0:B * NT]))
            rank_in(ch, dve, 1, bank[0][:, B * NT:2 * B * NT])
            ch.link(dve.tensor_tensor(pos[:], pos[:], sel[:], ALU.mult))
            ch.link(dve.tensor_scalar(pos[:], pos[:], -1.0, None, ALU.add))
            for b in range(B):
                with dve.Fori(0, NT) as c:
                    dve.tensor_scalar(flat(choose[:, b, bass.ds(c, 1), :]), iota256[:], pos[:, b, bass.ds(c, 1)], None, ALU.is_equal)
            ch.link(dve.tensor_copy(tmp_ln[:, 0:1], ones[:, 0:1]))
            dve.sem_inc(did("choose_ready"), 1)
            dve.wait_ge(*upto("picks_ps", 1))
            ch.link(dve.tensor_copy(picks[:].rearrange("p s j -> p (s j)"), bank[1][:, 0:2 * NS4]))
            ch.link(dve.scalar_tensor_tensor(out=idx[:], in0=picks[:, :, 0], scalar=float(P), in1=picks[:, :, 1], op0=ALU.mult, op1=ALU.add))
            ch.link(dve.tensor_scalar(cidx[:], idx[:], float(ML - 1), None, ALU.min))
            for b in range(B):
                c0, c1 = b * NSEL, (b + 1) * NSEL
                dve.tensor_scalar(gidx[:, 0, c0:c1], idx[:, c0:c1], float(b * T), None, ALU.add)
                ins = dve.tensor_scalar(gidx[:, 1, c0:c1], cidx[:, c0:c1], float(b * ML), None, ALU.add)
            ins.then_inc(did("gidx_ready"), 1)
            for b in range(B):
                dve.wait_ge(*upto("cidx_ps", b + 1))
                for k in range(ML // P):
                    ins = dve.tensor_scalar(colsel[:, b, k, :], bank[6 + b][:, 0:TOPK], iotap[:, k:k + 1], None, ALU.is_equal)
                ins.then_inc(did("colsel_ready"), 1)

            def rms(src, j):
                dve.wait_ge(*upto("ss_ready", j + 1))
                ch.link(dve.tensor_scalar(ss[:], ss[:], 1.0 / D, RMS_EPS, ALU.mult, ALU.add))
                dve.sem_inc(did("ms_ready"), 1)
                dve.wait_ge(*upto("sroot_ready", j + 1))
                ch.link(dve.reciprocal(srr[:], sroot[:]))
                ch.link(dve.tensor_tensor(st[:], srr[:], srr[:], ALU.mult))
                ch.link(dve.tensor_tensor(st[:], st[:], ss[:], ALU.mult))
                ch.link(dve.tensor_scalar(st[:], st[:], -0.5, 1.5, ALU.mult, ALU.add))
                ch.link(dve.tensor_tensor(srr[:], srr[:], st[:], ALU.mult))
                ch.link(dve.tensor_tensor(hn[:], src, srr[:].unsqueeze(2).to_broadcast([P, NS4, D]), ALU.mult))
                dve.tensor_tensor(hn[:], hn[:], ln_row[:, j:j + 1, :].to_broadcast([P, NS4, D]), ALU.mult).then_inc(did("hn_ready"), 1)

            dve.wait_ge(once("sx_loaded"), 16 * NS4)
            rms(sx[:, :, D:2 * D], 0)
            dve.wait_ge(once("spos_loaded"), 16 * NS4)
            ch.link(dve.tensor_copy(st[:], spos[:]))
            ch.link(dve.tensor_tensor(ang[:, 0], st[:].unsqueeze(2).to_broadcast([P, NS4, AD // 2]),
                                      inv[:].unsqueeze(1).to_broadcast([P, NS4, AD // 2]), ALU.mult))
            ch.link(dve.tensor_scalar(ang[:, 1], ang[:, 0], 0.0, None, ALU.add))
            two_pi = 2.0 * np.pi
            ch.link(dve.tensor_scalar(angk[:, 0], ang[:, 0], 1.0 / two_pi, None, ALU.mult))
            ch.link(dve.tensor_scalar(angk[:, 1], ang[:, 1], 1.0 / two_pi, 0.25, ALU.mult, ALU.add))
            ch.link(dve.tensor_copy(angi[:], angk[:]))
            ch.link(dve.tensor_copy(angk[:], angi[:]))
            part1 = 6.28125
            part2 = 1.9350051879882812e-3
            part3 = two_pi - part1 - part2
            for part in (part1, part2, part3):
                ch.link(dve.scalar_tensor_tensor(out=ang[:].rearrange("p t s i -> p (t s i)"), in0=angk[:].rearrange("p t s i -> p (t s i)"),
                                                 scalar=-part, in1=ang[:].rearrange("p t s i -> p (t s i)"), op0=ALU.mult, op1=ALU.add))
            ch.link(dve.tensor_scalar(ang[:, 1], ang[:, 1], float(np.pi / 2), None, ALU.add))
            dve.tensor_scalar(ang[:], ang[:], 3.1415925, -3.1415925, ALU.min, ALU.max).then_inc(did("ang_ready"), 1)
            dve.wait_ge(*upto("sin_ready", 1))
            for s_ in range(NS4):
                dve.wait_ge(*upto("qk_ready", s_ + 1))

                def halves(t):
                    return t.rearrange("p (h t i) -> p h t i", t=2, i=AD // 2)

                def angle(j):
                    return sc_[:, j, s_:s_ + 1, :].unsqueeze(1).to_broadcast([P, 2 * AH, 2, AD // 2])

                dve.tensor_tensor(halves(qks[:]), halves(qk[:, s_]), angle(0), ALU.mult)
                ch.link(dve.tensor_tensor(halves(qkc[:]), halves(qk[:, s_]), angle(1), ALU.mult))
                c_, n_, o_ = halves(qkc[:]), halves(qks[:]), halves(qk[:, s_])
                dve.tensor_tensor(o_[:, :, 0, :], c_[:, :, 0, :], n_[:, :, 1, :], ALU.subtract)
                ch.link(dve.tensor_tensor(o_[:, :, 1, :], c_[:, :, 1, :], n_[:, :, 0, :], ALU.add))
                dve.tensor_scalar(qk[:, s_, 0:D], qk[:, s_, 0:D], float(1.0 / np.sqrt(AD)), None, ALU.mult).then_inc(did("rope_ready"), 1)
            dve.wait_ge(*upto("msel_ps", NS4))
            for i in range(NS4):
                dve.tensor_copy(msel[:, i], bank[1 + i][:, 0:TOPK])
            ch.link(dve.tensor_copy(tmp_ln[:, 0:1], ones[:, 0:1]))
            ch.link(dve.memset(msel[:, :, SEL:TOPK], -3.0e38))
            dve.sem_inc(did("msel_ready"), 1)
            dve.wait_ge(*upto("qkT_ready", 1))

            def one_head(b, h):
                return dve.tensor_scalar(kTm[:, b, h, :], kT[:, b * TOPK:(b + 1) * TOPK], headmask[:, h:h + 1], None, ALU.mult)

            for h in range(2):
                ins = one_head(0, h)
            ins.then_inc(kTm_ready, 1)
            for m in range(NM + LAG_O):
                if m < NM:
                    i, p, slot = m // PAIRS, m % PAIRS, m % SC_SLOTS
                    dve.wait_ge(*upto("score_ps", m + 1))
                    if m >= SC_SLOTS:
                        dve.wait_ge(*upto("pT_ps", m - SC_SLOTS + 1))
                    dve.tensor_tensor(sc[:, slot], bank[5 + m % 2][:].rearrange("p (h k) -> p h k", h=2),
                                      msel[:, i:i + 1, :].to_broadcast([P, 2, TOPK]), ALU.add).then_inc(did("masked_ready"), 1)
                    n = m + 1
                    if n < NM and n // PAIRS % NSEL == 0:
                        for h in range(2):
                            ins = one_head(n // PAIRS // NSEL, 2 * (n % PAIRS) + h)
                        ins.then_inc(kTm_ready, 1)
                    dve.wait_ge(*upto("masked_ready", m + 1))
                    dve.tensor_reduce(smax[:, i, 2 * p:2 * p + 2], sc[:, slot], AX.X, ALU.max, negate=True).then_inc(did("smax_ready"), 1)
                m -= LAG_O
                if m >= 0 and m % PAIRS == PAIRS - 1:
                    i = m // PAIRS
                    dve.wait_ge(*upto("exp_ready", m + 1))
                    ch.link(dve.reciprocal(sinv[:, i % 2], ssum[:, i]))
                    dve.wait_ge(*upto("pv_ps", m + 1))
                    dve.tensor_tensor(on[:, i].rearrange("p (h d) -> p h d", h=AH), bank[i % 2][:, 0:D].rearrange("p (h d) -> p h d", h=AH),
                                      sinv[:, i % 2].unsqueeze(2).to_broadcast([P, AH, AD]), ALU.mult).then_inc(did("on_ready"), 1)
            dve.wait_ge(*upto("wo_ps", 1))
            dve.tensor_tensor(x1[:], bank[1][:].rearrange("p (s d) -> p s d", s=NS4), sx[:, :, D:2 * D], ALU.add).then_inc(did("x1_ready"), 1)
            rms(x1[:], 1)
            dve.wait_ge(*upto("w2_ps", 1))
            ch.link(dve.tensor_tensor(x2[:], bank[5][:].rearrange("p (s d) -> p s d", s=NS4), x1[:], ALU.add))
            ch.link(dve.tensor_tensor(x2[:], x2[:], sx[:, :, 2 * D:].to_broadcast([P, NS4, D]), ALU.mult))
            for b in range(B):
                c0, c1 = b * NSEL, (b + 1) * NSEL
                ins = dve.tensor_scalar(notsel[:, c0:c1], sx[:, c0:c1, 2 * D], thr[:, b:b + 1].bitcast(F32), None, ALU.is_le)
            ch.link(ins)
            ch.link(dve.tensor_tensor(res[:], sx[:, :, D:2 * D], notsel[:].unsqueeze(2).to_broadcast([P, NS4, D]), ALU.mult))
            ch.link(dve.tensor_tensor(x2[:], x2[:], res[:], ALU.add))
            for b in range(B):
                c0, c1 = b * NSEL, (b + 1) * NSEL
                ins = dve.tensor_tensor(x2[:, c0:c1], x2[:, c0:c1], rows[:, b, 2:3, :].to_broadcast([P, NSEL, D]), ALU.mult)
            ch.link(ins)
            dve.tensor_tensor(res[:], x2[:], sx[:, :, 0:D], ALU.add).then_inc(did("res_ready"), 1)

        def transposes(pe, g, b):
            n = 2 * g + b
            pe.wait_ge(xhat_ready, now(n))
            pe.wait_ge(hT_ready, back2(n))
            for q in range(GT):
                ins = pe.transpose(bank[b][:, q * P:(q + 1) * P], xhat[:, b, q, :], ident[:])
            ins.then_inc(trans_ps, 1)

        @block.tensor
        def _(pe):
            credit(pe, "pe")
            pe.wait_ge(c_silu, 1)
            pe.wait_ge(mod_loaded, 64)
            pe.wait_ge(consts_ready, 1)
            for l in range(2):
                for j in range(6):
                    ins = pe.matmul(bank[4 + l][:, 2 * j:2 * j + 2], wmod[l][:, j * D:(j + 1) * D], cS[l][:], start=True, stop=True)
            ins.then_inc(mod_ps, 1)
            for l in range(2):
                for b in range(B):
                    i = l * B + b
                    ins = pe.matmul(bank[6][:, i * P:(i + 1) * P], crep[l][:, b, :], wmod[l][:, 2 * D:3 * D], start=True, stop=True)
            ins.then_inc(ga_ps, 1)
            pe.wait_ge(w_loaded, W_ALL)
            pe.wait_ge(ga_done, 1)
            with pe.Fori(0, NG) as g:
                for b in range(B):
                    transposes(pe, g, b)
                for b in range(B):
                    n = 2 * g + b
                    pe.wait_ge(hT_ready, now(n))
                    pe.wait_ge(z_kept, back1(n))
                    for k in range(2):
                        ins = pe.matmul(bank[2 + k][:], wz[:, k * P:(k + 1) * P], hT[:, b, :], start=True, stop=True)
                    ins.then_inc(z_ps, 1)
                    pe.wait_ge(bc_kept, back1(n))
                    for k in range(2):
                        ins = pe.matmul(bank[4 + k][b * NS:(b + 1) * NS, :], win[:, k * NS:(k + 1) * NS], hT[:, b, :], start=True, stop=True)
                    ins.then_inc(bc_ps, 1)
                    pe.wait_ge(tok_kept, back1(n))
                    for q in range(GT):
                        ins = pe.matmul(bank[6][:, q * (NS + H):(q + 1) * (NS + H)], hT[:, b, q * P:(q + 1) * P], wbdt[:], start=True, stop=True)
                    ins.then_inc(tok_ps, 1)
            pe.wait_ge(a_ready, 1)
            pe.wait_ge(z_kept, now(2 * NG - 1))
            af = a_dec[:].rearrange("p b c h -> p (b c h)")
            for i, mask in enumerate((upper, lower, ones)):
                ins = pe.matmul(bank[i][:, 0:TH], mask[:], af, start=True, stop=True)
            ins.then_inc(cum_ps, 1)
            pe.wait_ge(decays_ready, 1)
            pe.wait_ge(bc_kept, now(2 * NG - 1))
            pe.wait_ge(tok_kept, now(2 * NG - 1))
            with pe.Fori(0, NT) as c:
                for b in range(B):
                    n = 2 * c + b
                    lo, hi = b * NS, (b + 1) * NS
                    pe.wait_ge(pk_loaded[b], 32 * (c + 1))
                    pe.wait_ge(gm_done, back1(n))
                    if b == 0:
                        pe.wait_ge(y2_done, back1(n))
                    pe.matmul(bank[6][:, 0:P], bc_slot[lo:hi, 0, :], bc_slot[lo:hi, 1, :], start=True, stop=True).then_inc(g_ps, 1)
                    pe.wait_ge(segrhs_ready, now(n))
                    pe.wait_ge(expA_done, back1(n))
                    pe.matmul(bank[0][:], lower[:], seg_rhs[:, b, 0:4, :].rearrange("p h t -> p (h t)"), start=True, stop=True).then_inc(segA_ps, 1)
                    pe.wait_ge(expB_done, back1(n))
                    pe.matmul(bank[1][:], lower[:], seg_rhs[:, b, 4:8, :].rearrange("p h t -> p (h t)"), start=True, stop=True).then_inc(segB_ps, 1)
                    pe.wait_ge(xsb_done, back1(n))
                    pe.wait_ge(s_upd, back1(c))
                    pe.matmul(bank[2][:], pk_slot[:, b, PK_H:PK_H + P], win[:, 2 * NS + H:], start=True, stop=True).then_inc(x_ps, 1)
                    pe.wait_ge(yoff_done, back1(n))
                    pe.wait_ge(yg_done, back2(n))
                    for k in range(2):
                        ins = pe.matmul(bank[4 + b][:], pk_slot[:, b, PK_S + k * P:PK_S + (k + 1) * P], wzg[:, k, :], start=k == 0, stop=k == 1)
                    ins.then_inc(zg_ps, 1)
                    if b == 0:
                        pe.wait_ge(ygT_done, back1(n))
                    pe.matmul(bank[3][:], bc_slot[lo:hi, 1, :], S[lo:hi, :], start=True, stop=True).then_inc(off_ps, 1)
                for b in range(B):
                    n = 2 * c + b
                    pe.wait_ge(m_ready, now(n))
                    if b == 0:
                        pe.wait_ge(gm_done, now(n + 1))
                    else:
                        pe.wait_ge(y2_done, back1(n))
                    for h in range(H):
                        ins = pe.matmul(bank[6][:, h * HD:(h + 1) * HD], M[:, b, h, :], dX[:, b, h * HD:(h + 1) * HD], start=True, stop=True)
                    ins.then_inc(diag_ps, 1)
                    pe.wait_ge(xsb_done, now(2 * c + 1))
                    pe.wait_ge(dx_done, now(n))
                    pe.matmul(bank[2][b * NS:(b + 1) * NS, :], pk_slot[:, b, PK_B:PK_B + NS], dXw[:, b], start=True, stop=True).then_inc(ds_ps, 1)
                for b in range(B):
                    n = 2 * c + b
                    pe.wait_ge(yg_done, now(n))
                    pe.wait_ge(ygT_done, back1(n))
                    for k in range(4):
                        ins = pe.transpose(bank[3][:, k * P:(k + 1) * P], yg[:, b, k * P:(k + 1) * P], ident[:])
                    ins.then_inc(yT_ps, 1)
                for b in range(B):
                    n = 2 * c + b
                    pe.wait_ge(ygT_done, now(n))
                    pe.wait_ge(xres_done, back1(n))
                    for k in range(4):
                        ins = pe.matmul(bank[7][:, 0:P], ygT[:, b, k, :], woutg[:, b, k, :], start=k == 0, stop=k == 3)
                    ins.then_inc(out_ps, 1)

            pe.wait_ge(xres_done, now(2 * NT - 1))
            for b in range(B):
                ins = pe.matmul(bank[6 + b][:, 0:3 * D], crep[0][:, b, :], wmod[0][:, 3 * D:6 * D], start=True, stop=True)
            ins.then_inc(did("rows0_ps"), 1)
            with pe.Fori(0, NG) as g:
                for b in range(B):
                    n = 2 * g + b
                    pe.wait_ge(xhat2_ready, now(n))
                    pe.wait_ge(hT2_ready, back2(n))
                    for q in range(GT):
                        ins = pe.transpose(bank[b][:, q * P:(q + 1) * P], xhat[:, b, q, :], ident[:])
                    ins.then_inc(trans2_ps, 1)
                for b in range(B):
                    n = 2 * g + b
                    pe.wait_ge(hT2_ready, now(n))
                    pe.wait_ge(logits_kept, back2(n))
                    for q in range(GT):
                        ins = pe.matmul(bank[2 + b][:, q * EX:(q + 1) * EX], hT[:, b, q * P:(q + 1) * P], wrouter[:], start=True, stop=True)
                    ins.then_inc(router_ps, 1)
            pe.wait_ge(*upto("onehot_ready", 1))
            oh = onehot[:].rearrange("p i e -> p (i e)")
            pe.matmul(bank[0][:, 0:B * NT * EX], upper[:], oh, start=True, stop=True)
            pe.matmul(bank[1][:, 0:B * NT * EX], ones[:], oh, start=True, stop=True).then_inc(did("ranks_ps"), 1)
            pe.wait_ge(*upto("place_ready", 1))
            pe.wait_ge(moe_loaded, MOE_ALL)
            with pe.Fori(0, NG) as g:
                for b in range(B):
                    n = 2 * g + b
                    h_ = hT_all[:, b, bass.ds(g * GW, GW)]
                    pe.wait_ge(xres2_done, back2(n))
                    for k in range(HID // P):
                        ins = pe.matmul(bank[4 * b + k][:], wgu_s[:, k * P:(k + 1) * P], h_, start=True, stop=True)
                    ins.then_inc(gate_ps, 1)
                    for k in range(HID // P):
                        ins = pe.matmul(bank[4 * b + 2 + k][:], wgu_s[:, HID + k * P:HID + (k + 1) * P], h_, start=True, stop=True)
                    ins.then_inc(up_ps, 1)
                for b in range(B):
                    n = 2 * g + b
                    pe.wait_ge(hid_ready, now(n))
                    for q in range(GT):
                        for k in range(HID // P):
                            ins = pe.matmul(bank[4 * b][:, q * D:(q + 1) * D], hid[:, b, k, q * P:(q + 1) * P], wdown_g[:, b, k, :],
                                            start=k == 0, stop=k == HID // P - 1)
                    ins.then_inc(down_ps, 1)
            tile_expert = []
            pe.wait_ge(*upto("expert_ready", 1))
            pe.wait_ge(xres2_done, now(2 * NG - 1))
            for s_ in range(SLOTS):
                pe.wait_ge(hs_loaded[s_], 16)
                pe.transpose(bank[6][:, s_ * P:(s_ + 1) * P], hs[:, s_, 0:D], ident[:]).then_inc(hsT_ps, 1)
            with pe.Fori(0, NSORT // SLOTS) as i:
                for s_ in range(SLOTS):
                    n = SLOTS * i + s_
                    e = pe.value_load(expert_i[0:1, bass.ds(n, 1)], min_val=0, max_val=EX - 1)
                    tile_expert.append(e)
                    pe.wait_ge(hsT_ready, now(i))
                    pe.wait_ge(ys_ready, back3(n))
                    pe.matmul(bank[s_][:], hsT[:, s_, :], wgu[:, bass.ds(e, 1), :].rearrange("p a h -> p (a h)"), start=True, stop=True).then_inc(gu_ps, 1)
                for s_ in range(SLOTS):
                    pe.wait_ge(hs_loaded[s_], 16 * (i + 2))
                    pe.wait_ge(hsT_ready, now(i))
                    pe.transpose(bank[6][:, s_ * P:(s_ + 1) * P], hs[:, s_, 0:D], ident[:]).then_inc(hsT_ps, 1)
                for s_ in range(SLOTS):
                    n = SLOTS * i + s_
                    pe.wait_ge(hids_ready, now(n))
                    pe.wait_ge(hidsT_ready, back3(n))
                    for k in range(HID // P):
                        ins = pe.transpose(bank[3 + s_][:, k * P:(k + 1) * P], hids[:, s_, k * P:(k + 1) * P], ident[:])
                    ins.then_inc(hidsT_ps, 1)
                for s_ in range(SLOTS):
                    n = SLOTS * i + s_
                    e = tile_expert[s_]
                    pe.wait_ge(hidsT_ready, now(n))
                    for k in range(HID // P):
                        ins = pe.matmul(bank[s_][:, 0:D], hidsT[:, s_, k * P:(k + 1) * P],
                                        wdown[:, bass.ds(e, 1), k, :].rearrange("p a d -> p (a d)"), start=k == 0, stop=k == HID // P - 1)
                    ins.then_inc(ys_ps, 1)
            pe.wait_ge(s4_ready, 1)
            pe.wait_ge(s4_loaded, S4_ALL)
            pe.wait_ge(ys_ready, now(NSORT - 1))
            with pe.Fori(0, NG) as g:
                for b in range(B):
                    n = 2 * g + b
                    pe.wait_ge(xhat3_ready, now(n))
                    pe.wait_ge(hT3_ready, back2(n))
                    for q in range(GT):
                        ins = pe.transpose(bank[b][:, q * P:(q + 1) * P], xhat[:, b, q, :], ident[:])
                    ins.then_inc(trans3_ps, 1)
                pe.wait_ge(scan_done, back1(g))
                for b in range(B):
                    n = 2 * g + b
                    pe.wait_ge(hT3_ready, now(n))
                    pe.matmul(bank[2][b * NS:(b + 1) * NS, :], s4_B[:], hT[:, b, :], start=True, stop=True).then_inc(bu_ps, 1)
                for b in range(B):
                    n = 2 * g + b
                    lo, hi = b * NS, (b + 1) * NS
                    pe.wait_ge(scan_done, now(g))
                    pe.wait_ge(xres3_done, back2(n))
                    for q in range(GT):
                        o = bank[4 + b][:, q * P:(q + 1) * P]
                        pe.matmul(o, hT[:, b, q * P:(q + 1) * P], s4_Dg[:, b], start=True, stop=False)
                        ins = pe.matmul(o, s4_x[lo:hi, q * P:(q + 1) * P], s4_Cg[lo:hi], start=False, stop=True)
                    ins.then_inc(s4out_ps, 1)
            for b in range(B):
                ins = pe.matmul(bank[6 + b][:, 0:3 * D], crep[1][:, b, :], wmod[1][:, 3 * D:6 * D], start=True, stop=True)
            ins.then_inc(did("rows_ps"), 1)
            pe.wait_ge(xres3_done, now(2 * NG - 1))
            pe.wait_ge(hT3_ready, now(2 * NG - 1))
            for k in range(NSTEP):
                pe.wait_ge(*upto("cnt_ready", k + 1))
                pe.matmul(bank[0][:, 0:B * NJ], ones[:], cnt[:].rearrange("p b j -> p (b j)"), start=True, stop=True).then_inc(did("cnt_ps"), 1)
            pe.wait_ge(*upto("gteq_ready", 1))
            w_ = 2 * B * NT
            pe.matmul(bank[0][:, 0:w_], ones[:], gteq[:].rearrange("p k b c -> p (k b c)"), start=True, stop=True)
            pe.matmul(bank[0][:, w_:w_ + B * NT], upper[:], gteq[:, 1].rearrange("p b c -> p (b c)"), start=True, stop=True).then_inc(did("gteq_ps"), 1)
            pe.wait_ge(*upto("sel_ready", 1))
            sf = sel[:].rearrange("p b c -> p (b c)")
            pe.matmul(bank[0][:, 0:B * NT], ones[:], sf, start=True, stop=True)
            pe.matmul(bank[0][:, B * NT:2 * B * NT], upper[:], sf, start=True, stop=True).then_inc(did("sel_ps"), 1)
            pe.wait_ge(*upto("choose_ready", 1))
            for s_ in range(NS4):
                b, k = s_ // NSEL, s_ % NSEL
                for c in range(NT):
                    ins = pe.matmul(bank[1][:, 2 * s_:2 * s_ + 2], choose[:, b, c, k * P:(k + 1) * P], tokid[:, c, :], start=c == 0, stop=c == NT - 1)
            ins.then_inc(did("picks_ps"), 1)
            pe.wait_ge(*upto("gidx_ready", 1))
            for b in range(B):
                for k in range(NSEL):
                    j = b * NSEL + k
                    ins = pe.matmul(bank[6 + b][:, k * P:(k + 1) * P], cidx[:, j:j + 1].to_broadcast([P, P]), ident[:], start=True, stop=True)
                ins.then_inc(did("cidx_ps"), 1)
            pe.wait_ge(*upto("hn_ready", 1))
            for s_ in range(NS4):
                ins = pe.transpose(bank[0][:, s_ * P:(s_ + 1) * P], hn[:, s_], ident[:])
            ins.then_inc(did("hnT_ps"), 1)
            pe.wait_ge(*upto("hnT_ready", 1))
            pe.wait_ge(once("l1_loaded"), L1_ALL)
            for s_ in range(NS4):
                pe.matmul(bank[1 + s_][:, 0:3 * D], hnT[:, s_ * P:(s_ + 1) * P], wqkv[:], start=True, stop=True).then_inc(did("qkv_ps"), 1)
            pe.wait_ge(once("smask_loaded"), 16 * NS4)
            for i in range(NS4 + 1):
                if i < NS4:
                    if i >= 2:
                        pe.wait_ge(*upto("maskT_ready", i - 1))
                    for k in range(ML // P):
                        ins = pe.transpose(bank[5 * (1 - i % 2)][:, k * P:(k + 1) * P], smask[:, i, k * P:(k + 1) * P], ident[:])
                    ins.then_inc(did("maskT_ps"), 1)
                if i > 0:
                    pe.wait_ge(*upto("maskT_ready", i))
                    pe.wait_ge(*upto("qk_ready", i))
                    pe.wait_ge(*upto("colsel_ready", (i - 1) // NSEL + 1))
                    for k in range(ML // P):
                        ins = pe.matmul(bank[i][:, 0:TOPK], maskT[:, (i - 1) % 2, k, :], colsel[:, (i - 1) // NSEL, k, :], start=k == 0, stop=k == ML // P - 1)
                    ins.then_inc(did("msel_ps"), 1)
            pe.wait_ge(*upto("rope_ready", NS4))
            pe.wait_ge(*upto("maskT_ready", NS4))
            for j in range(2):
                for s_ in range(NS4):
                    ins = pe.transpose(bank[5 + j][:, s_ * P:(s_ + 1) * P], qk[:, s_, j * D:(j + 1) * D], ident[:])
            ins.then_inc(did("qT_ps"), 1)
            pe.wait_ge(*upto("qkT_ready", 1))
            pe.wait_ge(*upto("msel_ready", 1))
            for m in range(NM + LAG_O):
                if m < NM:
                    i, p = m // PAIRS, m % PAIRS
                    b = i // NSEL
                    pe.wait_ge(kTm_ready, b * PAIRS + p + 1)
                    if m >= 2:
                        pe.wait_ge(*upto("masked_ready", m - 1))
                    pe.matmul(bank[5 + m % 2][:], qT[:, i * P:(i + 1) * P], kTm[:, b, 2 * p:2 * p + 2, :].rearrange("p h k -> p (h k)"),
                              start=True, stop=True).then_inc(did("score_ps"), 1)
                t = m - LAG_T
                if 0 <= t < NM:
                    pe.wait_ge(*upto("exp_ready", t + 1))
                    if t >= 2:
                        pe.wait_ge(*upto("pT_ready", t - 1))
                    for j in range(2 * NSEL):
                        h, kh = j // NSEL, j % NSEL
                        ins = pe.transpose(bank[2 + t % 2][:, j * P:(j + 1) * P], sc[:, t % SC_SLOTS, h, kh * P:(kh + 1) * P], ident[:])
                    ins.then_inc(did("pT_ps"), 1)
                v = m - LAG_V
                if 0 <= v < NM:
                    i, p = v // PAIRS, v % PAIRS
                    pe.wait_ge(*upto("pT_ready", v + 1))
                    if p == 0 and i >= 2:
                        pe.wait_ge(*upto("on_ready", i - 1))
                    for j in range(2 * NSEL):
                        h, kh = 2 * p + j // NSEL, j % NSEL
                        ins = pe.matmul(bank[i % 2][:, h * AD:(h + 1) * AD], pT[:, v % SC_SLOTS, j, :], vv[:, i // NSEL * NSEL + kh, h * AD:(h + 1) * AD],
                                        start=kh == 0, stop=kh == NSEL - 1)
                    ins.then_inc(did("pv_ps"), 1)
            pe.wait_ge(*upto("on_ready", NS4))
            for s_ in range(NS4):
                ins = pe.transpose(bank[0][:, s_ * P:(s_ + 1) * P], on[:, s_], ident[:])
            ins.then_inc(did("onT_ps"), 1)
            pe.wait_ge(*upto("onT_ready", 1))
            for s_ in range(NS4):
                ins = pe.matmul(bank[1][:, s_ * D:(s_ + 1) * D], onT[:, s_ * P:(s_ + 1) * P], wo[:], start=True, stop=True)
            ins.then_inc(did("wo_ps"), 1)
            pe.wait_ge(*upto("hn_ready", 2))
            for s_ in range(NS4):
                ins = pe.transpose(bank[0][:, s_ * P:(s_ + 1) * P], hn[:, s_], ident[:])
            ins.then_inc(did("hnT_ps"), 1)
            pe.wait_ge(*upto("hnT_ready", 2))
            for k in range(FF // P):
                pe.matmul(bank[1 + k][:], w1[:, k * P:(k + 1) * P], hnT[:], start=True, stop=True).then_inc(did("hid_ps"), 1)
            pe.wait_ge(*upto("gelu_ready", FF // P))
            for s_ in range(NS4):
                for k in range(FF // P):
                    ins = pe.matmul(bank[5][:, s_ * D:(s_ + 1) * D], hid1[:, k, s_ * P:(s_ + 1) * P], w2[:, k, :], start=k == 0, stop=k == FF // P - 1)
            ins.then_inc(did("w2_ps"), 1)


_INS = ["L0_attn_x", "L0_attn_Wz", "L0_attn_Win", "L0_attn_Wzg", "L0_attn_Wout", "L0_attn_dt_bias", "L0_attn_A_log",
        "L0_attn_D_param", "L0_wmod", "L1_wmod", "L1_attn_Lambda", "L1_attn_log_dt", "L1_attn_D",
        "L1_ffn_attention_mask", "L1_ffn_position_ids", "L1_ffn_router_w", "L1_ffn_router_b", "L1_ffn_wq", "L1_ffn_wk",
        "L1_ffn_wv", "L1_ffn_wo", "L1_ffn_w1", "L1_ffn_w2", "L1_ffn_ln1", "L1_ffn_ln2"]
_TRANSPOSED = {"L0_cT": "L0_c", "L1_cT": "L1_c", "upT": "L0_ffn_up", "gateT": "L0_ffn_gate", "downT": "L0_ffn_down",
               "routerT": "L0_ffn_router", "up_sT": "L0_ffn_w_up_s", "gate_sT": "L0_ffn_w_gate_s",
               "down_sT": "L0_ffn_w_down_s", "s4_BT": "L1_attn_B", "s4_CT": "L1_attn_C"}


def kernel(**inputs):
    import concourse.bacc as bacc
    from concourse.bass_utils import run_bass_kernel_spmd

    nc = bacc.Bacc("TRN2", target_bir_lowering=False, num_devices=1)
    arrays = {n: np.ascontiguousarray(inputs[n]) for n in _INS}
    for n, src in _TRANSPOSED.items():
        arrays[n] = np.ascontiguousarray(np.swapaxes(np.asarray(inputs[src]), -1, -2))
    io = {n: nc.dram_tensor(f"in_{n}", a.shape, mybir.dt.from_np(a.dtype), kind="ExternalInput").ap() for n, a in arrays.items()}
    out = nc.dram_tensor("out_0", (B, T, D), F32, kind="ExternalOutput").ap()
    build(nc, io, out)
    r = run_bass_kernel_spmd(nc, [{f"in_{n}": a for n, a in arrays.items()}], core_ids=[0])
    return r.results[0]["out_0"]
```

```python
from contextlib import ExitStack

import numpy as np

import concourse.bass as bass
from concourse import mybir
from concourse.alu_op_type import AluOpType as ALU

ACT = mybir.ActivationFunctionType
AX = mybir.AxisListType
F32 = mybir.dt.float32
BF16 = mybir.dt.bfloat16
I32 = mybir.dt.int32

P = 128
B = 2
T = 2048
D = 128
NT = T // P
GT = 4
NG = NT // GT
GW = GT * P
H = 8
HD = 64
NS = 64
DI = H * HD
ZW = 2 * D
EX = 8
HID = 256
NSORT = (B * T + EX * (P - 1)) // P
SLOTS = 3
LN_EPS = 1e-5
RMS_EPS = 1e-6
AH = 16
AD = D // AH
FF = 512
ML = 512
TOPK = T // 8
SEL = TOPK - 1
NSEL = TOPK // P
ROPE_BASE = 10000.0


class Chain:

    def __init__(self, eng, sem):
        self.eng, self.sem, self.base, self.k = eng, sem, 0, 0

    def link(self, ins):
        self.k += 1
        ins.then_inc(self.sem, 1)
        self.eng.wait_ge(self.sem, self.base + self.k)

    def loop(self, count, per, first=0):
        outer = self.base + self.k
        with self.eng.Fori(first, count) as i:
            self.base, self.k = (i - first) * per + outer, 0
            yield i, self.link
            assert self.k == per, f"{self.k} links in a loop of {per}"
        self.base, self.k = outer + (count - first) * per, 0


def build(nc, io, out):
    ctx = ExitStack()
    with ctx:
        def sb(name, shape, dt=F32):
            return ctx.enter_context(nc.sbuf_tensor(name, shape, dt))

        def sem(name):
            return ctx.enter_context(nc.semaphore(name))

        bank = [ctx.enter_context(nc.psum_tensor(f"bank{i}", [P, 512], F32)) for i in range(8)]

        xs = sb("xs", [P, B, NT, D])
        stats = sb("stats", [P, B * NT, 6])
        mean = sb("mean", [P, B * NT])
        var = sb("var", [P, B * NT])
        std = sb("std", [P, B * NT])
        rstd = sb("rstd", [P, B * NT])
        tmp_ln = sb("tmp_ln", [P, B * NT])
        xhat = sb("xhat", [P, B, GT, D])
        hT = sb("hT", [P, B, GW])

        ident = sb("ident", [P, P])
        upper = sb("upper", [P, P])
        lower = sb("lower", [P, P])
        ones = sb("ones", [P, P])
        eps_ln = sb("eps_ln", [P, 1])

        cT = [sb(f"cT{l}", [P, B]) for l in range(2)]
        cE = [sb(f"cE{l}", [P, B]) for l in range(2)]
        cS = [sb(f"cS{l}", [P, B]) for l in range(2)]
        wmod = [sb(f"wmod{l}", [P, 6 * D]) for l in range(2)]
        modT = [sb(f"modT{l}", [P, 6, B]) for l in range(2)]

        gabc = [sb(f"gabc{l}", [P, B, D]) for l in range(2)]
        crep = [sb(f"crep{l}", [P, B, P]) for l in range(2)]
        gt0 = sb("gt0", [P, B, D])
        gt1 = sb("gt1", [P, B, D])

        wrouter = sb("wrouter", [P, EX])
        keep, ssd_mem = sb, ctx.enter_context(ExitStack())

        def sb(name, shape, dt=F32):
            return ssd_mem.enter_context(nc.sbuf_tensor(name, shape, dt))

        wz = sb("wz", [P, ZW])
        win = sb("win", [P, 2 * NS + H + DI])
        wbdt = sb("wbdt", [P, NS + H])
        wzg = sb("wzg", [P, 2, DI])
        wout = sb("wout", [P, 4, D])
        woutg = sb("woutg", [P, B, 4, D])
        dtb = sb("dtb", [P, H])
        alog = sb("alog", [P, H])
        expa = sb("expa", [P, H])
        dpar = sb("dpar", [P, H])

        PK_H, PK_S, PK_B = 0, P, P + 2 * P
        PKW = P + 2 * P + NS
        pk = sb("pk", [P, B, NT, PKW])
        bcT = sb("bcT", [P, NT, 2, P])
        pk_slot = sb("pk_slot", [P, B, PKW])
        bc_slot = sb("bc_slot", [P, 2, P])

        TH = B * NT * H
        dts = sb("dts", [P, B, NT, H])
        v_ = sb("v_", [P, TH])
        e_ = sb("e_", [P, TH])
        u_ = sb("u_", [P, TH])
        l_ = sb("l_", [P, TH])
        r_ = sb("r_", [P, TH])
        delta = sb("delta", [P, B, NT, H])
        a_dec = sb("a_dec", [P, B, NT, H])
        e_cum = sb("e_cum", [P, B, NT, H])
        e_rest = sb("e_rest", [P, B, NT, H])
        dw = sb("dw", [P, B, NT, H])
        e_all = sb("e_all", [P, NT, H])

        seg_rhs = sb("seg_rhs", [P, B, H, P])
        E = sb("E", [P, B, H, P])
        M = sb("M", [P, B, H, P])
        Gm = sb("Gm", [P, B, P])
        dX = sb("dX", [P, B, DI])
        dXw = sb("dXw", [P, B, DI])
        Xsb = sb("Xsb", [P, B, DI])
        XD = sb("XD", [P, B, DI])
        yoff = sb("yoff", [P, B, DI])
        ysum = sb("ysum", [P, B, DI])
        y2 = sb("y2", [P, B, DI])
        yg = sb("yg", [P, B, DI])
        ygT = sb("ygT", [P, B, 4, P])
        S = sb("S", [P, DI])
        Sd = sb("Sd", [P, DI])

        ssd_mem.close()
        sb = keep

        s4_B = sb("s4_B", [P, NS])
        s4_C = sb("s4_C", [P, D])
        s4_Cg = sb("s4_Cg", [P, D])
        s4_lam = sb("s4_lam", [P, 1])
        s4_ldt = sb("s4_ldt", [P, 1])
        s4_D = sb("s4_D", [P, 1])
        s4_a = sb("s4_a", [P, 1])
        s4_abc = sb("s4_abc", [P, GW])
        s4_Dg = sb("s4_Dg", [P, B, D])
        s4_x = sb("s4_x", [P, GW])
        s4_carry = sb("s4_carry", [P, 1])

        NJ = 15
        NSTEP = 8
        NS4 = B * NSEL
        rows = sb("rows", [P, B, 3, D])
        nbias = sb("nbias", [P, B * NT])
        hT_s4 = [hT, sb("hT_odd", [P, B, GW])]
        w_all = sb("w_all", [P, B, NT])
        rw_col = sb("rw_col", [P, 1])
        rb_col = sb("rb_col", [P, 1])
        ln_row = sb("ln_row", [P, 2, D])
        wqkv = sb("wqkv", [P, 3 * D])
        wo = sb("wo", [P, D])
        w1 = sb("w1", [P, FF])
        w2 = sb("w2", [P, FF // P, D])
        jt = sb("jt", [P, NJ], I32)
        scan_ones = sb("scan_ones", [P, NT])
        iota256 = sb("iota256", [P, TOPK], BF16)
        tokid = sb("tokid", [P, NT, 2], BF16)
        inv = sb("inv", [P, AD // 2])
        eps_rms = sb("eps_rms", [P, 1])
        headmask = sb("headmask", [P, AH])
        iotap = sb("iotap", [P, ML // P])

        moe_mem = ctx.enter_context(ExitStack())

        def sb(name, shape, dt=F32):
            return moe_mem.enter_context(nc.sbuf_tensor(name, shape, dt))

        ROW = D + 1
        wgu = sb("wgu", [P, EX, 2 * HID])
        wdown = sb("wdown", [P, EX, HID // P, D])
        wgu_s = sb("wgu_s", [P, 2 * HID])
        wdown_s = sb("wdown_s", [P, HID // P, D])
        wdown_g = sb("wdown_g", [P, B, HID // P, D])
        rows0 = sb("rows0", [P, B, 3, D])
        h_all = sb("h_all", [P, B, NT, ROW])
        hT_all = sb("hT_all", [P, B, T])
        eighths = sb("eighths", [P, EX])
        lmax = sb("lmax", [P, B * NT])
        onehot = sb("onehot", [P, B * NT, EX])
        in_tile = sb("in_tile", [P, B * NT, EX])
        tile_tot = sb("tile_tot", [P, EX, B * NT])
        keep_cum = sb("keep_cum", [P, EX, B * NT])
        tile_cum = sb("tile_cum", [P, EX, B * NT])
        need_i = sb("need_i", [P, EX], I32)
        need = sb("need", [P, EX])
        ends = sb("ends", [P, EX])
        starts = sb("starts", [P, EX])
        place = sb("place", [P, B * NT, EX])
        place_f = sb("place_f", [P, B * NT])
        place_i = sb("place_i", [P, B * NT], I32)
        tile_no = sb("tile_no", [P, NSORT + SLOTS])
        past = sb("past", [P, NSORT + SLOTS, EX])
        expert_f = sb("expert_f", [P, NSORT + SLOTS])
        expert_i = sb("expert_i", [P, NSORT // SLOTS + 1, 4], I32)
        fill = sb("fill", [P, NSORT, ROW])
        spare = sb("spare", [P, SLOTS], I32)
        sg = sb("sg", [P, B, HID // P, GW])
        hid = sb("hid", [P, B, HID // P, GW])
        hs = sb("hs", [P, SLOTS, D])
        token_no = sb("token_no", [P, SLOTS], I32)
        hsT = sb("hsT", [P, SLOTS, P])
        sgs = sb("sgs", [P, SLOTS, HID])
        hids = sb("hids", [P, SLOTS, HID])
        hidsT = sb("hidsT", [P, SLOTS, HID])
        ys = sb("ys", [P, SLOTS, D])
        yx = sb("yx", [P, B, NT, D])

        moe_mem.close()
        sb = keep
        h4 = sb("h4", [P, B, GT, D])
        dflt = sb("dflt", [P, B, GT, D])
        J = sb("J", [P, NSTEP, NJ], I32)
        pre = sb("pre", [P, B], I32)
        digit = sb("digit", [P, B], I32)
        candt = sb("candt", [P, NJ], I32)
        candf = sb("candf", [P, B, NJ], I32)
        cmp_ = sb("cmp_", [P, B, NJ, NT])
        cnt = sb("cnt", [P, B, NJ])
        ge256 = sb("ge256", [P, B, NJ])
        thr_t = sb("thr_t", [P, B], I32)
        thr = sb("thr", [P, B], I32)
        gteq = sb("gteq", [P, 2, B, NT])
        tot = sb("tot", [P, 3, B, NT])
        incl = sb("incl", [P, 2, B, NT])
        ngt = sb("ngt", [P, B])
        sel = sb("sel", [P, B, NT])
        pos = sb("pos", [P, B, NT])
        C_POOL = NT * 5 // 8
        choose = sb("choose", [P, B, NT, TOPK], BF16)
        picks = sb("picks", [P, NS4, 2])
        idx = sb("idx", [P, NS4])
        cidx = sb("cidx", [P, NS4])
        gidx = sb("gidx", [P, 2, NS4], I32)
        sx = sb("sx", [P, NS4, 2 * D + 1])
        smask = sb("smask", [P, NS4, ML])
        spos = sb("spos", [P, NS4], I32)
        ang = sb("ang", [P, 2, NS4, AD // 2])
        angk = sb("angk", [P, 2, NS4, AD // 2])
        angi = sb("angi", [P, 2, NS4, AD // 2], I32)
        sc_ = sb("sc_", [P, 2, NS4, AD // 2])
        ss = sb("ss", [P, NS4])
        sroot = sb("sroot", [P, NS4])
        srr = sb("srr", [P, NS4])
        st = sb("st", [P, NS4])
        squares = sb("squares", [P, NS4, D])
        hn = sb("hn", [P, NS4, D])
        hnT = sb("hnT", [P, NS4 * P])
        qk = sb("qk", [P, NS4, 2 * D])
        qks = sb("qks", [P, 2, 2 * D])
        qkc = sb("qkc", [P, 2, 2 * D])
        vv = sb("vv", [P, NS4, D])
        qT = sb("qT", [P, NS4 * P])
        kT = sb("kT", [P, NS4 * P])
        kTm = sb("kTm", [P, B, AH, TOPK])
        colsel = sb("colsel", [P, B, ML // P, TOPK])
        msel = sb("msel", [P, NS4, TOPK])
        SC_SLOTS = 4
        sc = sb("sc", [P, SC_SLOTS, 2, TOPK])
        smax = sb("smax", [P, NS4, AH])
        ssum = sb("ssum", [P, NS4, AH])
        sinv = sb("sinv", [P, 2, AH])
        pT = sb("pT", [P, SC_SLOTS, 2 * NSEL, P])
        on = sb("on", [P, NS4, D])
        onT = sb("onT", [P, NS4 * P])
        x1 = sb("x1", [P, NS4, D])
        hid1 = sb("hid1", [P, FF // P, NS4 * P])
        gw = sb("gw", [P, NS4, D])
        rest = sb("rest", [P, NS4, D])
        warm = sb("warm", [P, 1])
        notsel = sb("notsel", [P, NS4])
        res = sb("res", [P, NS4, D])

        TE = B * NT * EX
        assert 2 * TE <= 512
        assert NSORT % SLOTS == 0
        hs_dram = nc.dram_tensor("sorted_scratch", ((NSORT + SLOTS) * P, ROW), F32, kind="Internal").ap()
        ys_dram = nc.dram_tensor("expert_scratch", (B * T + (NSORT + SLOTS) * P, D), F32, kind="Internal").ap()
        hx_dram = nc.dram_tensor("hx_scratch", (B * T, 2 * D + 1), F32, kind="Internal").ap()

        def now(n):
            return n + 4

        def back1(n):
            return n + 3

        def back2(n):
            return n + 2

        def back3(n):
            return n + 1

        own = {}

        def handoff(engine, *names):
            got = [sem(x) for x in names]
            own.setdefault(engine, []).extend(got)
            return got

        def credit(eng, engine):
            for s_ in own.get(engine, []):
                eng.sem_inc(s_, 3)

        dve_self = sem("dve_self")
        pool_self = sem("pool_self")
        pool_awake = sem("pool_awake")
        mod_loaded = sem("mod_loaded")
        c_loaded = sem("c_loaded")
        x_loaded = [sem(f"x_loaded{i}") for i in range(2)]
        w_loaded = sem("w_loaded")
        consts_ready = sem("consts_ready")
        c_exp = sem("c_exp")
        c_silu = sem("c_silu")
        mod_ps = sem("mod_ps")
        mod_ready = sem("mod_ready")
        ga_ps = sem("ga_ps")
        ga_done = sem("ga_done")
        wbdt_ready = sem("wbdt_ready")
        var_ready = sem("var_ready")
        std_ready = sem("std_ready")
        (xhat_ready, hT_ready, bc_kept, tok_kept) = handoff("dve", "xhat_ready", "hT_ready", "bc_kept", "tok_kept")
        (trans_ps, z_ps, bc_ps, tok_ps) = handoff("pe", "trans_ps", "z_ps", "bc_ps", "tok_ps")
        (z_kept,) = handoff("act", "z_kept")
        (hT_kept,) = handoff("pool", "hT_kept")
        v_abs = sem("v_abs")
        e_exp = sem("e_exp")
        u_ready = sem("u_ready")
        ln_ready = sem("ln_ready")
        a_ready = sem("a_ready")
        cum_ps = sem("cum_ps")
        decays_ready = sem("decays_ready")
        dw_ready = sem("dw_ready")
        pk_loaded = [sem(f"pk_loaded{b}") for b in range(B)]
        (g_ps, segA_ps, segB_ps, x_ps, zg_ps, off_ps, diag_ps, ds_ps, yT_ps, out_ps) = handoff(
            "pe", "g_ps", "segA_ps", "segB_ps", "x_ps", "zg_ps", "off_ps", "diag_ps", "ds_ps", "yT_ps", "out_ps")
        (gm_done, dx_done, yoff_done, m_ready, y2_done, yg_done, s_upd, xres_done) = handoff(
            "dve", "gm_done", "dx_done", "yoff_done", "m_ready", "y2_done", "yg_done", "s_upd", "xres_done")
        (expA_done, expB_done, xsb_done, ygT_done) = handoff("act", "expA_done", "expB_done", "xsb_done", "ygT_done")
        (segrhs_ready, xd_ready, ysum_ready) = handoff("pool", "segrhs_ready", "xd_ready", "ysum_ready")
        moe_loaded = sem("moe_loaded")
        s4_loaded = sem("s4_loaded")
        moe_consts = sem("moe_consts")
        (xhat2_ready, hid_ready, xres2_done, hids_ready, yx_added) = handoff(
            "dve", "xhat2_ready", "hid_ready", "xres2_done", "hids_ready", "yx_added")
        (trans2_ps, gate_ps, up_ps, down_ps, hsT_ps, gu_ps, hidsT_ps, ys_ps) = handoff(
            "pe", "trans2_ps", "gate_ps", "up_ps", "down_ps", "hsT_ps", "gu_ps", "hidsT_ps", "ys_ps")
        (hT2_ready, silu_done, silus_done, hidsT_ready, ys_ready) = handoff(
            "act", "hT2_ready", "silu_done", "silus_done", "hidsT_ready", "ys_ready")
        (hsT_ready,) = handoff("dve", "hsT_ready")
        (scaled2_ready, h2_ready, yg_ready) = handoff("pool", "scaled2_ready", "h2_ready", "yg_ready")
        numbers_loaded = [sem(f"numbers_loaded{i}") for i in range(SLOTS)]
        hs_loaded = [sem(f"hs_loaded{i}") for i in range(SLOTS)]
        yx_loaded = [sem(f"yx_loaded{b}") for b in range(2)]
        ys_stored = [sem(f"ys_stored{i}") for i in range(SLOTS)]
        s4_exp1 = sem("s4_exp1")
        s4_prod = sem("s4_prod")
        s4_exp2 = sem("s4_exp2")
        s4_ready = sem("s4_ready")
        (scan_done, xres3_done) = handoff("dve", "scan_done", "xres3_done")
        (trans3_ps, bu_ps, s4out_ps) = handoff("pe", "trans3_ps", "bu_ps", "s4out_ps")
        (xhat3_ready, hT3_ready) = handoff("act", "xhat3_ready", "hT3_ready")

        (h4_ready,) = handoff("dve", "h4_ready")
        (trans4_ps,) = handoff("pe", "trans4_ps")
        (xhat4_ready, hT4_ready) = handoff("act", "xhat4_ready", "hT4_ready")
        (hg_ready, dflt_ready) = handoff("pool", "hg_ready", "dflt_ready")
        hx_stored = [sem(f"hx_stored{b}") for b in range(B)]
        dflt_stored = [sem(f"dflt_stored{b}") for b in range(B)]
        single = {}

        def once(name):
            if name not in single:
                single[name] = sem(name)
            return single[name]

        PAIRS = AH // 2
        NM = NS4 * PAIRS
        KT_DVE = 2
        LAG_T, LAG_V, LAG_O = 2, 3, 4
        MASK_STEPS = [2 * i - 1 for i in range(1, NS4)]

        def attention(*steps):
            return [name for m in range(NM + LAG_O) for name, lag in steps if 0 <= m - lag < NM]

        def mask_bank(i):
            return bank[4 + 3 * (i % 2)][:, 0:TOPK]

        def attention_pe():
            names = []
            for m in range(NM + LAG_O):
                names += [name for name, lag in (("score_ps", 0), ("pT_ps", LAG_T), ("pv_ps", LAG_V)) if 0 <= m - lag < NM]
                names += ["msel_ps"] if m in MASK_STEPS else []
            return names

        def attention_dve():
            names = []
            for m in range(NM + LAG_O):
                names += ["masked_ready", "smax_ready"] if m < NM else []
                names += ["on_ready"] if m >= LAG_O and (m - LAG_O) % PAIRS == PAIRS - 1 else []
            return names

        STEPS = {
            "pe": ["rows0_ps", "router_ps", "ranks_ps", "rows_ps"] + 2 * NG * ["w_ps"] + NSTEP * ["cnt_ps"]
                  + ["gteq_ps", "sel_ps", "picks_ps"] + B * ["cidx_ps"]
                  + ["hnT_ps"] + NS4 * ["qkv_ps"] + NS4 * ["maskT_ps"] + ["msel_ps", "qT_ps"] + attention_pe()
                  + ["onT_ps", "wo_ps", "hnT_ps"] + FF // P * ["hid_ps"] + ["w2_ps"],
            "dve": ["rows0_ready", "onehot_ready", "ranks_kept", "place_ready", "expert_ready"]
                   + ["nbias_ready", "rows_ready", "nbias_ready", "w_ready"] + NSTEP * ["cnt_ready"]
                   + ["gteq_ready", "sel_ready", "pos_ready"] + B * ["choose_ready"] + ["gidx_ready"] + B * ["colsel_ready"]
                   + ["ms_ready", "hn_ready", "ang_ready"] + NS4 * ["rope_ready"]
                   + KT_DVE * ["keys_ready"] + attention_dve() + ["x1_ready", "ms_ready", "hn_ready", "res_ready"],
            "act": ["ss_ready", "sroot_ready", "hnT_ready", "sin_ready"] + NS4 * ["qk_ready"] + NS4 * ["maskT_ready"] + ["qkT_ready"]
                   + attention(("pT_ready", LAG_T), ("exp_ready", 0))
                   + ["onT_ready", "ss_ready", "sroot_ready", "hnT_ready"] + FF // P * ["gelu_ready"],
            "pool": ["l1_consts", "choose_rest"],
        }
        kTm_ready = sem("kTm_ready")
        step_sem = {e: sem(f"{e}_step") for e in STEPS}
        taken = {e: 0 for e in STEPS}

        def did(name):
            e = next(e for e in STEPS if name in STEPS[e])
            assert STEPS[e][taken[e]] == name, f"{e} takes {name}, not {STEPS[e][taken[e]]}"
            taken[e] += 1
            return step_sem[e]

        def upto(name, nth):
            e = next(e for e in STEPS if name in STEPS[e])
            at_ = [i for i, x in enumerate(STEPS[e]) if x == name]
            return step_sem[e], at_[nth - 1] + 1

        block = ctx.enter_context(nc.Block())

        x_t = io["L0_attn_x"].rearrange("b (c p) d -> p b c d", p=P)
        out_t = out.rearrange("b (c p) d -> p b c d", p=P)
        W_ALL = 16 * 8
        MOE_ALL = 16 * 9
        S4_ALL = 16 * 7
        L1_ALL = 16 * 10

        def flat(ap):
            return ap.rearrange("p a d -> p (a d)")

        def at(t, b, c):
            return flat(t[:, b, bass.ds(c, 1), :])

        def per_head(ap):
            return ap.unsqueeze(2).to_broadcast([P, H, HD])

        def heads(ap):
            return ap.rearrange("p (h d) -> p h d", h=H)

        @block.sync
        def _(sp):
            for l in range(2):
                sp.dma_start(cT[l][:], io[f"L{l}_cT"]).then_inc(c_loaded, 16)
            for half in range(2):
                c0 = half * NT // 2
                for b in range(B):
                    sp.dma_start(xs[:, b, c0:c0 + NT // 2, :], x_t[:, b, c0:c0 + NT // 2, :]).then_inc(x_loaded[half], 16)
                sp.dma_start(wmod[half][:], io[f"L{half}_wmod"]).then_inc(mod_loaded, 16)
            sp.dma_start(wz[:], io["L0_attn_Wz"]).then_inc(w_loaded, 16)
            sp.dma_start(win[:], io["L0_attn_Win"]).then_inc(w_loaded, 16)
            sp.dma_start(wzg[:], io["L0_attn_Wzg"].rearrange("(k p) n -> p k n", p=P)).then_inc(w_loaded, 16)
            sp.dma_start(wout[:], io["L0_attn_Wout"].rearrange("(k p) n -> p k n", p=P)).then_inc(w_loaded, 16)
            sp.dma_start(wrouter[:], io["routerT"]).then_inc(w_loaded, 16)
            sp.dma_start(dtb[:], io["L0_attn_dt_bias"].partition_broadcast(P)).then_inc(w_loaded, 16)
            sp.dma_start(alog[:], io["L0_attn_A_log"].partition_broadcast(P)).then_inc(w_loaded, 16)
            sp.dma_start(dpar[:], io["L0_attn_D_param"].partition_broadcast(P)).then_inc(w_loaded, 16)

            sp.wait_ge(hT_kept, now(2 * NG - 1))
            sp.wait_ge(z_kept, now(2 * NG - 1))
            sp.wait_ge(tok_kept, now(2 * NG - 1))
            sp.wait_ge(bc_kept, now(2 * NG - 1))
            with sp.Fori(0, NT) as c:
                for b in range(B):
                    sp.wait_ge(ds_ps, back2(2 * c + b))
                    sp.dma_start(pk_slot[:, b, :], at(pk, b, c)).then_inc(pk_loaded[b], 16)
                    sp.dma_start(bc_slot[b * NS:(b + 1) * NS], bcT[b * NS:(b + 1) * NS, bass.ds(c, 1), :, :].rearrange("p a k t -> p (a k) t")).then_inc(pk_loaded[b], 16)
            sp.wait_ge(out_ps, now(2 * NT - 1))
            sp.wait_ge(xres_done, now(2 * NT - 1))
            for j, src in enumerate(("gate", "up")):
                sp.dma_start(wgu_s[:, j * HID:(j + 1) * HID], io[f"{src}_sT"]).then_inc(moe_loaded, 16)
            sp.dma_start(wdown_s[:], io["down_sT"].rearrange("(k p) c -> p k c", p=P)).then_inc(moe_loaded, 16)
            for j, src in enumerate(("gate", "up")):
                for half in range(2):
                    e0, e1 = half * EX // 2, (half + 1) * EX // 2
                    sp.dma_start(wgu[:, e0:e1, j * HID:(j + 1) * HID], io[f"{src}T"][e0:e1].rearrange("e c h -> c e h")).then_inc(moe_loaded, 16)
            for half in range(2):
                e0, e1 = half * EX // 2, (half + 1) * EX // 2
                sp.dma_start(wdown[:, e0:e1], io["downT"][e0:e1].rearrange("e (k p) c -> p e k c", p=P)).then_inc(moe_loaded, 16)
            sp.wait_ge(moe_consts, 1)
            sp.dma_start(hs_dram[0:NSORT * P].rearrange("(j p) d -> p j d", p=P), fill[:]).then_inc(once("filled"), 16)
            sp.dma_start(hs_dram[NSORT * P:].rearrange("(j p) d -> p j d", p=P), fill[:, 0:SLOTS]).then_inc(once("filled"), 16)
            sp.dma_start(s4_B[:], io["s4_BT"]).then_inc(s4_loaded, 16)
            for b in range(B):
                sp.dma_start(s4_C[b * NS:(b + 1) * NS], io["s4_CT"]).then_inc(s4_loaded, 16)
                sp.dma_start(s4_lam[b * NS:(b + 1) * NS], io["L1_attn_Lambda"].unsqueeze(1)).then_inc(s4_loaded, 16)
            sp.dma_start(s4_ldt[:], io["L1_attn_log_dt"].partition_broadcast(P)).then_inc(s4_loaded, 16)
            sp.dma_start(s4_D[:], io["L1_attn_D"].unsqueeze(1)).then_inc(s4_loaded, 16)
            for j, name in enumerate(("wq", "wk", "wv")):
                sp.dma_start(wqkv[:, j * D:(j + 1) * D], io[f"L1_ffn_{name}"]).then_inc(once("l1_loaded"), 16)
            sp.dma_start(wo[:], io["L1_ffn_wo"]).then_inc(once("l1_loaded"), 16)
            sp.dma_start(w1[:], io["L1_ffn_w1"]).then_inc(once("l1_loaded"), 16)
            sp.dma_start(w2[:], io["L1_ffn_w2"].rearrange("(k p) d -> p k d", p=P)).then_inc(once("l1_loaded"), 16)
            for j in range(2):
                sp.dma_start(ln_row[:, j], io[f"L1_ffn_ln{j + 1}"].partition_broadcast(P)).then_inc(once("l1_loaded"), 16)
            sp.dma_start(rw_col[:], io["L1_ffn_router_w"]).then_inc(once("l1_loaded"), 16)
            sp.dma_start(rb_col[:], io["L1_ffn_router_b"].partition_broadcast(P)).then_inc(once("l1_loaded"), 16)
            sp.wait_ge(once("rows_sorted"), 16 * B * NT)
            hs_t = hs_dram.rearrange("(j p) d -> p j d", p=P)

            def load_tiles(i):
                for s_ in range(SLOTS):
                    n = SLOTS * i + s_
                    sp.wait_ge(hsT_ps, back3(n))
                    sp.dma_start(hs[:, s_, :], flat(hs_t[:, bass.ds(n, 1), 0:D])).then_inc(hs_loaded[s_], 16)

            load_tiles(0)
            with sp.Fori(0, NSORT // SLOTS) as i:
                load_tiles(i + 1)
                for s_ in range(SLOTS):
                    sp.wait_ge(ys_stored[s_], 16 * (i + 1))
                    sp.dma_start(token_no[:, s_:s_ + 1], flat(hs_t[:, bass.ds(SLOTS * i + s_, 1), D:].bitcast(I32)),
                                 allow_slow_non_contiguous=True).then_inc(numbers_loaded[s_], 16)
            for s_ in range(SLOTS):
                sp.wait_ge(ys_stored[s_], 16 * (NSORT // SLOTS + 1))
            ys_t = ys_dram[0:B * T].rearrange("(b c p) d -> p b c d", p=P, b=B)
            for half in range(2):
                c0, c1 = half * NT // 2, (half + 1) * NT // 2
                for b in range(B):
                    sp.dma_start(yx[:, b, c0:c1, :], ys_t[:, b, c0:c1, :]).then_inc(yx_loaded[half], 16)
            hx_t = hx_dram.rearrange("(b c p) d -> p b c d", p=P, b=B)
            with sp.Fori(0, NG) as g:
                for b in range(B):
                    sp.wait_ge(xres3_done, now(2 * g + b))
                    sp.dma_start(hx_t[:, b, bass.ds(g * GT, GT), 0:D], xs[:, b, bass.ds(g * GT, GT), :]).then_inc(once("x_rows_stored"), 16)
            for b in range(B):
                sp.sem_inc(hx_stored[b], 16)
                sp.sem_inc(dflt_stored[b], 16)
            with sp.Fori(0, NG) as g:
                for b in range(B):
                    n = 2 * g + b
                    sp.wait_ge(h4_ready, now(n))
                    sp.dma_start(hx_t[:, b, bass.ds(g * GT, GT), D:2 * D], h4[:, b]).then_inc(hx_stored[b], 16)
                    sp.wait_ge(dflt_ready, now(n))
                    sp.dma_start(out_t[:, b, bass.ds(g * GT, GT), :], dflt[:, b]).then_inc(dflt_stored[b], 16)
            sp.wait_ge(*upto("w_ready", 1))
            for b in range(B):
                sp.dma_start(hx_t[:, b, :, 2 * D], w_all[:, b], allow_slow_non_contiguous=True).then_inc(once("w_stored"), 16)
            for b in range(B):
                sp.wait_ge(dflt_stored[b], 16 * (NG + 1))
            sp.wait_ge(once("rows_scattered"), 16 * NS4)

        @block.gpsimd
        def _(pool):
            credit(pool, "pool")
            ch = Chain(pool, pool_self)
            pool.memset(eps_ln[:], LN_EPS)
            pool.memset(ident[:], 0.0)
            pool.memset(upper[:], 1.0)
            ch.link(pool.memset(lower[:], 1.0))
            pool.affine_select(out=ident[:], in_=ident[:], compare_op=ALU.not_equal, fill=1.0, base=0,
                               pattern=[[-1, P]], channel_multiplier=1)
            pool.affine_select(out=upper[:], in_=upper[:], compare_op=ALU.is_ge, fill=0.0, base=0,
                               pattern=[[1, P]], channel_multiplier=-1)
            pool.affine_select(out=lower[:], in_=lower[:], compare_op=ALU.is_gt, fill=0.0, base=0,
                               pattern=[[-1, P]], channel_multiplier=1)
            pool.memset(S[:], 0.0)
            pool.memset(ones[:], 1.0).then_inc(consts_ready, 1)
            with pool.Fori(0, NG) as g:
                for b in range(B):
                    pool.wait_ge(hT_ready, now(2 * g + b))
                    pool.tensor_copy(pk[:, b, bass.ds(g * GT, GT), PK_H:PK_H + P],
                                     hT[:, b, :].rearrange("p (q t) -> p q t", q=GT)).then_inc(hT_kept, 1)
            pool.wait_ge(a_ready, 1)

            def decay_terms(c, b):
                n = 2 * c + b
                pool.wait_ge(segA_ps, back2(n))
                pool.wait_ge(segB_ps, back2(n))
                pool.tensor_tensor(seg_rhs[:, b], upper[:].unsqueeze(1).to_broadcast([P, H, P]),
                                   at(a_dec, b, c).unsqueeze(2).to_broadcast([P, H, P]), ALU.mult).then_inc(segrhs_ready, 1)

            def skips(c, more):
                for b in range(B):
                    pool.wait_ge(xsb_done, now(2 * c + b))
                    pool.wait_ge(ysum_ready, back2(2 * c + b))
                    pool.tensor_tensor(heads(XD[:, b]), heads(Xsb[:, b]), per_head(dpar[:]), ALU.mult).then_inc(xd_ready, 1)
                    if more:
                        decay_terms(c + 1, b)
                for b in range(B):
                    n = 2 * c + b
                    pool.wait_ge(xd_ready, now(n))
                    pool.wait_ge(yoff_done, now(n))
                    pool.wait_ge(y2_done, back2(n))
                    pool.tensor_tensor(ysum[:, b], yoff[:, b], XD[:, b], ALU.add).then_inc(ysum_ready, 1)

            for b in range(B):
                decay_terms(0, b)
            with pool.Fori(0, NT - 1) as c:
                skips(c, True)
            skips(NT - 1, False)
            pool.wait_ge(out_ps, now(2 * NT - 1))
            pool.wait_ge(xres_done, now(2 * NT - 1))
            pool.iota(eighths[:], pattern=[[-1, EX]], base=EX, channel_multiplier=0, allow_small_or_imprecise_dtypes=True)
            pool.iota(tile_no[:], pattern=[[1, NSORT + SLOTS]], base=0, channel_multiplier=0, allow_small_or_imprecise_dtypes=True)
            ch.link(pool.memset(keep_cum[:], 1.0))
            pool.memset(keep_cum[:, :, 0], 0.0)
            pool.iota(h_all[:, :, :, D].bitcast(I32), pattern=[[T, B], [P, NT]], base=0, channel_multiplier=1)
            pool.iota(spare[:], pattern=[[P, SLOTS]], base=B * T + NSORT * P, channel_multiplier=1)
            ch.link(pool.memset(fill[:], 0.0))
            pool.iota(fill[:, :, D].bitcast(I32), pattern=[[P, NSORT]], base=B * T, channel_multiplier=1)
            pool.memset(s4_carry[:], 0.0).then_inc(moe_consts, 1)
            pool.wait_ge(*upto("rows0_ready", 1))
            with pool.Fori(0, NG) as g:
                for b in range(B):
                    n = 2 * g + b
                    h_ = h_all[:, b, bass.ds(g * GT, GT), 0:D]
                    pool.wait_ge(trans2_ps, now(n))
                    pool.sem_inc(pool_awake, 1)
                    pool.tensor_tensor(h_, h_, rows0[:, b, 1:2, :].to_broadcast([P, GT, D]), ALU.mult).then_inc(scaled2_ready, 1)
                    pool.wait_ge(scaled2_ready, now(n))
                    pool.sem_inc(pool_awake, 1)
                    pool.tensor_tensor(h_, h_, rows0[:, b, 0:1, :].to_broadcast([P, GT, D]), ALU.add).then_inc(h2_ready, 1)
            for s_ in range(SLOTS):
                pool.indirect_dma_start(out=ys_dram, in_=fill[:, 0, 0:D], in_offset=None,
                                        out_offset=bass.IndirectOffsetOnAxis(ap=spare[:, s_:s_ + 1], axis=0)).then_inc(ys_stored[s_], 16)
            pool.wait_ge(once("filled"), 32)
            pool.wait_ge(*upto("place_ready", 1))
            pool.wait_ge(h2_ready, now(2 * NG - 1))
            for b in range(B):
                for c in range(NT):
                    i = b * NT + c
                    pool.indirect_dma_start(out=hs_dram, in_=h_all[:, b, c, :], in_offset=None,
                                            out_offset=bass.IndirectOffsetOnAxis(ap=place_i[:, i:i + 1], axis=0)).then_inc(once("rows_sorted"), 16)
            with pool.Fori(0, NSORT // SLOTS) as i:
                for s_ in range(SLOTS):
                    n = SLOTS * i + s_
                    pool.wait_ge(numbers_loaded[s_], 16 * (i + 1))
                    pool.wait_ge(ys_ready, now(n))
                    pool.sem_inc(pool_awake, 1)
                    pool.indirect_dma_start(out=ys_dram, in_=ys[:, s_, :], in_offset=None,
                                            out_offset=bass.IndirectOffsetOnAxis(ap=token_no[:, s_:s_ + 1], axis=0)).then_inc(ys_stored[s_], 16)
            for half in range(2):
                pool.wait_ge(yx_loaded[half], 16 * B)
                with pool.Fori(half * NG // 2, (half + 1) * NG // 2) as g:
                    for b in range(B):
                        y_ = yx[:, b, bass.ds(g * GT, GT), :]
                        pool.tensor_tensor(y_, y_, rows0[:, b, 2:3, :].to_broadcast([P, GT, D]), ALU.mult).then_inc(yg_ready, 1)
            pool.iota(jt[:], pattern=[[1, NJ]], base=1, channel_multiplier=0)
            pool.iota(iota256[:], pattern=[[1, TOPK]], base=0, channel_multiplier=0, allow_small_or_imprecise_dtypes=True)
            pool.iota(tokid[:, :, 0], pattern=[[1, NT]], base=0, channel_multiplier=0, allow_small_or_imprecise_dtypes=True)
            pool.iota(tokid[:, :, 1], pattern=[[0, NT]], base=0, channel_multiplier=1, allow_small_or_imprecise_dtypes=True)
            pool.iota(iotap[:], pattern=[[P, ML // P]], base=0, channel_multiplier=1, allow_small_or_imprecise_dtypes=True)
            pool.memset(scan_ones[:], 1.0)
            pool.memset(eps_rms[:], RMS_EPS)
            for i in range(AD // 2):
                pool.memset(inv[:, i:i + 1], float(np.float32(1.0) / np.float32(ROPE_BASE ** (2.0 * i / AD))))
            ch.link(pool.memset(headmask[:], 1.0))
            ch.link(pool.affine_select(out=headmask[:], in_=headmask[:], compare_op=ALU.is_ge, fill=0.0, base=0,
                                       pattern=[[-AD, AH]], channel_multiplier=1))
            pool.affine_select(out=headmask[:], in_=headmask[:], compare_op=ALU.is_ge, fill=0.0, base=AD - 1,
                               pattern=[[AD, AH]], channel_multiplier=-1).then_inc(did("l1_consts"), 1)
            pool.wait_ge(*upto("rows_ready", 1))
            with pool.Fori(0, NG) as g:
                for b in range(B):
                    n = 2 * g + b
                    pool.wait_ge(dflt_stored[b], 16 * (g + 1))
                    pool.wait_ge(h4_ready, now(n))
                    pool.tensor_tensor(dflt[:, b], h4[:, b], rows[:, b, 2:3, :].to_broadcast([P, GT, D]), ALU.mult).then_inc(hg_ready, 1)
                    pool.wait_ge(hg_ready, now(n))
                    pool.sem_inc(pool_awake, 1)
                    pool.tensor_tensor(dflt[:, b], dflt[:, b], xs[:, b, bass.ds(g * GT, GT), :], ALU.add).then_inc(dflt_ready, 1)
            pool.wait_ge(once("x_rows_stored"), 16 * 2 * NG)
            pool.wait_ge(once("w_stored"), 16 * B)
            pool.wait_ge(*upto("pos_ready", 1))
            for c in range(C_POOL, NT):
                ins = pool.tensor_scalar(choose[:, B - 1, c, :], iota256[:], pos[:, B - 1, c:c + 1], None, ALU.is_equal)
            ins.then_inc(did("choose_rest"), 1)
            for b in range(B):
                pool.wait_ge(hx_stored[b], 16 * (NG + 1))
            pool.wait_ge(*upto("gidx_ready", 1))
            mask_t = io["L1_ffn_attention_mask"].rearrange("b a q k -> (b a q) k")
            pos_t = io["L1_ffn_position_ids"].rearrange("b (q a) -> (b q) a", a=1)
            for s_ in range(NS4):
                tok, mrow = gidx[:, 0, s_:s_ + 1], gidx[:, 1, s_:s_ + 1]
                pool.indirect_dma_start(out=sx[:, s_, :], out_offset=None, in_=hx_dram,
                                        in_offset=bass.IndirectOffsetOnAxis(ap=tok, axis=0)).then_inc(once("sx_loaded"), 16)
            for s_ in range(NS4):
                mrow = gidx[:, 1, s_:s_ + 1]
                pool.indirect_dma_start(out=spos[:, s_:s_ + 1], out_offset=None, in_=pos_t,
                                        in_offset=bass.IndirectOffsetOnAxis(ap=mrow, axis=0)).then_inc(once("spos_loaded"), 16)
            for s_ in range(NS4):
                mrow = gidx[:, 1, s_:s_ + 1]
                pool.indirect_dma_start(out=smask[:, s_, :], out_offset=None, in_=mask_t,
                                        in_offset=bass.IndirectOffsetOnAxis(ap=mrow, axis=0)).then_inc(once("smask_loaded"), 16)
            pool.wait_ge(*upto("qkT_ready", 1))
            for b in range(B):
                for h in range(0 if b else 2 * KT_DVE, AH):
                    ins = pool.tensor_scalar(kTm[:, b, h, :], kT[:, b * TOPK:(b + 1) * TOPK], headmask[:, h:h + 1], None, ALU.mult)
                    if h % 2 == 1:
                        ins.then_inc(kTm_ready, 1)
            pool.wait_ge(*upto("res_ready", 1))
            for b in range(B):
                pool.wait_ge(dflt_stored[b], 16 * (NG + 1))
            for s_ in range(NS4):
                m = P if s_ % NSEL < NSEL - 1 else P - (TOPK - SEL)
                pool.indirect_dma_start(out=out.rearrange("b t d -> (b t) d"), in_=res[0:m, s_, :], in_offset=None,
                                        out_offset=bass.IndirectOffsetOnAxis(ap=gidx[0:m, 0, s_:s_ + 1], axis=0)).then_inc(once("rows_scattered"), 16)
            pool.wait_ge(once("rows_scattered"), 16 * NS4)

        @block.scalar
        def _(act):
            credit(act, "act")
            act.wait_ge(c_loaded, 32)
            for l in range(2):
                act.activation(cE[l][:], cT[l][:], ACT.Exp, scale=-1.0).then_inc(c_exp, 1)
            act.wait_ge(var_ready, 1)
            act.wait_ge(consts_ready, 1)
            act.activation(std[:], var[:], ACT.Sqrt, bias=eps_ln[:, 0:1]).then_inc(std_ready, 1)

            with act.Fori(0, NG) as g:
                for b in range(B):
                    act.wait_ge(z_ps, now(2 * g + b))
                    for k in range(2):
                        ins = act.activation(pk[:, b, bass.ds(g * GT, GT), PK_S + k * P:PK_S + (k + 1) * P],
                                             bank[2 + k][:].rearrange("p (q t) -> p q t", q=GT), ACT.Silu)
                    ins.then_inc(z_kept, 1)
            act.wait_ge(v_abs, 1)
            act.wait_ge(w_loaded, W_ALL)
            act.activation(expa[:], alog[:], ACT.Exp)
            act.activation(e_[:], r_[:], ACT.Exp, scale=-1.0).then_inc(e_exp, 1)
            act.wait_ge(u_ready, 1)
            act.activation(l_[:], u_[:], ACT.Ln).then_inc(ln_ready, 1)
            act.wait_ge(cum_ps, 1)
            act.activation(e_cum[:].rearrange("p b c h -> p (b c h)"), bank[0][:, 0:TH], ACT.Exp)
            act.activation(e_rest[:].rearrange("p b c h -> p (b c h)"), bank[1][:, 0:TH], ACT.Exp)
            for b in range(B):
                ins = act.activation(e_all[b * NS:(b + 1) * NS].rearrange("p c h -> p (c h)"),
                                     bank[2][b * NS:(b + 1) * NS, b * TH // B:(b + 1) * TH // B], ACT.Exp)
            ins.then_inc(decays_ready, 1)

            def turned(c, b):
                n = 2 * c + b
                act.wait_ge(yT_ps, now(n))
                act.wait_ge(out_ps, back2(n))
                act.activation(ygT[:, b].rearrange("p k t -> p (k t)"), bank[3 + 4 * b][:], ACT.Copy).then_inc(ygT_done, 1)

            def chunk(c, last):
                for b in range(B):
                    n = 2 * c + b
                    act.wait_ge(segA_ps, now(n))
                    act.wait_ge(m_ready, back2(n))
                    act.activation(E[:, b, 0:4, :].rearrange("p h t -> p (h t)"), bank[0][:], ACT.Exp).then_inc(expA_done, 1)
                    act.wait_ge(segB_ps, now(n))
                    act.activation(E[:, b, 4:8, :].rearrange("p h t -> p (h t)"), bank[1][:], ACT.Exp).then_inc(expB_done, 1)
                    if last and b == 1:
                        turned(c - 1, b)
                    act.wait_ge(x_ps, now(n))
                    act.wait_ge(ysum_ready, back2(n))
                    act.wait_ge(dx_done, back2(n))
                    act.activation(Xsb[:, b], bank[2][:], ACT.Copy).then_inc(xsb_done, 1)
                    if last and b == 0:
                        turned(c - 1, b)

            chunk(0, False)
            with act.Fori(1, NT) as c:
                chunk(c, True)
            for b in range(B):
                turned(NT - 1, b)
            act.wait_ge(var_ready, 2)
            act.activation(std[:], var[:], ACT.Sqrt, bias=eps_ln[:, 0:1]).then_inc(std_ready, 1)
            for g in range(NG):
                for b in range(B):
                    act.wait_ge(trans2_ps, now(2 * g + b))
                    act.activation(hT_all[:, b, g * GW:(g + 1) * GW], bank[b][:], ACT.Identity,
                                   bias=modT[0][:, 3, b:b + 1], scale=modT[0][:, 4, b:b + 1]).then_inc(hT2_ready, 1)
            with act.Fori(0, NG) as g:
                for b in range(B):
                    n = 2 * g + b
                    act.wait_ge(gate_ps, now(n))
                    act.wait_ge(hid_ready, back2(n))
                    for k in range(HID // P):
                        ins = act.activation(sg[:, b, k, :], bank[4 * b + k][:], ACT.Silu)
                    ins.then_inc(silu_done, 1)
            with act.Fori(0, NSORT // SLOTS) as i:
                for s_ in range(SLOTS):
                    n = SLOTS * i + s_
                    act.wait_ge(gu_ps, now(n))
                    act.wait_ge(hids_ready, back3(n))
                    act.activation(sgs[:, s_, :], bank[s_][:, 0:HID], ACT.Silu).then_inc(silus_done, 1)
                for s_ in range(SLOTS):
                    n = SLOTS * i + s_
                    act.wait_ge(hidsT_ps, now(n))
                    act.wait_ge(ys_ps, back3(n))
                    act.activation(hidsT[:, s_, :], bank[3 + s_][:, 0:HID], ACT.Copy).then_inc(hidsT_ready, 1)
                for s_ in range(SLOTS):
                    n = SLOTS * i + s_
                    act.wait_ge(ys_ps, now(n))
                    act.wait_ge(ys_stored[s_], 16 * (i + 1))
                    act.activation(ys[:, s_, :], bank[s_][:, 0:D], ACT.Copy).then_inc(ys_ready, 1)
            act.wait_ge(s4_loaded, S4_ALL)
            act.activation(s4_ldt[:], s4_ldt[:], ACT.Exp)
            act.activation(s4_lam[:], s4_lam[:], ACT.Exp).then_inc(s4_exp1, 1)
            act.wait_ge(s4_prod, 1)
            act.activation(s4_a[:], s4_a[:], ACT.Exp, scale=-1.0).then_inc(s4_exp2, 1)
            act.wait_ge(var_ready, 3)
            act.activation(std[:], var[:], ACT.Sqrt, bias=eps_ln[:, 0:1]).then_inc(std_ready, 1)
            act.wait_ge(*upto("nbias_ready", 1))
            for g in range(NG):
                for b in range(B):
                    n = 2 * g + b
                    if g:
                        act.wait_ge(trans3_ps, now(n - 2))
                    for q in range(GT):
                        i = b * NT + g * GT + q
                        ins = act.activation(xhat[:, b, q, :], xs[:, b, g * GT + q, :], ACT.Identity, bias=nbias[:, i:i + 1], scale=rstd[:, i:i + 1])
                    ins.then_inc(xhat3_ready, 1)
                for b in range(B):
                    n = 2 * g + b
                    act.wait_ge(trans3_ps, now(n))
                    if g >= 2:
                        act.wait_ge(s4out_ps, now(n - 4))
                    act.activation(hT_s4[g % 2][:, b, :], bank[b][:], ACT.Identity, bias=modT[1][:, 0, b:b + 1],
                                   scale=modT[1][:, 1, b:b + 1]).then_inc(hT3_ready, 1)

            act.wait_ge(var_ready, 4)
            act.activation(std[:], var[:], ACT.Sqrt, bias=eps_ln[:, 0:1]).then_inc(std_ready, 1)
            act.wait_ge(*upto("nbias_ready", 2))
            def turned4(n):
                act.wait_ge(trans4_ps, now(n))
                if n >= 2:
                    act.wait_ge(*upto("w_ps", n - 1))
                act.activation(hT[:, n % 2, :], bank[n % 2][:], ACT.Identity, bias=modT[1][:, 3, n % 2:n % 2 + 1],
                               scale=modT[1][:, 4, n % 2:n % 2 + 1]).then_inc(hT4_ready, 1)

            for n in range(2 * NG):
                g, b = n // 2, n % 2
                act.wait_ge(h4_ready, back2(n))
                act.wait_ge(trans4_ps, back2(n))
                for q in range(GT):
                    c = g * GT + q
                    i = b * NT + c
                    ins = act.activation(xhat[:, b, q, :], xs[:, b, c, :], ACT.Identity, bias=nbias[:, i:i + 1], scale=rstd[:, i:i + 1])
                ins.then_inc(xhat4_ready, 1)
                if n:
                    turned4(n - 1)
            turned4(2 * NG - 1)
            act.wait_ge(once("sx_loaded"), 16 * NS4)
            for s_ in range(NS4):
                ins = act.activation(squares[:, s_], sx[:, s_, D:2 * D], ACT.Square, accum_out=ss[:, s_:s_ + 1])
            ins.then_inc(did("ss_ready"), 1)
            act.wait_ge(*upto("ms_ready", 1))
            act.activation(sroot[:], ss[:], ACT.Sqrt).then_inc(did("sroot_ready"), 1)
            act.wait_ge(*upto("hnT_ps", 1))
            act.activation(hnT[:], bank[0][:], ACT.Copy).then_inc(did("hnT_ready"), 1)
            act.wait_ge(*upto("ang_ready", 1))
            act.activation(sc_[:], ang[:], ACT.Sin).then_inc(did("sin_ready"), 1)
            for s_ in range(NS4):
                act.wait_ge(*upto("qkv_ps", s_ + 1))
                act.activation(vv[:, s_], bank[1 + s_][:, 2 * D:3 * D], ACT.Copy)
                act.activation(qk[:, s_], bank[1 + s_][:, 0:2 * D], ACT.Copy).then_inc(did("qk_ready"), 1)
            for i in range(NS4):
                act.wait_ge(*upto("maskT_ps", i + 1))
                act.activation(smask[:, i], bank[5 * (1 - i % 2)][:], ACT.Copy).then_inc(did("maskT_ready"), 1)
            act.wait_ge(*upto("qT_ps", 1))
            act.activation(qT[:], bank[5][:], ACT.Copy, scale=float(1.0 / np.sqrt(AD)))
            act.activation(kT[:], bank[6][:], ACT.Copy).then_inc(did("qkT_ready"), 1)
            for m in range(NM + LAG_O):
                t = m - LAG_T
                if 0 <= t < NM:
                    act.wait_ge(*upto("pT_ps", t + 1))
                    if t >= SC_SLOTS:
                        act.wait_ge(*upto("pv_ps", t - SC_SLOTS + 1))
                    act.activation(pT[:, t % SC_SLOTS].rearrange("p k q -> p (k q)"), bank[2 + t % 2][:], ACT.Copy).then_inc(did("pT_ready"), 1)
                if m < NM:
                    i, p, slot = m // PAIRS, m % PAIRS, m % SC_SLOTS
                    act.wait_ge(*upto("smax_ready", m + 1))
                    for k in range(2):
                        h = 2 * p + k
                        ins = act.activation(sc[:, slot, k], sc[:, slot, k], ACT.Exp, bias=smax[:, i, h:h + 1], accum_out=ssum[:, i, h:h + 1])
                    ins.then_inc(did("exp_ready"), 1)
            act.wait_ge(*upto("onT_ps", 1))
            act.activation(onT[:], bank[0][:], ACT.Copy).then_inc(did("onT_ready"), 1)
            act.activation(warm[:], eps_rms[:], ACT.Sqrt)
            act.wait_ge(*upto("x1_ready", 1))
            for s_ in range(NS4):
                ins = act.activation(squares[:, s_], x1[:, s_], ACT.Square, accum_out=ss[:, s_:s_ + 1])
            ins.then_inc(did("ss_ready"), 1)
            act.wait_ge(*upto("ms_ready", 2))
            act.activation(sroot[:], ss[:], ACT.Sqrt).then_inc(did("sroot_ready"), 1)
            act.activation(warm[:], eps_rms[:], ACT.Gelu_apprx_tanh)
            act.wait_ge(*upto("hnT_ps", 2))
            act.activation(hnT[:], bank[0][:], ACT.Copy).then_inc(did("hnT_ready"), 1)
            for k in range(FF // P):
                act.wait_ge(*upto("hid_ps", k + 1))
                act.activation(hid1[:, k], bank[1 + k][:], ACT.Gelu_apprx_tanh).then_inc(did("gelu_ready"), 1)

        def settled(dve, ch):
            ch.link(dve.tensor_copy(tmp_ln[:, 0:1], ones[:, 0:1]))

        def ln_finish(dve, ch):
            me, mo = stats[:, :, 1], stats[:, :, 4]
            ve, vo = stats[:, :, 2], stats[:, :, 5]
            dve.tensor_tensor(mean[:], me, mo, ALU.add)
            dve.tensor_tensor(tmp_ln[:], me, mo, ALU.subtract)
            ch.link(dve.tensor_tensor(var[:], ve, vo, ALU.add))
            dve.tensor_scalar(mean[:], mean[:], 0.5, None, ALU.mult)
            dve.tensor_scalar(var[:], var[:], 1.0 / D, None, ALU.mult)
            ch.link(dve.scalar_tensor_tensor(out=tmp_ln[:], in0=tmp_ln[:], scalar=0.25, in1=tmp_ln[:],
                                             op0=ALU.mult, op1=ALU.mult))
            dve.tensor_tensor(var[:], var[:], tmp_ln[:], ALU.add).then_inc(var_ready, 1)

        def ln_rstd(dve, ch, n):
            dve.wait_ge(std_ready, n)
            ch.link(dve.reciprocal(rstd[:], std[:]))
            ch.link(dve.tensor_tensor(tmp_ln[:], rstd[:], rstd[:], ALU.mult))
            ch.link(dve.scalar_tensor_tensor(out=tmp_ln[:], in0=var[:], scalar=eps_ln[:, 0:1], in1=tmp_ln[:], op0=ALU.add, op1=ALU.mult))
            ch.link(dve.tensor_scalar(tmp_ln[:], tmp_ln[:], -0.5, 1.5, ALU.mult, ALU.add))
            ch.link(dve.tensor_tensor(rstd[:], rstd[:], tmp_ln[:], ALU.mult))

        def normalise(dve, g, b):
            for q in range(GT):
                i = g * GT + (b * NT + q)
                ins = dve.tensor_scalar(xhat[:, b, q, :], at(xs, b, g * GT + q), mean[:, bass.ds(i, 1)],
                                        rstd[:, bass.ds(i, 1)], ALU.subtract, ALU.mult)
            return ins

        def gate_(dve, ch, m, t0, t1):
            dve.tensor_scalar(t0, m, 0.0, 2.0, ALU.is_ge, ALU.mult)
            ch.link(dve.scalar_tensor_tensor(out=t1, in0=m, scalar=-1.0, in1=m, op0=ALU.mult, op1=ALU.max))
            ch.link(dve.tensor_scalar(t1, t1, 0.25, None, ALU.max))
            ch.link(dve.scalar_tensor_tensor(out=m, in0=t0, scalar=-1.0, in1=t1, op0=ALU.add, op1=ALU.mult))

        def rank_in(ch, dve, k, in_tile):
            for b in range(B):
                ins = dve.tensor_tensor_scan(incl[:, 0, b], scan_ones[:], tot[:, k, b], 0.0, ALU.mult, ALU.add)
            ch.link(ins)
            ch.link(dve.tensor_tensor(incl[:, 1], incl[:, 0], tot[:, k], ALU.subtract))
            ch.link(dve.tensor_tensor(pos[:].rearrange("p b c -> p (b c)"), incl[:, 1].rearrange("p b c -> p (b c)"), in_tile, ALU.add))

        @block.vector
        def _(dve):
            credit(dve, "dve")
            ch = Chain(dve, dve_self)

            def statistics_of_half(half):
                dve.wait_ge(x_loaded[half], 32)
                for b in range(B):
                    for c in range(half * NT // 2, (half + 1) * NT // 2):
                        dve.bn_stats(stats[:, b * NT + c, :], xs[:, b, c, :])

            statistics_of_half(0)
            dve.wait_ge(c_exp, 2)
            for l in range(2):
                ch.link(dve.tensor_scalar(cE[l][:], cE[l][:], 1.0, None, ALU.add))
                ch.link(dve.reciprocal(cE[l][:], cE[l][:]))
                ch.link(dve.tensor_tensor(cS[l][:], cT[l][:], cE[l][:], ALU.mult))
            dve.wait_ge(consts_ready, 1)
            for l in range(2):
                for b in range(B):
                    ins = dve.tensor_scalar(crep[l][:, b, :], ones[:], cS[l][:, b:b + 1], None, ALU.mult)
            ins.then_inc(c_silu, 1)
            statistics_of_half(1)
            settled(dve, ch)
            ln_finish(dve, ch)
            dve.wait_ge(mod_ps, 1)
            for l in range(2):
                ins = dve.tensor_copy(modT[l][:], bank[4 + l][:, 0:12].rearrange("p (j b) -> p j b", b=B))
            ch.link(ins)
            for l in range(2):
                for j in (1, 4):
                    ins = dve.tensor_scalar(modT[l][:, j, :], modT[l][:, j, :], 1.0, None, ALU.add)
            ins.then_inc(mod_ready, 1)
            dve.wait_ge(w_loaded, W_ALL)
            dve.tensor_copy(wbdt[:, 0:NS], win[:, 0:NS])
            dve.tensor_copy(wbdt[:, NS:], win[:, 2 * NS:2 * NS + H]).then_inc(wbdt_ready, 1)
            ln_rstd(dve, ch, 1)

            def modulate(g, b):
                n = 2 * g + b
                dve.wait_ge(trans_ps, now(n))
                dve.wait_ge(hT_kept, back2(n))
                dve.wait_ge(tok_ps, back2(n))
                dve.tensor_scalar(hT[:, b, :], bank[b][:], modT[0][:, 1, b:b + 1], modT[0][:, 0, b:b + 1],
                                  ALU.mult, ALU.add).then_inc(hT_ready, 1)

            def keep_item(g, b):
                n = 2 * g + b
                dve.wait_ge(bc_ps, now(n))
                for k in range(2):
                    ins = dve.tensor_copy(bcT[b * NS:(b + 1) * NS, bass.ds(g * GT, GT), k, :],
                                          bank[4 + k][b * NS:(b + 1) * NS, :].rearrange("p (q t) -> p q t", q=GT))
                ins.then_inc(bc_kept, 1)
                dve.wait_ge(tok_ps, now(n))
                tok = bank[6][:, 0:GT * (NS + H)].rearrange("p (q n) -> p q n", q=GT)
                dve.tensor_copy(pk[:, b, bass.ds(g * GT, GT), PK_B:PK_B + NS], tok[:, :, 0:NS])
                dve.tensor_copy(dts[:, b, bass.ds(g * GT, GT), :], tok[:, :, NS:]).then_inc(tok_kept, 1)

            for b in range(B):
                normalise(dve, 0, b).then_inc(xhat_ready, 1)
            dve.wait_ge(mod_ready, 1)
            modulate(0, 0)
            with dve.Fori(0, NG - 1) as g:
                for b in range(B):
                    modulate(g + b, 1 - b)
                    normalise(dve, g + 1, b).then_inc(xhat_ready, 1)
                    keep_item(g, b)
            modulate(NG - 1, 1)
            for b in range(B):
                keep_item(NG - 1, b)
            def rep(ap):
                return ap.unsqueeze(1).to_broadcast([P, B * NT, H])

            def by8(ap):
                return ap.rearrange("p (i h) -> p i h", h=H)

            fl = "p b c h -> p (b c h)"
            dve.wait_ge(tok_kept, now(2 * NG - 1))
            ch.link(dve.tensor_tensor(by8(v_[:]), by8(dts[:].rearrange(fl)), rep(dtb[:]), ALU.add))
            dve.scalar_tensor_tensor(out=r_[:], in0=v_[:], scalar=-1.0, in1=v_[:], op0=ALU.mult, op1=ALU.max).then_inc(v_abs, 1)
            dve.wait_ge(e_exp, 1)
            dve.tensor_scalar(u_[:], e_[:], 1.0, None, ALU.add).then_inc(u_ready, 1)
            dve.wait_ge(u_ready, 1)
            dve.reciprocal(r_[:], u_[:])
            ch.link(dve.scalar_tensor_tensor(out=e_[:], in0=u_[:], scalar=-1.0, in1=e_[:], op0=ALU.add, op1=ALU.subtract))
            ch.link(dve.tensor_tensor(e_[:], e_[:], r_[:], ALU.mult))
            ch.link(dve.scalar_tensor_tensor(out=v_[:], in0=v_[:], scalar=0.0, in1=e_[:], op0=ALU.max, op1=ALU.subtract))
            dve.wait_ge(ln_ready, 1)
            ch.link(dve.tensor_tensor(delta[:].rearrange(fl), v_[:], l_[:], ALU.add))
            dve.scalar_tensor_tensor(out=by8(a_dec[:].rearrange(fl)), in0=by8(delta[:].rearrange(fl)), scalar=-1.0,
                                     in1=rep(expa[:]), op0=ALU.mult, op1=ALU.mult).then_inc(a_ready, 1)
            dve.wait_ge(ga_ps, 1)
            for l in range(2):
                ch.link(dve.tensor_copy(gabc[l][:], bank[7][:, l * B * P:(l + 1) * B * P].rearrange("p (b d) -> p b d", b=B)))
                gate_(dve, ch, gabc[l][:], gt0[:], gt1[:])
            for b in range(B):
                ins = dve.tensor_tensor(woutg[:, b], wout[:], gabc[0][:, b:b + 1, :].to_broadcast([P, 4, D]), ALU.mult)
            gate_(dve, ch, modT[1][:, 2, :], tmp_ln[:, 0:B], tmp_ln[:, B:2 * B])
            dve.sem_inc(ga_done, 1)
            dve.wait_ge(decays_ready, 1)
            dve.tensor_tensor(dw[:].rearrange(fl), delta[:].rearrange(fl), e_rest[:].rearrange(fl), ALU.mult).then_inc(dw_ready, 1)
            dve.wait_ge(dw_ready, 1)

            def residual(c, b):
                n = 2 * c + b
                dve.wait_ge(out_ps, now(n))
                dve.tensor_tensor(at(xs, b, c), at(xs, b, c), bank[3 + 4 * b][:, 0:P], ALU.add).then_inc(xres_done, 1)

            def statistics(c, b):
                dve.wait_ge(xres_done, now(2 * c + b))
                dve.bn_stats(flat(stats[:, bass.ds(c + b * NT, 1), :]), at(xs, b, c))

            def chunk(c, last, links):
                for b in range(B):
                    n = 2 * c + b
                    dve.wait_ge(xsb_done, now(n))
                    dve.tensor_tensor(heads(dX[:, b]), heads(Xsb[:, b]), per_head(at(delta, b, c)), ALU.mult)
                    dve.tensor_tensor(heads(dXw[:, b]), heads(Xsb[:, b]), per_head(at(dw, b, c)), ALU.mult).then_inc(dx_done, 1)
                    dve.wait_ge(g_ps, now(n))
                    dve.tensor_tensor(Gm[:, b], bank[6][:, 0:P], upper[:], ALU.mult).then_inc(gm_done, 1)
                    if last and b == 1:
                        for b_ in range(B):
                            residual(c - 1, b_)
                    dve.wait_ge(gm_done, now(n))
                    dve.wait_ge(expA_done, now(n))
                    dve.wait_ge(expB_done, now(n))
                    dve.tensor_tensor(M[:, b], Gm[:, b:b + 1, :].to_broadcast([P, H, P]), E[:, b], ALU.mult).then_inc(m_ready, 1)
                for b in range(B):
                    dve.wait_ge(off_ps, now(2 * c + b))
                    dve.tensor_tensor(heads(yoff[:, b]), heads(bank[3 + 4 * b][:]), per_head(at(e_cum, b, c)), ALU.mult).then_inc(yoff_done, 1)
                links(dve.tensor_tensor(heads(Sd[:]), heads(S[:]), per_head(flat(e_all[:, bass.ds(c, 1), :])), ALU.mult))
                for b in range(B):
                    n = 2 * c + b
                    dve.wait_ge(diag_ps, now(n))
                    dve.wait_ge(ysum_ready, now(n))
                    dve.tensor_tensor(y2[:, b], bank[6][:], ysum[:, b], ALU.add).then_inc(y2_done, 1)
                    if b == 0:
                        dve.wait_ge(ds_ps, now(2 * c + 1))
                        dve.tensor_tensor(S[:], Sd[:], bank[2][:], ALU.add).then_inc(s_upd, 1)
                    dve.wait_ge(y2_done, now(n))
                    dve.wait_ge(zg_ps, now(n))
                    dve.tensor_tensor(yg[:, b], y2[:, b], bank[4 + b][:], ALU.mult).then_inc(yg_done, 1)
                if last:
                    for b in range(B):
                        statistics(c - 1, b)

            chunk(0, False, ch.link)
            for (c, links) in ch.loop(NT, 1, first=1):
                chunk(c, True, links)
            for b in range(B):
                residual(NT - 1, b)
            for b in range(B):
                statistics(NT - 1, b)
            settled(dve, ch)
            ln_finish(dve, ch)
            dve.wait_ge(*upto("rows0_ps", 1))
            for b in range(B):
                ins = dve.tensor_copy(rows0[:, b], bank[6 + b][:, 0:3 * D].rearrange("p (j d) -> p j d", j=3))
            ch.link(ins)
            dve.tensor_scalar(rows0[:, :, 1, :], rows0[:, :, 1, :], 1.0, None, ALU.add).then_inc(did("rows0_ready"), 1)
            ln_rstd(dve, ch, 2)
            for g in range(NG):
                for b in range(B):
                    for q in range(GT):
                        c = g * GT + q
                        i = b * NT + c
                        ins = dve.tensor_scalar(h_all[:, b, c, 0:D], xs[:, b, c, :], mean[:, i:i + 1], rstd[:, i:i + 1], ALU.subtract, ALU.mult)
                    ins.then_inc(xhat2_ready, 1)
            gate_(dve, ch, rows0[:, :, 2, :], gt0[:], gt1[:])
            dve.wait_ge(moe_loaded, MOE_ALL)
            for b in range(B):
                ins = dve.tensor_tensor(wdown_g[:, b], wdown_s[:], rows0[:, b, 2:3, :].to_broadcast([P, HID // P, D]), ALU.mult)
            ch.link(ins)
            dve.wait_ge(moe_consts, 1)
            dve.wait_ge(*upto("router_ps", 1))
            logits = bank[2][:, 0:B * NT * EX].rearrange("p (i e) -> p i e", e=EX)

            def experts(ap):
                return ap.unsqueeze(2).to_broadcast([P, B * NT, EX])

            ch.link(dve.tensor_reduce(lmax[:], logits, AX.X, ALU.max))
            ch.link(dve.tensor_tensor(onehot[:], logits, experts(lmax[:]), ALU.is_equal))
            ch.link(dve.tensor_tensor(onehot[:], onehot[:], eighths[:].unsqueeze(1).to_broadcast([P, B * NT, EX]), ALU.mult))
            ch.link(dve.tensor_reduce(lmax[:], onehot[:], AX.X, ALU.max))
            dve.tensor_tensor(onehot[:], onehot[:], experts(lmax[:]), ALU.is_equal).then_inc(did("onehot_ready"), 1)
            def hidden(g, b):
                n = 2 * g + b
                dve.wait_ge(silu_done, now(n))
                dve.wait_ge(up_ps, now(n))
                dve.wait_ge(down_ps, back2(n))
                for k in range(HID // P):
                    ins = dve.tensor_tensor(hid[:, b, k, :], sg[:, b, k, :], bank[4 * b + 2 + k][:], ALU.mult)
                ins.then_inc(hid_ready, 1)

            def residual2(g, b):
                dve.wait_ge(down_ps, now(2 * g + b))
                dve.tensor_tensor(xs[:, b, bass.ds(g * GT, GT), :], xs[:, b, bass.ds(g * GT, GT), :],
                                  bank[4 * b][:].rearrange("p (q d) -> p q d", q=GT), ALU.add).then_inc(xres2_done, 1)

            dve.wait_ge(*upto("ranks_ps", 1))
            dve.tensor_copy(in_tile[:].rearrange("p i e -> p (i e)"), bank[7][:, 0:TE])
            ch.link(dve.tensor_copy(tile_tot[:], bank[7][:, TE:2 * TE].rearrange("p (i e) -> p e i", e=EX)))
            dve.sem_inc(did("ranks_kept"), 1)
            ch.link(dve.tensor_tensor_scan(tile_cum[:].rearrange("p e i -> p (e i)"), keep_cum[:].rearrange("p e i -> p (e i)"),
                                           tile_tot[:].rearrange("p e i -> p (e i)"), 0.0, ALU.mult, ALU.add))
            ch.link(dve.tensor_scalar(need_i[:], tile_cum[:, :, B * NT - 1], float(P - 1), None, ALU.add))
            ch.link(dve.tensor_scalar(need_i[:], need_i[:], 7, None, ALU.arith_shift_right))
            ch.link(dve.tensor_copy(need[:], need_i[:]))
            ch.link(dve.tensor_tensor_scan(ends[:], ones[:, 0:EX], need[:], 0.0, ALU.mult, ALU.add))
            ch.link(dve.tensor_tensor(starts[:], ends[:], need[:], ALU.subtract))
            ch.link(dve.tensor_scalar(starts[:], starts[:], float(P), -1.0, ALU.mult, ALU.add))
            ch.link(dve.tensor_tensor(tile_cum[:], tile_cum[:], tile_tot[:], ALU.subtract))
            ch.link(dve.tensor_tensor(tile_cum[:], tile_cum[:], starts[:].unsqueeze(2).to_broadcast([P, EX, B * NT]), ALU.add))
            ch.link(dve.tensor_tensor(place[:], in_tile[:], tile_cum[:].rearrange("p e i -> p i e"), ALU.add))
            ch.link(dve.tensor_tensor(place[:], place[:], onehot[:], ALU.mult))
            ch.link(dve.tensor_reduce(place_f[:], place[:], AX.X, ALU.add))
            ch.link(dve.tensor_copy(place_i[:], place_f[:]))
            dve.sem_inc(did("place_ready"), 1)
            ch.link(dve.tensor_tensor(past[:], tile_no[:].unsqueeze(2).to_broadcast([P, NSORT + SLOTS, EX]),
                                      ends[:].unsqueeze(1).to_broadcast([P, NSORT + SLOTS, EX]), ALU.is_ge))
            ch.link(dve.tensor_reduce(expert_f[:], past[:], AX.X, ALU.add))
            ch.link(dve.tensor_scalar(expert_i[:, :, 0:SLOTS], expert_f[:].rearrange("p (i s) -> p i s", s=SLOTS), float(EX - 1), None, ALU.min))
            dve.sem_inc(did("expert_ready"), 1)
            for b in range(B):
                hidden(0, b)
            for b in range(B):
                residual2(0, b)
            with dve.Fori(1, NG) as g:
                for b in range(B):
                    hidden(g, b)
                for b in range(B):
                    residual2(g, b)
            def keep_hsT(i):
                dve.wait_ge(hsT_ps, now(SLOTS * i + SLOTS - 1))
                dve.wait_ge(gu_ps, back1(SLOTS * i))
                dve.tensor_copy(hsT[:].rearrange("p s q -> p (s q)"), bank[6][:, 0:SLOTS * P]).then_inc(hsT_ready, 1)

            keep_hsT(0)
            with dve.Fori(0, NSORT // SLOTS) as i:
                for s_ in range(SLOTS):
                    n = SLOTS * i + s_
                    dve.wait_ge(silus_done, now(n))
                    dve.wait_ge(hidsT_ps, back3(n))
                    dve.tensor_tensor(hids[:, s_, :], sgs[:, s_, :], bank[s_][:, HID:], ALU.mult).then_inc(hids_ready, 1)
                keep_hsT(i + 1)
            def y_statistics(n):
                g, b = n // 2, n % 2
                dve.wait_ge(yx_added, now(n))
                for q in range(GT):
                    dve.bn_stats(stats[:, b * NT + g * GT + q, :], xs[:, b, g * GT + q, :])

            for n in range(2 * NG):
                g, b = n // 2, n % 2
                dve.wait_ge(yg_ready, now(n))
                dve.tensor_tensor(xs[:, b, g * GT:(g + 1) * GT, :], xs[:, b, g * GT:(g + 1) * GT, :],
                                  yx[:, b, g * GT:(g + 1) * GT, :], ALU.add).then_inc(yx_added, 1)
                if n:
                    y_statistics(n - 1)
            y_statistics(2 * NG - 1)
            dve.wait_ge(s4_exp1, 1)
            dve.tensor_tensor(s4_a[:], s4_ldt[:], s4_lam[:], ALU.mult).then_inc(s4_prod, 1)
            settled(dve, ch)
            ln_finish(dve, ch)
            dve.wait_ge(s4_exp2, 1)
            for k in range(GT):
                dve.tensor_scalar(s4_abc[:, k * P:(k + 1) * P], ones[:], s4_a[:, 0:1], None, ALU.mult)
            for b in range(B):
                dve.tensor_tensor(s4_Cg[b * NS:(b + 1) * NS], s4_C[b * NS:(b + 1) * NS], gabc[1][b * NS:(b + 1) * NS, b, :], ALU.mult)
                ins = dve.tensor_scalar(s4_Dg[:, b], ident[:], s4_D[:, 0:1], modT[1][:, 2, b:b + 1], ALU.mult, ALU.mult)
            ch.link(ins)
            dve.sem_inc(s4_ready, 1)
            ln_rstd(dve, ch, 3)

            def negate_bias():
                ch.link(dve.tensor_tensor(nbias[:], mean[:], rstd[:], ALU.mult))
                ch.link(dve.tensor_scalar(nbias[:], nbias[:], -1.0, None, ALU.mult))
                dve.sem_inc(did("nbias_ready"), 1)

            negate_bias()
            for g in range(NG):
                dve.wait_ge(bu_ps, now(2 * g + 1))
                if g:
                    dve.wait_ge(s4out_ps, now(2 * g - 1))
                dve.tensor_tensor_scan(s4_x[:], s4_abc[:], bank[2][:], s4_carry[:, 0:1], ALU.mult, ALU.add).then_inc(scan_done, 1)
                dve.wait_ge(scan_done, now(g))
                ch.link(dve.tensor_copy(s4_carry[:], s4_x[:, GW - 1:GW]))
                for b in range(B):
                    dve.wait_ge(s4out_ps, now(2 * g + b))
                    dve.tensor_tensor(xs[:, b, g * GT:(g + 1) * GT, :], xs[:, b, g * GT:(g + 1) * GT, :],
                                      bank[4 + b + 2 * (g % 2)][:].rearrange("p (q d) -> p q d", q=GT), ALU.add).then_inc(xres3_done, 1)
                for b in range(B):
                    dve.wait_ge(xres3_done, now(2 * g + b))
                    for q in range(GT):
                        dve.bn_stats(stats[:, b * NT + g * GT + q, :], xs[:, b, g * GT + q, :])

            dve.wait_ge(*upto("rows_ps", 1))
            for b in range(B):
                dve.tensor_copy(rows[:, b], bank[6 + b][:, 0:3 * D].rearrange("p (j d) -> p j d", j=3))
            settled(dve, ch)
            dve.tensor_scalar(rows[:, :, 1, :], rows[:, :, 1, :], 1.0, None, ALU.add)
            gate_(dve, ch, rows[:, :, 2, :], gt0[:], gt1[:])
            dve.sem_inc(did("rows_ready"), 1)
            ln_finish(dve, ch)
            ln_rstd(dve, ch, 4)
            negate_bias()
            dve.wait_ge(once("l1_loaded"), L1_ALL)
            for n in range(2 * NG):
                g, b = n // 2, n % 2
                dve.wait_ge(xhat4_ready, now(n))
                if g:
                    dve.wait_ge(hx_stored[b], 16 * (g + 1))
                dve.wait_ge(dflt_ready, back2(n))
                ch.link(dve.tensor_tensor(h4[:, b], xhat[:, b], rows[:, b, 1:2, :].to_broadcast([P, GT, D]), ALU.mult))
                dve.tensor_tensor(h4[:, b], h4[:, b], rows[:, b, 0:1, :].to_broadcast([P, GT, D]), ALU.add).then_inc(h4_ready, 1)
            dve.wait_ge(*upto("w_ps", 2 * NG))
            dve.tensor_scalar(w_all[:].rearrange("p b c -> p (b c)"), bank[2][:, 0:B * NT], rb_col[:, 0:1], None, ALU.add).then_inc(did("w_ready"), 1)
            dve.wait_ge(*upto("w_ready", 1))
            dve.wait_ge(*upto("l1_consts", 1))
            for k in range(NSTEP):
                ins = dve.tensor_scalar(J[:, k], jt[:], 28 - 4 * k, None, ALU.logical_shift_left)
            ch.link(ins)

            def to_float_bits(out_, tmp, u):
                ch.link(dve.tensor_scalar(tmp, u, 31, -1, ALU.arith_shift_right, ALU.bitwise_xor))
                ch.link(dve.scalar_tensor_tensor(out=out_, in0=tmp, scalar=-2**31, in1=u, op0=ALU.bitwise_or, op1=ALU.bitwise_xor))

            to_float_bits(candf[:, 0], candt[:], J[:, 0])
            ch.link(dve.tensor_copy(candf[:, 1], candf[:, 0]))
            for k in range(NSTEP):
                if k:
                    ch.link(dve.tensor_tensor(candf[:], thr[:].unsqueeze(2).to_broadcast([P, B, NJ]),
                                              J[:, k:k + 1, :].to_broadcast([P, B, NJ]), ALU.bitwise_xor))
                ch.link(dve.tensor_tensor(cmp_[:], w_all[:].unsqueeze(2).to_broadcast([P, B, NJ, NT]),
                                          candf[:].bitcast(F32).unsqueeze(3).to_broadcast([P, B, NJ, NT]), ALU.is_ge))
                dve.tensor_reduce(cnt[:], cmp_[:], AX.X, ALU.add).then_inc(did("cnt_ready"), 1)
                dve.wait_ge(*upto("cnt_ps", k + 1))
                ch.link(dve.tensor_scalar(ge256[:].rearrange("p b j -> p (b j)"), bank[0][:, 0:B * NJ], float(TOPK), None, ALU.is_ge))
                with nc.allow_low_precision(reason="counts up to 15"):
                    ch.link(dve.tensor_reduce(digit[:], ge256[:], AX.X, ALU.add))
                if k:
                    ch.link(dve.scalar_tensor_tensor(out=thr[:], in0=digit[:], scalar=28 - 4 * k, in1=thr[:],
                                                     op0=ALU.logical_shift_left, op1=ALU.bitwise_xor))
                else:
                    ch.link(dve.tensor_scalar(pre[:], digit[:], 28, None, ALU.logical_shift_left))
                    to_float_bits(thr[:], thr_t[:], pre[:])
            thrb = thr[:].bitcast(F32).unsqueeze(2).to_broadcast([P, B, NT])
            dve.tensor_tensor(gteq[:, 0], w_all[:], thrb, ALU.is_gt)
            dve.tensor_tensor(gteq[:, 1], w_all[:], thrb, ALU.is_equal).then_inc(did("gteq_ready"), 1)
            dve.wait_ge(*upto("gteq_ps", 1))
            ch.link(dve.tensor_copy(tot[:, 0:2].rearrange("p k b c -> p (k b c)"), bank[0][:, 0:2 * B * NT]))
            rank_in(ch, dve, 1, bank[0][:, 2 * B * NT:3 * B * NT])
            ch.link(dve.tensor_reduce(ngt[:], tot[:, 0], AX.X, ALU.add))
            ch.link(dve.tensor_scalar(ngt[:], ngt[:], -1.0, float(SEL), ALU.mult, ALU.add))
            ch.link(dve.tensor_tensor(sel[:], pos[:], ngt[:].unsqueeze(2).to_broadcast([P, B, NT]), ALU.is_le))
            ch.link(dve.tensor_tensor(sel[:], sel[:], gteq[:, 1], ALU.mult))
            dve.tensor_tensor(sel[:], sel[:], gteq[:, 0], ALU.add).then_inc(did("sel_ready"), 1)
            dve.wait_ge(*upto("sel_ps", 1))
            ch.link(dve.tensor_copy(tot[:, 1].rearrange("p b c -> p (b c)"), bank[0][:, 0:B * NT]))
            rank_in(ch, dve, 1, bank[0][:, B * NT:2 * B * NT])
            ch.link(dve.tensor_tensor(pos[:], pos[:], sel[:], ALU.mult))
            ch.link(dve.tensor_scalar(pos[:], pos[:], -1.0, None, ALU.add))
            dve.sem_inc(did("pos_ready"), 1)
            for b in range(B):
                for c in range(NT if b < B - 1 else C_POOL):
                    ins = dve.tensor_scalar(choose[:, b, c, :], iota256[:], pos[:, b, c:c + 1], None, ALU.is_equal)
                ins.then_inc(did("choose_ready"), 1)
            dve.wait_ge(*upto("picks_ps", 1))
            ch.link(dve.tensor_copy(picks[:].rearrange("p s j -> p (s j)"), bank[1][:, 0:2 * NS4]))
            ch.link(dve.scalar_tensor_tensor(out=idx[:], in0=picks[:, :, 0], scalar=float(P), in1=picks[:, :, 1], op0=ALU.mult, op1=ALU.add))
            ch.link(dve.tensor_scalar(cidx[:], idx[:], float(ML - 1), None, ALU.min))
            for b in range(B):
                c0, c1 = b * NSEL, (b + 1) * NSEL
                dve.tensor_scalar(gidx[:, 0, c0:c1], idx[:, c0:c1], float(b * T), None, ALU.add)
                ins = dve.tensor_scalar(gidx[:, 1, c0:c1], cidx[:, c0:c1], float(b * ML), None, ALU.add)
            ins.then_inc(did("gidx_ready"), 1)
            for b in range(B):
                dve.wait_ge(*upto("cidx_ps", b + 1))
                for k in range(ML // P):
                    ins = dve.tensor_scalar(colsel[:, b, k, :], bank[6 + b][:, 0:TOPK], iotap[:, k:k + 1], None, ALU.is_equal)
                ins.then_inc(did("colsel_ready"), 1)

            def rms(src, j):
                dve.wait_ge(*upto("ss_ready", j + 1))
                ch.link(dve.tensor_scalar(ss[:], ss[:], 1.0 / D, RMS_EPS, ALU.mult, ALU.add))
                dve.sem_inc(did("ms_ready"), 1)
                dve.wait_ge(*upto("sroot_ready", j + 1))
                ch.link(dve.reciprocal(srr[:], sroot[:]))
                ch.link(dve.tensor_tensor(st[:], srr[:], srr[:], ALU.mult))
                ch.link(dve.tensor_tensor(st[:], st[:], ss[:], ALU.mult))
                ch.link(dve.tensor_scalar(st[:], st[:], -0.5, 1.5, ALU.mult, ALU.add))
                ch.link(dve.tensor_tensor(srr[:], srr[:], st[:], ALU.mult))
                for s_ in range(NS4):
                    ins = dve.scalar_tensor_tensor(out=hn[:, s_], in0=src[:, s_], scalar=srr[:, s_:s_ + 1], in1=ln_row[:, j], op0=ALU.mult, op1=ALU.mult)
                ins.then_inc(did("hn_ready"), 1)

            dve.wait_ge(once("sx_loaded"), 16 * NS4)
            rms(sx[:, :, D:2 * D], 0)
            dve.wait_ge(once("spos_loaded"), 16 * NS4)
            ch.link(dve.tensor_copy(st[:], spos[:]))
            ch.link(dve.tensor_tensor(ang[:, 0], st[:].unsqueeze(2).to_broadcast([P, NS4, AD // 2]),
                                      inv[:].unsqueeze(1).to_broadcast([P, NS4, AD // 2]), ALU.mult))
            ch.link(dve.tensor_scalar(ang[:, 1], ang[:, 0], 0.0, None, ALU.add))
            two_pi = 2.0 * np.pi
            ch.link(dve.tensor_scalar(angk[:, 0], ang[:, 0], 1.0 / two_pi, None, ALU.mult))
            ch.link(dve.tensor_scalar(angk[:, 1], ang[:, 1], 1.0 / two_pi, 0.25, ALU.mult, ALU.add))
            ch.link(dve.tensor_copy(angi[:], angk[:]))
            ch.link(dve.tensor_copy(angk[:], angi[:]))
            part1 = 6.28125
            part2 = 1.9350051879882812e-3
            part3 = two_pi - part1 - part2
            for part in (part1, part2, part3):
                ch.link(dve.scalar_tensor_tensor(out=ang[:].rearrange("p t s i -> p (t s i)"), in0=angk[:].rearrange("p t s i -> p (t s i)"),
                                                 scalar=-part, in1=ang[:].rearrange("p t s i -> p (t s i)"), op0=ALU.mult, op1=ALU.add))
            ch.link(dve.tensor_scalar(ang[:, 1], ang[:, 1], float(np.pi / 2), None, ALU.add))
            dve.tensor_scalar(ang[:], ang[:], 3.1415925, -3.1415925, ALU.min, ALU.max).then_inc(did("ang_ready"), 1)
            dve.wait_ge(*upto("sin_ready", 1))
            for s_ in range(NS4):
                dve.wait_ge(*upto("qk_ready", s_ + 1))

                def halves(t):
                    return t.rearrange("p (h t i) -> p h t i", t=2, i=AD // 2)

                def angle(j):
                    return sc_[:, j, s_:s_ + 1, :].unsqueeze(1).to_broadcast([P, 2 * AH, 2, AD // 2])

                dve.tensor_tensor(halves(qks[:, s_ % 2]), halves(qk[:, s_]), angle(0), ALU.mult)
                ch.link(dve.tensor_tensor(halves(qkc[:, s_ % 2]), halves(qk[:, s_]), angle(1), ALU.mult))
                c_, n_, o_ = halves(qkc[:, s_ % 2]), halves(qks[:, s_ % 2]), halves(qk[:, s_])
                dve.tensor_tensor(o_[:, :, 0, :], c_[:, :, 0, :], n_[:, :, 1, :], ALU.subtract)
                dve.tensor_tensor(o_[:, :, 1, :], c_[:, :, 1, :], n_[:, :, 0, :], ALU.add).then_inc(did("rope_ready"), 1)
            dve.memset(msel[:, :, SEL:TOPK], -3.0e38)

            def keep_mask(i):
                dve.wait_ge(*upto("msel_ps", i + 1))
                ch.link(dve.tensor_copy(msel[:, i, 0:SEL], mask_bank(i)[:, 0:SEL]))

            keep_mask(0)
            dve.wait_ge(*upto("qkT_ready", 1))
            for h in range(2 * KT_DVE):
                ins = dve.tensor_scalar(kTm[:, 0, h, :], kT[:, 0:TOPK], headmask[:, h:h + 1], None, ALU.mult)
                if h % 2 == 1:
                    ins.then_inc(did("keys_ready"), 1)
            for m in range(NM + LAG_O):
                if m < NM:
                    i, p, slot = m // PAIRS, m % PAIRS, m % SC_SLOTS
                    dve.wait_ge(*upto("score_ps", m + 1))
                    if m >= SC_SLOTS:
                        dve.wait_ge(*upto("pT_ps", m - SC_SLOTS + 1))
                    dve.tensor_tensor(sc[:, slot], bank[5 + m % 2][:].rearrange("p (h k) -> p h k", h=2),
                                      msel[:, i:i + 1, :].to_broadcast([P, 2, TOPK]), ALU.add).then_inc(did("masked_ready"), 1)
                    dve.wait_ge(*upto("masked_ready", m + 1))
                    dve.tensor_reduce(smax[:, i, 2 * p:2 * p + 2], sc[:, slot], AX.X, ALU.max, negate=True).then_inc(did("smax_ready"), 1)
                    if m - 1 in MASK_STEPS:
                        keep_mask(MASK_STEPS.index(m - 1) + 1)
                m -= LAG_O
                if m >= 0 and m % PAIRS == PAIRS - 1:
                    i = m // PAIRS
                    dve.wait_ge(*upto("exp_ready", m + 1))
                    ch.link(dve.reciprocal(sinv[:, i % 2], ssum[:, i]))
                    dve.wait_ge(*upto("pv_ps", m + 1))
                    dve.tensor_tensor(on[:, i].rearrange("p (h d) -> p h d", h=AH), bank[i % 2][:, 0:D].rearrange("p (h d) -> p h d", h=AH),
                                      sinv[:, i % 2].unsqueeze(2).to_broadcast([P, AH, AD]), ALU.mult).then_inc(did("on_ready"), 1)
            dve.wait_ge(*upto("wo_ps", 1))
            dve.tensor_tensor(x1[:], bank[1][:].rearrange("p (s d) -> p s d", s=NS4), sx[:, :, D:2 * D], ALU.add).then_inc(did("x1_ready"), 1)
            rms(x1[:], 1)
            gate_row = [rows[:, b, 2:3, :].to_broadcast([P, NSEL, D]) for b in range(B)]
            for b in range(B):
                c0, c1 = b * NSEL, (b + 1) * NSEL
                dve.tensor_tensor(gw[:, c0:c1], gate_row[b], sx[:, c0:c1, 2 * D:].to_broadcast([P, NSEL, D]), ALU.mult)
                dve.tensor_scalar(notsel[:, c0:c1], sx[:, c0:c1, 2 * D], thr[:, b:b + 1].bitcast(F32), None, ALU.is_le)
            ch.link(dve.tensor_tensor(rest[:], x1[:], sx[:, :, 2 * D:].to_broadcast([P, NS4, D]), ALU.mult))
            ch.link(dve.tensor_tensor(res[:], sx[:, :, D:2 * D], notsel[:].unsqueeze(2).to_broadcast([P, NS4, D]), ALU.mult))
            ch.link(dve.tensor_tensor(rest[:], rest[:], res[:], ALU.add))
            for b in range(B):
                c0, c1 = b * NSEL, (b + 1) * NSEL
                ins = dve.tensor_tensor(rest[:, c0:c1], rest[:, c0:c1], gate_row[b], ALU.mult)
            ch.link(ins)
            ch.link(dve.tensor_tensor(rest[:], rest[:], sx[:, :, 0:D], ALU.add))
            dve.wait_ge(*upto("w2_ps", 1))
            ch.link(dve.tensor_tensor(res[:], bank[5][:].rearrange("p (s d) -> p s d", s=NS4), gw[:], ALU.mult))
            dve.tensor_tensor(res[:], res[:], rest[:], ALU.add).then_inc(did("res_ready"), 1)

        def transposes(pe, g, b):
            n = 2 * g + b
            pe.wait_ge(xhat_ready, now(n))
            pe.wait_ge(hT_ready, back2(n))
            for q in range(GT):
                ins = pe.transpose(bank[b][:, q * P:(q + 1) * P], xhat[:, b, q, :], ident[:])
            ins.then_inc(trans_ps, 1)

        @block.tensor
        def _(pe):
            credit(pe, "pe")
            pe.wait_ge(c_silu, 1)
            pe.wait_ge(mod_loaded, 32)
            pe.wait_ge(consts_ready, 1)
            for l in range(2):
                for j in range(6):
                    ins = pe.matmul(bank[4 + l][:, 2 * j:2 * j + 2], wmod[l][:, j * D:(j + 1) * D], cS[l][:], start=True, stop=True)
            ins.then_inc(mod_ps, 1)
            for l in range(2):
                for b in range(B):
                    i = l * B + b
                    ins = pe.matmul(bank[7][:, i * P:(i + 1) * P], crep[l][:, b, :], wmod[l][:, 2 * D:3 * D], start=True, stop=True)
            ins.then_inc(ga_ps, 1)
            pe.wait_ge(w_loaded, W_ALL)
            pe.wait_ge(wbdt_ready, 1)
            pe.wait_ge(mod_ready, 1)

            def project_in(g, b):
                n = 2 * g + b
                pe.wait_ge(hT_ready, now(n))
                pe.wait_ge(z_kept, back1(n))
                for k in range(2):
                    ins = pe.matmul(bank[2 + k][:], wz[:, k * P:(k + 1) * P], hT[:, b, :], start=True, stop=True)
                ins.then_inc(z_ps, 1)
                pe.wait_ge(bc_kept, back1(n))
                for k in range(2):
                    ins = pe.matmul(bank[4 + k][b * NS:(b + 1) * NS, :], win[:, k * NS:(k + 1) * NS], hT[:, b, :], start=True, stop=True)
                ins.then_inc(bc_ps, 1)
                pe.wait_ge(tok_kept, back1(n))
                for q in range(GT):
                    ins = pe.matmul(bank[6][:, q * (NS + H):(q + 1) * (NS + H)], hT[:, b, q * P:(q + 1) * P], wbdt[:], start=True, stop=True)
                ins.then_inc(tok_ps, 1)

            transposes(pe, 0, 0)
            with pe.Fori(0, NG - 1) as g:
                transposes(pe, g, 1)
                project_in(g, 0)
                transposes(pe, g + 1, 0)
                project_in(g, 1)
            transposes(pe, NG - 1, 1)
            for b in range(B):
                project_in(NG - 1, b)
            pe.wait_ge(a_ready, 1)
            pe.wait_ge(z_kept, now(2 * NG - 1))
            af = a_dec[:].rearrange("p b c h -> p (b c h)")
            for i, mask in enumerate((upper, lower, ones)):
                ins = pe.matmul(bank[i][:, 0:TH], mask[:], af, start=True, stop=True)
            ins.then_inc(cum_ps, 1)
            pe.wait_ge(decays_ready, 1)
            pe.wait_ge(bc_kept, now(2 * NG - 1))
            pe.wait_ge(tok_kept, now(2 * NG - 1))

            def inputs_(c, b, last):
                n = 2 * c + b
                lo, hi = b * NS, (b + 1) * NS
                pe.wait_ge(segrhs_ready, now(n))
                pe.wait_ge(expA_done, back1(n))
                pe.matmul(bank[0][:], lower[:], seg_rhs[:, b, 0:4, :].rearrange("p h t -> p (h t)"), start=True, stop=True).then_inc(segA_ps, 1)
                pe.wait_ge(expB_done, back1(n))
                pe.matmul(bank[1][:], lower[:], seg_rhs[:, b, 4:8, :].rearrange("p h t -> p (h t)"), start=True, stop=True).then_inc(segB_ps, 1)
                if b == 1 and last:
                    turn(c - 1, 1)
                pe.wait_ge(pk_loaded[b], 32 * (c + 1))
                pe.wait_ge(xsb_done, back1(n))
                pe.wait_ge(s_upd, back1(c))
                pe.matmul(bank[2][:], pk_slot[:, b, PK_H:PK_H + P], win[:, 2 * NS + H:], start=True, stop=True).then_inc(x_ps, 1)
                if b == 0:
                    pe.wait_ge(y2_done, back1(n))
                else:
                    pe.wait_ge(gm_done, back1(n))
                pe.matmul(bank[6][:, 0:P], bc_slot[lo:hi, 0, :], bc_slot[lo:hi, 1, :], start=True, stop=True).then_inc(g_ps, 1)
                pe.wait_ge(yg_done, back2(n))
                for k in range(2):
                    ins = pe.matmul(bank[4 + b][:], pk_slot[:, b, PK_S + k * P:PK_S + (k + 1) * P], wzg[:, k, :], start=k == 0, stop=k == 1)
                ins.then_inc(zg_ps, 1)

            def turn(c, b):
                pe.wait_ge(yg_done, now(2 * c + b))
                for k in range(4):
                    ins = pe.transpose(bank[3 + 4 * b][:, k * P:(k + 1) * P], yg[:, b, k * P:(k + 1) * P], ident[:])
                ins.then_inc(yT_ps, 1)

            def project(c, b):
                pe.wait_ge(ygT_done, now(2 * c + b))
                for k in range(4):
                    ins = pe.matmul(bank[3 + 4 * b][:, 0:P], ygT[:, b, k, :], woutg[:, b, k, :], start=k == 0, stop=k == 3)
                ins.then_inc(out_ps, 1)

            def chunk(c, last):
                inputs_(c, 0, last)
                if last:
                    turn(c - 1, 0)
                inputs_(c, 1, last)
                if last:
                    for b in range(B):
                        project(c - 1, b)
                def diagonal(b):
                    pe.wait_ge(m_ready, now(2 * c + b))
                    if b == 0:
                        pe.wait_ge(gm_done, now(2 * c + 1))
                    else:
                        pe.wait_ge(y2_done, now(2 * c))
                    for h in range(H):
                        ins = pe.matmul(bank[6][:, h * HD:(h + 1) * HD], M[:, b, h, :], dX[:, b, h * HD:(h + 1) * HD], start=True, stop=True)
                    ins.then_inc(diag_ps, 1)

                if not last:
                    pe.wait_ge(ga_done, 1)
                pe.wait_ge(s_upd, back1(c))
                for b in range(B):
                    n = 2 * c + b
                    lo, hi = b * NS, (b + 1) * NS
                    pe.wait_ge(xres_done, back2(n))
                    pe.matmul(bank[3 + 4 * b][:], bc_slot[lo:hi, 1, :], S[lo:hi, :], start=True, stop=True).then_inc(off_ps, 1)
                diagonal(0)
                pe.wait_ge(xsb_done, now(2 * c + 1))
                for b in range(B):
                    pe.wait_ge(dx_done, now(2 * c + b))
                    pe.matmul(bank[2][b * NS:(b + 1) * NS, :], pk_slot[:, b, PK_B:PK_B + NS], dXw[:, b], start=True, stop=True).then_inc(ds_ps, 1)
                diagonal(1)

            chunk(0, False)
            with pe.Fori(1, NT) as c:
                chunk(c, True)
            for b in range(B):
                turn(NT - 1, b)
            for b in range(B):
                project(NT - 1, b)

            pe.wait_ge(xres_done, now(2 * NT - 1))
            for b in range(B):
                ins = pe.matmul(bank[6 + b][:, 0:3 * D], crep[0][:, b, :], wmod[0][:, 3 * D:6 * D], start=True, stop=True)
            ins.then_inc(did("rows0_ps"), 1)

            def transposes2(n):
                g, b = n // 2, n % 2
                pe.wait_ge(xhat2_ready, now(n))
                pe.wait_ge(hT2_ready, back2(n))
                for q in range(GT):
                    ins = pe.transpose(bank[b][:, q * P:(q + 1) * P], h_all[:, b, g * GT + q, 0:D], ident[:])
                ins.then_inc(trans2_ps, 1)

            def route(n):
                g, b = n // 2, n % 2
                pe.wait_ge(hT2_ready, now(n))
                for q in range(GT):
                    c = g * GT + q
                    i = b * NT + c
                    ins = pe.matmul(bank[2][:, i * EX:(i + 1) * EX], hT_all[:, b, c * P:(c + 1) * P], wrouter[:], start=True, stop=True)
                return ins

            for n in range(2 * NG):
                transposes2(n)
                if n:
                    route(n - 1)
            route(2 * NG - 1).then_inc(did("router_ps"), 1)

            def expand(g, b, before_last=lambda: None):
                n = 2 * g + b
                h_ = hT_all[:, b, bass.ds(g * GW, GW)]
                pe.wait_ge(xres2_done, back2(n))
                for k in range(HID // P):
                    ins = pe.matmul(bank[4 * b + k][:], wgu_s[:, k * P:(k + 1) * P], h_, start=True, stop=True)
                ins.then_inc(gate_ps, 1)
                before_last()
                for k in range(HID // P):
                    ins = pe.matmul(bank[4 * b + 2 + k][:], wgu_s[:, HID + k * P:HID + (k + 1) * P], h_, start=True, stop=True)
                ins.then_inc(up_ps, 1)

            def down(g, b):
                n = 2 * g + b
                pe.wait_ge(hid_ready, now(n))
                for q in range(GT):
                    for k in range(HID // P):
                        ins = pe.matmul(bank[4 * b][:, q * D:(q + 1) * D], hid[:, b, k, q * P:(q + 1) * P], wdown_g[:, b, k, :],
                                        start=k == 0, stop=k == HID // P - 1)
                ins.then_inc(down_ps, 1)

            pe.wait_ge(moe_loaded, MOE_ALL)
            pe.wait_ge(hT2_ready, now(2 * NG - 1))

            def ranks():
                pe.wait_ge(*upto("onehot_ready", 1))
                pe.wait_ge(*upto("rows0_ready", 1))
                oh = onehot[:].rearrange("p i e -> p (i e)")
                pe.matmul(bank[7][:, 0:TE], upper[:], oh, start=True, stop=True)
                pe.matmul(bank[7][:, TE:2 * TE], ones[:], oh, start=True, stop=True).then_inc(did("ranks_ps"), 1)

            expand(0, 0, ranks)
            expand(0, 1, lambda: pe.wait_ge(*upto("ranks_kept", 1)))
            for b in range(B):
                down(0, b)
            with pe.Fori(1, NG) as g:
                for b in range(B):
                    expand(g, b)
                for b in range(B):
                    down(g, b)
            pe.wait_ge(*upto("expert_ready", 1))
            pe.wait_ge(xres2_done, now(2 * NG - 1))
            for s_ in range(SLOTS):
                pe.wait_ge(hs_loaded[s_], 16)
                pe.transpose(bank[6][:, s_ * P:(s_ + 1) * P], hs[:, s_, :], ident[:]).then_inc(hsT_ps, 1)
            next_expert = [pe.alloc_register(f"next_expert{s_}") for s_ in range(SLOTS)]
            pe.load(next_expert, expert_i[0:1, 0, 0:SLOTS])
            with pe.Fori(0, NSORT // SLOTS) as i:
                tile_expert = [pe.snap(r, min_val=0, max_val=EX - 1) for r in next_expert]
                for s_ in range(SLOTS):
                    n = SLOTS * i + s_
                    e = tile_expert[s_]
                    pe.wait_ge(hsT_ready, now(i))
                    pe.wait_ge(ys_ready, back3(n))
                    pe.matmul(bank[s_][:], hsT[:, s_, :], wgu[:, bass.ds(e, 1), :].rearrange("p a h -> p (a h)"), start=True, stop=True).then_inc(gu_ps, 1)
                pe.load(next_expert, expert_i[0:1, bass.ds(i + 1, 1), 0:SLOTS].rearrange("p a s -> p (a s)"))
                for s_ in range(SLOTS):
                    pe.wait_ge(hs_loaded[s_], 16 * (i + 2))
                    pe.wait_ge(hsT_ready, now(i))
                    pe.transpose(bank[6][:, s_ * P:(s_ + 1) * P], hs[:, s_, :], ident[:]).then_inc(hsT_ps, 1)
                for s_ in range(SLOTS):
                    n = SLOTS * i + s_
                    pe.wait_ge(hids_ready, now(n))
                    pe.wait_ge(hidsT_ready, back3(n))
                    for k in range(HID // P):
                        ins = pe.transpose(bank[3 + s_][:, k * P:(k + 1) * P], hids[:, s_, k * P:(k + 1) * P], ident[:])
                    ins.then_inc(hidsT_ps, 1)
                for s_ in range(SLOTS):
                    n = SLOTS * i + s_
                    e = tile_expert[s_]
                    pe.wait_ge(hidsT_ready, now(n))
                    for k in range(HID // P):
                        ins = pe.matmul(bank[s_][:, 0:D], hidsT[:, s_, k * P:(k + 1) * P],
                                        wdown[:, bass.ds(e, 1), k, :].rearrange("p a d -> p (a d)"), start=k == 0, stop=k == HID // P - 1)
                    ins.then_inc(ys_ps, 1)
            pe.wait_ge(s4_ready, 1)
            pe.wait_ge(s4_loaded, S4_ALL)
            pe.wait_ge(ys_ready, now(NSORT - 1))

            def transposes3(g):
                for b in range(B):
                    n = 2 * g + b
                    pe.wait_ge(xhat3_ready, now(n))
                    if g:
                        pe.wait_ge(hT3_ready, now(n - 2))
                    for q in range(GT):
                        ins = pe.transpose(bank[b][:, q * P:(q + 1) * P], xhat[:, b, q, :], ident[:])
                    ins.then_inc(trans3_ps, 1)

            transposes3(0)
            for g in range(NG):
                if g:
                    pe.wait_ge(scan_done, now(g - 1))
                for b in range(B):
                    pe.wait_ge(hT3_ready, now(2 * g + b))
                    pe.matmul(bank[2][b * NS:(b + 1) * NS, :], s4_B[:], hT_s4[g % 2][:, b, :], start=True, stop=True).then_inc(bu_ps, 1)
                if g + 1 < NG:
                    transposes3(g + 1)
                out_bank = [bank[4 + b + 2 * (g % 2)] for b in range(B)]
                for b in range(B):
                    if g >= 2:
                        pe.wait_ge(xres3_done, now(2 * g + b - 4))
                    for q in range(GT):
                        pe.matmul(out_bank[b][:, q * P:(q + 1) * P], hT_s4[g % 2][:, b, q * P:(q + 1) * P], s4_Dg[:, b], start=q == 0, stop=False)
                pe.wait_ge(scan_done, now(g))
                for b in range(B):
                    lo, hi = b * NS, (b + 1) * NS
                    for q in range(GT):
                        ins = pe.matmul(out_bank[b][:, q * P:(q + 1) * P], s4_x[lo:hi, q * P:(q + 1) * P], s4_Cg[lo:hi], start=False, stop=q == GT - 1)
                    ins.then_inc(s4out_ps, 1)
            pe.wait_ge(xres3_done, now(2 * NG - 1))
            for b in range(B):
                ins = pe.matmul(bank[6 + b][:, 0:3 * D], crep[1][:, b, :], wmod[1][:, 3 * D:6 * D], start=True, stop=True)
            ins.then_inc(did("rows_ps"), 1)
            pe.wait_ge(hT3_ready, now(2 * NG - 1))
            pe.wait_ge(scan_done, now(NG - 1))
            pe.wait_ge(once("l1_loaded"), L1_ALL)

            def transposes4(n):
                pe.wait_ge(xhat4_ready, now(n))
                pe.wait_ge(hT4_ready, back2(n))
                for q in range(GT):
                    ins = pe.transpose(bank[n % 2][:, q * P:(q + 1) * P], xhat[:, n % 2, q, :], ident[:])
                ins.then_inc(trans4_ps, 1)

            def weigh(n):
                pe.wait_ge(hT4_ready, now(n))
                for q in range(GT):
                    i = (n % 2) * NT + n // 2 * GT + q
                    ins = pe.matmul(bank[2][:, i:i + 1], hT[:, n % 2, q * P:(q + 1) * P], rw_col[:], start=True, stop=True)
                ins.then_inc(did("w_ps"), 1)

            for n in range(2 * NG):
                transposes4(n)
                if n:
                    weigh(n - 1)
            weigh(2 * NG - 1)
            pe.wait_ge(hT4_ready, now(2 * NG - 1))
            for k in range(NSTEP):
                pe.wait_ge(*upto("cnt_ready", k + 1))
                pe.matmul(bank[0][:, 0:B * NJ], ones[:], cnt[:].rearrange("p b j -> p (b j)"), start=True, stop=True).then_inc(did("cnt_ps"), 1)
            pe.wait_ge(*upto("gteq_ready", 1))
            w_ = 2 * B * NT
            pe.matmul(bank[0][:, 0:w_], ones[:], gteq[:].rearrange("p k b c -> p (k b c)"), start=True, stop=True)
            pe.matmul(bank[0][:, w_:w_ + B * NT], upper[:], gteq[:, 1].rearrange("p b c -> p (b c)"), start=True, stop=True).then_inc(did("gteq_ps"), 1)
            pe.wait_ge(*upto("sel_ready", 1))
            sf = sel[:].rearrange("p b c -> p (b c)")
            pe.matmul(bank[0][:, 0:B * NT], ones[:], sf, start=True, stop=True)
            pe.matmul(bank[0][:, B * NT:2 * B * NT], upper[:], sf, start=True, stop=True).then_inc(did("sel_ps"), 1)
            for s_ in range(NS4):
                b, k = s_ // NSEL, s_ % NSEL
                if k == 0:
                    pe.wait_ge(*upto("choose_ready", b + 1))
                    if b == B - 1:
                        pe.wait_ge(*upto("choose_rest", 1))
                for c in range(NT):
                    ins = pe.matmul(bank[1][:, 2 * s_:2 * s_ + 2], choose[:, b, c, k * P:(k + 1) * P], tokid[:, c, :], start=c == 0, stop=c == NT - 1)
            ins.then_inc(did("picks_ps"), 1)
            pe.wait_ge(*upto("gidx_ready", 1))
            for b in range(B):
                for k in range(NSEL):
                    j = b * NSEL + k
                    ins = pe.matmul(bank[6 + b][:, k * P:(k + 1) * P], cidx[:, j:j + 1].to_broadcast([P, P]), ident[:], start=True, stop=True)
                ins.then_inc(did("cidx_ps"), 1)
            pe.wait_ge(*upto("hn_ready", 1))
            for s_ in range(NS4):
                ins = pe.transpose(bank[0][:, s_ * P:(s_ + 1) * P], hn[:, s_], ident[:])
            ins.then_inc(did("hnT_ps"), 1)
            pe.wait_ge(*upto("hnT_ready", 1))
            pe.wait_ge(once("l1_loaded"), L1_ALL)
            for s_ in range(NS4):
                pe.matmul(bank[1 + s_][:, 0:3 * D], hnT[:, s_ * P:(s_ + 1) * P], wqkv[:], start=True, stop=True).then_inc(did("qkv_ps"), 1)
            pe.wait_ge(once("smask_loaded"), 16 * NS4)
            for i in range(NS4):
                if i >= 2:
                    pe.wait_ge(*upto("maskT_ready", i - 1))
                for k in range(ML // P):
                    ins = pe.transpose(bank[5 * (1 - i % 2)][:, k * P:(k + 1) * P], smask[:, i, k * P:(k + 1) * P], ident[:])
                ins.then_inc(did("maskT_ps"), 1)

            def mask_columns(i):
                pe.wait_ge(*upto("maskT_ready", i + 1))
                pe.wait_ge(*upto("colsel_ready", B))
                if i >= 2:
                    pe.wait_ge(*upto("masked_ready", 1 if i == 2 else MASK_STEPS[i - 3] + 3))
                for k in range(ML // P):
                    ins = pe.matmul(mask_bank(i), smask[:, i, k * P:(k + 1) * P], colsel[:, i // NSEL, k, :], start=k == 0, stop=k == ML // P - 1)
                ins.then_inc(did("msel_ps"), 1)

            pe.wait_ge(*upto("qk_ready", NS4))
            mask_columns(0)
            pe.wait_ge(*upto("rope_ready", NS4))
            pe.wait_ge(*upto("maskT_ready", NS4))
            for j in range(2):
                for s_ in range(NS4):
                    ins = pe.transpose(bank[5 + j][:, s_ * P:(s_ + 1) * P], qk[:, s_, j * D:(j + 1) * D], ident[:])
            ins.then_inc(did("qT_ps"), 1)
            pe.wait_ge(*upto("qkT_ready", 1))
            for m in range(NM + LAG_O):
                if m < NM:
                    i, p = m // PAIRS, m % PAIRS
                    b = i // NSEL
                    if m < KT_DVE:
                        pe.wait_ge(*upto("keys_ready", m + 1))
                    elif b > 0 or p >= KT_DVE:
                        pe.wait_ge(kTm_ready, b * PAIRS + p + 1 - KT_DVE)
                    if m >= 2:
                        pe.wait_ge(*upto("masked_ready", m - 1))
                    pe.matmul(bank[5 + m % 2][:], qT[:, i * P:(i + 1) * P], kTm[:, b, 2 * p:2 * p + 2, :].rearrange("p h k -> p (h k)"),
                              start=True, stop=True).then_inc(did("score_ps"), 1)
                t = m - LAG_T
                if 0 <= t < NM:
                    pe.wait_ge(*upto("exp_ready", t + 1))
                    if t >= 2:
                        pe.wait_ge(*upto("pT_ready", t - 1))
                    for j in range(2 * NSEL):
                        h, kh = j // NSEL, j % NSEL
                        ins = pe.transpose(bank[2 + t % 2][:, j * P:(j + 1) * P], sc[:, t % SC_SLOTS, h, kh * P:(kh + 1) * P], ident[:])
                    ins.then_inc(did("pT_ps"), 1)
                v = m - LAG_V
                if 0 <= v < NM:
                    i, p = v // PAIRS, v % PAIRS
                    pe.wait_ge(*upto("pT_ready", v + 1))
                    if p == 0 and i >= 2:
                        pe.wait_ge(*upto("on_ready", i - 1))
                    for j in range(2 * NSEL):
                        h, kh = 2 * p + j // NSEL, j % NSEL
                        ins = pe.matmul(bank[i % 2][:, h * AD:(h + 1) * AD], pT[:, v % SC_SLOTS, j, :], vv[:, i // NSEL * NSEL + kh, h * AD:(h + 1) * AD],
                                        start=kh == 0, stop=kh == NSEL - 1)
                    ins.then_inc(did("pv_ps"), 1)
                if m in MASK_STEPS:
                    mask_columns(MASK_STEPS.index(m) + 1)
            pe.wait_ge(*upto("on_ready", NS4))
            for s_ in range(NS4):
                ins = pe.transpose(bank[0][:, s_ * P:(s_ + 1) * P], on[:, s_], ident[:])
            ins.then_inc(did("onT_ps"), 1)
            pe.wait_ge(*upto("onT_ready", 1))
            for s_ in range(NS4):
                ins = pe.matmul(bank[1][:, s_ * D:(s_ + 1) * D], onT[:, s_ * P:(s_ + 1) * P], wo[:], start=True, stop=True)
            ins.then_inc(did("wo_ps"), 1)
            pe.wait_ge(*upto("hn_ready", 2))
            for s_ in range(NS4):
                ins = pe.transpose(bank[0][:, s_ * P:(s_ + 1) * P], hn[:, s_], ident[:])
            ins.then_inc(did("hnT_ps"), 1)
            pe.wait_ge(*upto("hnT_ready", 2))
            for k in range(FF // P):
                pe.matmul(bank[1 + k][:], w1[:, k * P:(k + 1) * P], hnT[:], start=True, stop=True).then_inc(did("hid_ps"), 1)
            pe.wait_ge(*upto("gelu_ready", FF // P))
            for s_ in range(NS4):
                for k in range(FF // P):
                    ins = pe.matmul(bank[5][:, s_ * D:(s_ + 1) * D], hid1[:, k, s_ * P:(s_ + 1) * P], w2[:, k, :], start=k == 0, stop=k == FF // P - 1)
            ins.then_inc(did("w2_ps"), 1)


_INS = ["L0_attn_x", "L0_attn_Wz", "L0_attn_Win", "L0_attn_Wzg", "L0_attn_Wout", "L0_attn_dt_bias", "L0_attn_A_log",
        "L0_attn_D_param", "L0_wmod", "L1_wmod", "L1_attn_Lambda", "L1_attn_log_dt", "L1_attn_D",
        "L1_ffn_attention_mask", "L1_ffn_position_ids", "L1_ffn_router_w", "L1_ffn_router_b", "L1_ffn_wq", "L1_ffn_wk",
        "L1_ffn_wv", "L1_ffn_wo", "L1_ffn_w1", "L1_ffn_w2", "L1_ffn_ln1", "L1_ffn_ln2"]
_TRANSPOSED = {"L0_cT": "L0_c", "L1_cT": "L1_c", "upT": "L0_ffn_up", "gateT": "L0_ffn_gate", "downT": "L0_ffn_down",
               "routerT": "L0_ffn_router", "up_sT": "L0_ffn_w_up_s", "gate_sT": "L0_ffn_w_gate_s",
               "down_sT": "L0_ffn_w_down_s", "s4_BT": "L1_attn_B", "s4_CT": "L1_attn_C"}


def kernel(**inputs):
    import concourse.bacc as bacc
    from concourse.bass_utils import run_bass_kernel_spmd

    nc = bacc.Bacc("TRN2", target_bir_lowering=False, num_devices=1)
    arrays = {n: np.ascontiguousarray(inputs[n]) for n in _INS}
    for n, src in _TRANSPOSED.items():
        arrays[n] = np.ascontiguousarray(np.swapaxes(np.asarray(inputs[src]), -1, -2))
    io = {n: nc.dram_tensor(f"in_{n}", a.shape, mybir.dt.from_np(a.dtype), kind="ExternalInput").ap() for n, a in arrays.items()}
    out = nc.dram_tensor("out_0", (B, T, D), F32, kind="ExternalOutput").ap()
    build(nc, io, out)
    r = run_bass_kernel_spmd(nc, [{f"in_{n}": a for n, a in arrays.items()}], core_ids=[0])
    return r.results[0]["out_0"]
```
